# Optimizing a Trainium2 kernel written in Bass

```python
import numpy as np
import jax
import jax.numpy as jnp

def _softmax(x, axis=-1):
    return jax.nn.softmax(x, axis=axis)

def _gelu(x):
    return jax.nn.gelu(x, approximate=True)

def _silu(x):
    return jax.nn.silu(x)

def _sigmoid(x):
    return jax.nn.sigmoid(x)

def _layernorm(x, axis=-1, eps=1e-05):
    m = jnp.mean(x, axis=axis, keepdims=True)
    v = jnp.var(x, axis=axis, keepdims=True)
    return (x - m) / jnp.sqrt(v + eps)

def _scatter_add(tgt, idx, src, axis=0):
    return tgt.at[idx].add(src)

def _segment_sum(src, seg, n):
    return jax.ops.segment_sum(src, seg, n)
kernel_name = 'mk_decoder_postln_d1_seqx_r8_5469e0'

def setup_inputs(seed: int=0):
    np.random.seed(seed)
    _w = jnp.asarray

    def _rec_inputs():
        import jax
        import jax.numpy as jnp
        _rk = jax.random.key(seed)
        x = -0.0003929 + 0.9999 * jax.random.normal(jax.random.fold_in(_rk, 1), (16, 64, 512), jnp.float32)
        _lenS = 64 - jax.random.randint(jax.random.fold_in(_rk, 7), (16,), 0, max(1, 64 // 4) + 1, jnp.int32)
        _lenS2 = 64 - jax.random.randint(jax.random.fold_in(_rk, 8), (16,), 0, max(1, 64 // 4) + 1, jnp.int32)
        _ctx_4096P = jax.random.normal(jax.random.fold_in(_rk, 11), (16, 16, 512), jnp.float32)
        _ctx_4096c = jax.random.dirichlet(jax.random.fold_in(_rk, 511), 0.3 * jnp.ones((16,), jnp.float32), (16, 64))
        _ctx_4096t = jnp.einsum('bsk,bkd->bsd', _ctx_4096c, _ctx_4096P)
        _ctx_4096t = _ctx_4096t * jax.lax.rsqrt(jnp.mean(jnp.square(_ctx_4096t)) + 1e-12) * 0.953939
        ctx_4096 = 2.81802e-05 + 1.00001 * (_ctx_4096t + 0.3 * jax.random.normal(jax.random.fold_in(_rk, 611), (16, 64, 512), jnp.float32))
        return (x, ctx_4096)
    x, ctx_4096 = _rec_inputs()

    def _L0_attn_setup():
        import jax, jax.numpy as jnp
        import numpy as np
        HIDDEN = 512
        NHQ = 32
        NHKV = 8
        HEAD_DIM = HIDDEN // NHQ
        THETA = 10000.0

        def _rope(x, theta_base):
            b, h, s, d = x.shape
            inv_freq = 1.0 / theta_base ** (jnp.arange(0, d, 2, dtype=jnp.float32)[:d // 2] / d)
            freqs = jnp.arange(s, dtype=jnp.float32)[:, None] * inv_freq[None, :]
            cos = jnp.cos(freqs).astype(x.dtype)
            sin = jnp.sin(freqs).astype(x.dtype)
            x1, x2 = (x[..., :d // 2], x[..., d // 2:])
            return jnp.concatenate([x1 * cos - x2 * sin, x2 * cos + x1 * sin], axis=-1)
        key = jax.random.key(seed)
        ks = jax.random.split(key, 5)
        std = 1.0 / np.sqrt(HIDDEN)
        x = jax.random.normal(ks[0], (2, 256, HIDDEN), dtype=jnp.float32)
        Wq = jax.random.normal(ks[1], (HIDDEN, HIDDEN), dtype=jnp.float32) * std
        Wk = jax.random.normal(ks[2], (HIDDEN, NHKV * HEAD_DIM), dtype=jnp.float32) * std
        Wv = jax.random.normal(ks[3], (HIDDEN, NHKV * HEAD_DIM), dtype=jnp.float32) * std
        Wo = jax.random.normal(ks[4], (HIDDEN, HIDDEN), dtype=jnp.float32) * std
        return {'x': x, 'Wq': Wq, 'Wk': Wk, 'Wv': Wv, 'Wo': Wo}
    _L0_attn_all = _L0_attn_setup()
    _L0_attn_in = {k: v for k, v in _L0_attn_all.items() if k in ('Wq', 'Wk', 'Wv', 'Wo')}
    del _L0_attn_all

    def _L0_xattn_setup():
        import jax, jax.numpy as jnp
        import numpy as np
        HEADS = 8
        DIM_HEAD = 64
        DIM = 64
        HIDDEN = HEADS * DIM_HEAD
        B, N = (8, 512)
        key = jax.random.key(seed)
        ks = jax.random.split(key, 7)
        s = 0.02
        return {'x': jax.random.normal(ks[0], (B, DIM, N), dtype=jnp.float32), 'context': jax.random.normal(ks[1], (B, DIM, N), dtype=jnp.float32), 'Wq': jax.random.normal(ks[2], (HIDDEN, DIM), dtype=jnp.float32) * s, 'Wkv': jax.random.normal(ks[3], (2 * HIDDEN, DIM), dtype=jnp.float32) * s, 'Wout': jax.random.normal(ks[4], (DIM, HIDDEN), dtype=jnp.float32) * s, 'b_out': jnp.zeros((DIM,), dtype=jnp.float32), 'g': jnp.ones((1, DIM, 1), dtype=jnp.float32)}
    _L0_xattn_all = _L0_xattn_setup()
    _L0_xattn_in = {k: v for k, v in _L0_xattn_all.items() if k in ('Wq', 'Wkv', 'Wout', 'b_out', 'g')}
    del _L0_xattn_all

    def _L0_ffn_setup():
        import jax, jax.numpy as jnp
        import numpy as np
        H = 512
        I = 256
        E = 16
        TOPK = 4
        SI = 256
        key = jax.random.key(seed)
        ks = jax.random.split(key, 9)
        s = 0.02
        return {'hidden_states': jax.random.normal(ks[0], (2, 256, H), dtype=jnp.float32), 'gate_w': jax.random.normal(ks[1], (E, H), dtype=jnp.float32) * s, 'bias': jnp.zeros((E,), dtype=jnp.float32), 'Wg': jax.random.normal(ks[2], (E, I, H), dtype=jnp.float32) * s, 'Wu': jax.random.normal(ks[3], (E, I, H), dtype=jnp.float32) * s, 'Wd': jax.random.normal(ks[4], (E, H, I), dtype=jnp.float32) * s, 'Sg': jax.random.normal(ks[5], (SI, H), dtype=jnp.float32) * s, 'Su': jax.random.normal(ks[6], (SI, H), dtype=jnp.float32) * s, 'Sd': jax.random.normal(ks[7], (H, SI), dtype=jnp.float32) * s}
    _L0_ffn_all = _L0_ffn_setup()
    _L0_ffn_in = {k: v for k, v in _L0_ffn_all.items() if k in ('gate_w', 'bias', 'Wg', 'Wu', 'Wd', 'Sg', 'Su', 'Sd')}
    del _L0_ffn_all
    return {'x': x, 'ctx_4096': ctx_4096, 'L0_attn_Wq': _L0_attn_in['Wq'], 'L0_attn_Wk': _L0_attn_in['Wk'], 'L0_attn_Wv': _L0_attn_in['Wv'], 'L0_attn_Wo': _L0_attn_in['Wo'], 'L0_xattn_Wq': _L0_xattn_in['Wq'], 'L0_xattn_Wkv': _L0_xattn_in['Wkv'], 'L0_xattn_Wout': _L0_xattn_in['Wout'], 'L0_xattn_b_out': _L0_xattn_in['b_out'], 'L0_xattn_g': _L0_xattn_in['g'], 'L0_ffn_gate_w': _L0_ffn_in['gate_w'], 'L0_ffn_bias': _L0_ffn_in['bias'], 'L0_ffn_Wg': _L0_ffn_in['Wg'], 'L0_ffn_Wu': _L0_ffn_in['Wu'], 'L0_ffn_Wd': _L0_ffn_in['Wd'], 'L0_ffn_Sg': _L0_ffn_in['Sg'], 'L0_ffn_Su': _L0_ffn_in['Su'], 'L0_ffn_Sd': _L0_ffn_in['Sd']}

def reference(x, ctx_4096, L0_attn_Wq, L0_attn_Wk, L0_attn_Wv, L0_attn_Wo, L0_xattn_Wq, L0_xattn_Wkv, L0_xattn_Wout, L0_xattn_b_out, L0_xattn_g, L0_ffn_gate_w, L0_ffn_bias, L0_ffn_Wg, L0_ffn_Wu, L0_ffn_Wd, L0_ffn_Sg, L0_ffn_Su, L0_ffn_Sd):
    import jax
    import jax.numpy as jnp

    def _L0_attn_ref(x, Wq, Wk, Wv, Wo):
        import jax, jax.numpy as jnp
        import numpy as np
        HIDDEN = 512
        NHQ = 32
        NHKV = 8
        HEAD_DIM = HIDDEN // NHQ
        THETA = 10000.0

        def _rope(x, theta_base):
            b, h, s, d = x.shape
            inv_freq = 1.0 / theta_base ** (jnp.arange(0, d, 2, dtype=jnp.float32)[:d // 2] / d)
            freqs = jnp.arange(s, dtype=jnp.float32)[:, None] * inv_freq[None, :]
            cos = jnp.cos(freqs).astype(x.dtype)
            sin = jnp.sin(freqs).astype(x.dtype)
            x1, x2 = (x[..., :d // 2], x[..., d // 2:])
            return jnp.concatenate([x1 * cos - x2 * sin, x2 * cos + x1 * sin], axis=-1)
        b, s, _ = x.shape
        q_per_kv = NHQ // NHKV
        q = (x @ Wq).reshape(b, s, NHQ, HEAD_DIM).transpose(0, 2, 1, 3)
        k = (x @ Wk).reshape(b, s, NHKV, HEAD_DIM).transpose(0, 2, 1, 3)
        v = (x @ Wv).reshape(b, s, NHKV, HEAD_DIM).transpose(0, 2, 1, 3)
        q = _rope(q, THETA)
        k = _rope(k, THETA)
        qg = q.reshape(b, NHKV, q_per_kv, s, HEAD_DIM)
        scores = jnp.einsum('bkgqd,bkmd->bkgqm', qg, k) / np.sqrt(HEAD_DIM)
        causal = jnp.tril(jnp.ones((s, s), dtype=bool))
        scores = jnp.where(causal, scores, -jnp.inf)
        attn = jax.nn.softmax(scores, axis=-1)
        out = jnp.einsum('bkgqm,bkmd->bkgqd', attn, v)
        out = out.reshape(b, NHQ, s, HEAD_DIM).transpose(0, 2, 1, 3).reshape(b, s, HIDDEN)
        return out @ Wo

    def _L0_xattn_ref(x, context, Wq, Wkv, Wout, b_out, g):
        import jax, jax.numpy as jnp
        import numpy as np
        HEADS = 8
        DIM_HEAD = 64
        DIM = 64
        HIDDEN = HEADS * DIM_HEAD
        B, N = (8, 512)
        scale = DIM_HEAD ** (-0.5)
        q = jnp.einsum('oc,bcn->bon', Wq, x)
        kv = jnp.einsum('oc,bcn->bon', Wkv, context)
        k, v = jnp.split(kv, 2, axis=1)

        def split_heads(t):
            b, hc, n = t.shape
            return t.reshape(b, HEADS, DIM_HEAD, n)
        q = jax.nn.softmax(split_heads(q), axis=-2) * scale
        k = jax.nn.softmax(split_heads(k), axis=-1)
        v = split_heads(v)
        ctx = jnp.einsum('bhdn,bhen->bhde', k, v)
        out = jnp.einsum('bhde,bhdn->bhen', ctx, q)
        b, h, e, n = out.shape
        out = out.reshape(b, h * e, n)
        out = jnp.einsum('oc,bcn->bon', Wout, out) + b_out[None, :, None]
        mean = jnp.mean(out, axis=1, keepdims=True)
        var = jnp.var(out, axis=1, keepdims=True)
        return (out - mean) * jax.lax.rsqrt(var + 1e-05) * g

    def _L0_ffn_ref(hidden_states, gate_w, bias, Wg, Wu, Wd, Sg, Su, Sd):
        import jax, jax.numpy as jnp
        import numpy as np
        H = 512
        I = 256
        E = 16
        TOPK = 4
        SI = 256
        orig_shape = hidden_states.shape
        x = hidden_states.reshape(-1, orig_shape[-1])
        scores = jax.nn.sigmoid(x @ gate_w.T) + bias
        topk_w, topk_idx = jax.lax.top_k(scores, TOPK)
        topk_w = topk_w / (jnp.sum(topk_w, axis=-1, keepdims=True) + 1e-20)
        cw = jnp.sum(jax.nn.one_hot(topk_idx, E, dtype=x.dtype) * topk_w[..., None], axis=1)
        g = jnp.einsum('th,eih->eti', x, Wg)
        u = jnp.einsum('th,eih->eti', x, Wu)
        z = jax.nn.silu(g) * u
        zw = z * cw.T[:, :, None]
        out = jnp.einsum('eti,ehi->th', zw, Wd)
        out = out + jax.nn.silu(x @ Sg.T) * (x @ Su.T) @ Sd.T
        return out.reshape(orig_shape)
    x = _layernorm(x + _L0_attn_ref(x, L0_attn_Wq, L0_attn_Wk, L0_attn_Wv, L0_attn_Wo), axis=-1)
    x = _layernorm(x + _L0_xattn_ref(x, ctx_4096, L0_xattn_Wq, L0_xattn_Wkv, L0_xattn_Wout, L0_xattn_b_out, L0_xattn_g), axis=-1)
    x = _layernorm(x + _L0_ffn_ref(x, L0_ffn_gate_w, L0_ffn_bias, L0_ffn_Wg, L0_ffn_Wu, L0_ffn_Wd, L0_ffn_Sg, L0_ffn_Su, L0_ffn_Sd), axis=-1)
    return x

_drawn_inputs = setup_inputs


def setup_inputs(seed=0):
    import zlib

    import numpy as np

    out = dict(_drawn_inputs(seed))
    spreads = {'L0_xattn_b_out': (0.0, 0.8), 'L0_xattn_g': (1.0, 0.6), 'L0_ffn_bias': (0.0, 0.535)}
    factors = {'ctx_4096': 8.0,
     'L0_xattn_Wq': 8.0,
     'L0_xattn_Wkv': 8.0,
     'L0_xattn_Wout': 8.0,
     'L0_ffn_gate_w': 4.32,
     'L0_ffn_Wg': 3.304,
     'L0_ffn_Wu': 3.262,
     'L0_ffn_Wd': 3.247}
    for name, (base, spread) in spreads.items():
        noise = np.random.default_rng([zlib.crc32(name.encode()), seed]).standard_normal(out[name].shape)
        drawn = base * np.exp(spread * noise) if base else spread * noise
        out[name] = jnp.asarray(drawn.astype(out[name].dtype))
    for name, factor in factors.items():
        out[name] = (out[name] * factor).astype(out[name].dtype)
    return out
```

```python
from contextlib import ExitStack

import concourse.bass as bass
import concourse.mybir as mybir
import numpy as np

F32, F16, BF16 = mybir.dt.float32, mybir.dt.float16, mybir.dt.bfloat16
ALU = mybir.AluOpType
ACT = mybir.ActivationFunctionType
AX = mybir.AxisListType

B, S, H = 16, 64, 512
PAIRS = B // 2
HC = H // 128
NHQ, NHKV, D = 32, 8, 16
REP = NHQ // NHKV
NKV = NHKV * D
XH, XD = 8, 64
E, TOPK, I = 16, 4, 256
EPS = 1e-5
WS = 64.0
NEG = -1e30
WEXP = 2 * I * HC + H * I // 128
ZS = 16.0


def due(count):
    return not isinstance(count, int) or count > 0


def decoder_layer(nc, d):
    ctx = ExitStack()
    with ctx:
        def sb(name, shape, dt=F32):
            return ctx.enter_context(nc.sbuf_tensor(name, shape, dt))

        pairs_stack = ExitStack()

        def sb_pairs(name, shape, dt=F32):
            return pairs_stack.enter_context(nc.sbuf_tensor(name, shape, dt))

        def sem(name):
            return ctx.enter_context(nc.semaphore(name))

        ident = sb("ident", [128, 128])
        eps = sb("eps", [128, 1])
        gbias = sb("gbias", [128, E])
        xres = sb("xres", [128, PAIRS, H])
        xf_h = sb("xf_h", [128, PAIRS, HC, 128], F16)
        xf_l = sb("xf_l", [128, PAIRS, HC, 128], F16)
        score = sb("score", [128, PAIRS, E])
        w_raw = sb("w_raw", [128, 2, WEXP])
        cw = sb("cw", [128, PAIRS, E + 1])
        before = sb("before", [128, E, E])

        rope = sb_pairs("rope", [128, 2, 16])
        kmask = sb_pairs("kmask", [128, NHKV])
        mask_q = sb_pairs("mask_q", [128, 128], BF16)
        mask_k = sb_pairs("mask_k", [128, NHKV, S], BF16)
        onesbd = sb_pairs("onesbd", [128, 128])
        wqkv_h = sb_pairs("wqkv_h", [128, HC, 768], F16)
        wqkv_l = sb_pairs("wqkv_l", [128, HC, 768], F16)
        wo = sb_pairs("wo", [128, REP, H])
        xwq_h = sb_pairs("xwq_h", [128, H], F16)
        xwq_l = sb_pairs("xwq_l", [128, H], F16)
        xwk_h = sb_pairs("xwk_h", [128, H], F16)
        xwk_l = sb_pairs("xwk_l", [128, H], F16)
        wv_in = sb_pairs("wv_in", [XD, XH, XD])
        wout_in = sb_pairs("wout_in", [XD, XH, XD])
        pbd = sb_pairs("pbd", [128, XH, 2, XD])
        pmean = sb_pairs("pmean", [128, XH])
        xvec = sb_pairs("xvec", [128, 2 + XD])
        bmean = sb_pairs("bmean", [128, 1])
        bc = sb_pairs("bc", [128, 1])
        pause = sb_pairs("pause", [128, 1])
        gw_in = sb_pairs("gw_in", [128, HC, E])
        gw_h = sb_pairs("gw_h", [128, HC, E], F16)
        gw_l = sb_pairs("gw_l", [128, HC, E], F16)

        x_st = sb_pairs("x_st", [128, H])
        xt_st = sb_pairs("xt_st", [128, HC, 128])
        xt_h = sb_pairs("xt_h", [128, HC, 128], F16)
        xt_l = sb_pairs("xt_l", [128, HC, 128], F16)
        qk_cos = sb_pairs("qk_cos", [128, NHQ + NHKV, 2, 8])
        qk_sin = sb_pairs("qk_sin", [128, NHQ + NHKV, 2, 8])
        vbd = sb_pairs("vbd", [128, 2, 4, 2, D])
        q_t = sb_pairs("q_t", [128, 2, REP, S])
        kbd = sb_pairs("kbd", [128, 2, NHKV, S])
        prob = sb_pairs("prob", [128, 2, 16, S])
        amax = sb_pairs("amax", [128, 2, 16])
        asum = sb_pairs("asum", [128, 2, 16])
        arec = sb_pairs("arec", [128, 2, 16])
        prob_t = sb_pairs("prob_t", [128, 2, 4, 256])
        o_t = sb_pairs("o_t", [128, REP, 2, S])
        y1 = sb_pairs("y1", [128, H])
        st1 = sb_pairs("st1", [128, 6])
        mv1 = sb_pairs("mv1", [128, 2])
        ln1 = sb_pairs("ln1", [128, 1])
        rstd1 = sb_pairs("rstd1", [128, 1])

        ctx_st = sb_pairs("ctx_st", [128, H])
        ctxt_st = sb_pairs("ctxt_st", [128, 4, 128])
        cs = sb_pairs("cs", [128, 2, H], F16)
        xs = sb_pairs("xs", [128, 2, H], F16)
        kmx = sb_pairs("kmx", [128, 8])
        kng = sb_pairs("kng", [128, 8])
        ksum = sb_pairs("ksum", [128, 4, 2])
        krec = sb_pairs("krec", [128, 4, 2])
        k_e = sb_pairs("k_e", [128, 2, H])
        k_t = sb_pairs("k_t", [128, 2, 4, H])
        kx = sb_pairs("kx", [128, H])
        m_t = sb_pairs("m_t", [128, 4, 2, XD])
        qmx = sb_pairs("qmx", [128, 8, XH])
        qsum = sb_pairs("qsum", [128, 8, XH])
        qrec = sb_pairs("qrec", [128, 8, XH])
        q_e = sb_pairs("q_e", [128, 2, H])
        x_q = sb_pairs("x_q", [128, 2, 4, H])
        mask_q_in = prob[:].rearrange("p b g m -> p (b g m)")[:, 0:128]
        mask_k_in = prob[:, 1, 0:NHKV, :]
        w_in = k_t[:].rearrange("p b t c -> p (b t c)")[:, 0:HC * 768].rearrange("p (c n) -> p c n", c=HC)
        xw_in = x_q[:].rearrange("p b t c -> p (b t c)")[:, 0:2 * H].rearrange("p (c n) -> p c n", c=2)
        oc = sb_pairs("oc", [128, H])
        osq = sb_pairs("osq", [128, H])
        ort = sb_pairs("ort", [128, H])
        y2 = sb_pairs("y2", [128, H])
        st2 = sb_pairs("st2", [128, 6])
        mv2 = sb_pairs("mv2", [128, 2])
        ln2 = sb_pairs("ln2", [128, 1])
        rstd2 = sb_pairs("rstd2", [128, 1])
        x2_st = sb_pairs("x2_st", [128, H])


        pa = ctx.enter_context(nc.psum_tensor("pa", [128, 1536], F32))
        pf = ctx.enter_context(nc.psum_tensor("pf", [128, 512], F32))
        pk = ctx.enter_context(nc.psum_tensor("pk", [128, 1024], F32))
        px = ctx.enter_context(nc.psum_tensor("px", [128, 1024], F32))

        pgu = pk[:].rearrange("p (i c) -> p i c", i=2)
        py = px[:].rearrange("p (i c) -> p i c", i=2)
        pzt = pf[:, 0:256]

        s_const, s_wraw = sem("s_const"), sem("s_wraw")
        s_setv, s_setp, s_seta = sem("s_setv"), sem("s_setp"), sem("s_seta")
        s_ld_xt, s_ld_x, s_ld_c, s_ld_ct = (sem(n) for n in ("s_ld_xt", "s_ld_x", "s_ld_c", "s_ld_ct"))
        s_xh, s_xl, s_qkv, s_rope, s_vbd = (sem(n) for n in ("s_xh", "s_xl", "s_qkv", "s_rope", "s_vbd"))
        s_qkt, s_qts, s_kbd, s_sc = (sem(n) for n in ("s_qkt", "s_qts", "s_kbd", "s_sc"))
        s_amax, s_asub, s_aexp, s_asum, s_arec = (sem(n) for n in ("s_amax", "s_asub", "s_aexp", "s_asum", "s_arec"))
        s_anorm, s_pt, s_pts, s_pv, s_ot, s_wo = (sem(n) for n in ("s_anorm", "s_pt", "s_pts", "s_pv", "s_ot", "s_wo"))
        s_ln1, s_rs1 = sem("s_ln1"), sem("s_rs1")
        s_ch, s_cl, s_x1h, s_x1l = (sem(n) for n in ("s_ch", "s_cl", "s_x1h", "s_x1l"))
        s_kmm, s_kmax, s_kneg, s_kexp, s_ktr, s_kts = (sem(n) for n in ("s_kmm", "s_kmax", "s_kneg", "s_kexp", "s_ktr", "s_kts"))
        s_kx, s_kxs, s_m, s_krec, s_mts = (sem(n) for n in ("s_kx", "s_kxs", "s_m", "s_krec", "s_mts"))
        s_qmm, s_qmax, s_qsub, s_qexp, s_qsum, s_qrec = (sem(n) for n in ("s_qmm", "s_qmax", "s_qsub", "s_qexp", "s_qsum", "s_qrec"))
        s_qnorm, s_qtr, s_xq = (sem(n) for n in ("s_qnorm", "s_qtr", "s_xq"))
        s_fin, s_oc, s_osq, s_var, s_vln, s_rst = (sem(n) for n in ("s_fin", "s_oc", "s_osq", "s_var", "s_vln", "s_rst"))
        s_ln2, s_rs2, s_x2st, s_x2t, s_xfh, s_xfl, s_gate, s_score = (
            sem(n) for n in ("s_ln2", "s_rs2", "s_x2st", "s_x2t", "s_xfh", "s_xfl", "s_gate", "s_score"))
        s_y2 = sem("s_y2")
        s_ldw, s_out = ([sem(f"{n}{i}") for i in range(2)] for n in ("s_ldw", "s_out"))
        s_whi, s_wlo, s_route, s_gu, s_sg, s_z, s_zt, s_zh, s_zl, s_y, s_acc = (
            sem(n) for n in ("s_whi", "s_wlo", "s_route", "s_gu", "s_sg", "s_z", "s_zt", "s_zh", "s_zl", "s_y", "s_acc"))
        s_stat3, s_rs3, s_norm3 = sem("s_stat3"), sem("s_rs3"), sem("s_norm3")


        SETA, SETV = 5, 15

        def walk(eng, attention, iteration, end):
            attention(0)
            iteration(0, True, False)
            iteration(1, True, True)
            with eng.Fori(2, PAIRS - 1) as j:
                iteration(j, True, True)
            iteration(PAIRS - 1, False, True)
            end(PAIRS - 1)

        CONSTS = [("ident", ident), ("rope", rope), ("kmask", kmask), ("mask_q", mask_q_in), ("mask_k", mask_k_in),
                  ("onesbd", onesbd)]
        RAW = [("wqkv", w_in), ("wo", wo), ("xw", xw_in), ("wv", wv_in), ("wout", wout_in), ("xvec", xvec),
               ("gw", gw_in), ("gbias", gbias), ("before", before)]

        with nc.Block() as block:
            @block.sync
            def _(sp):
                def load_a(j):
                    if due(j):
                        sp.wait_ge(s_xl, j)
                    sp.dma_start(xt_st[:], d["xt"][bass.ds(j, 1)].rearrange("o p c t -> (o p) c t")).then_inc(s_ld_xt, 16)
                    if due(4 * j - 3):
                        sp.wait_ge(s_ln1, 4 * j - 3)
                    sp.dma_start(x_st[:], d["x"][bass.ds(j, 1)].rearrange("o p h -> (o p) h")).then_inc(s_ld_x, 16)

                def load_k(j):
                    if due(2 * j):
                        sp.wait_ge(s_cl, 2 * j)
                    sp.dma_start(ctx_st[:], d["ctx"][bass.ds(j, 1)].rearrange("o p h -> (o p) h")).then_inc(s_ld_c, 16)
                    if due(j):
                        sp.wait_ge(s_kx, j)
                    sp.dma_start(ctxt_st[:], d["ctxt"][bass.ds(j, 1)].rearrange("o p c t -> (o p) c t")).then_inc(s_ld_ct, 16)

                def iteration(j, attend, finish):
                    if attend:
                        load_a(j + 1)
                        load_k(j + 1)

                for name, tile in RAW[:1]:
                    sp.dma_start(tile[:], d[name]).then_inc(s_wraw, 16)
                load_a(0)
                for name, tile in CONSTS:
                    sp.dma_start(tile[:], d[name]).then_inc(s_const, 16)
                for name, tile in RAW[1:]:
                    sp.dma_start(tile[:], d[name]).then_inc(s_wraw, 16)
                load_k(0)
                walk(sp, lambda j: None, iteration, lambda j: None)

            @block.tensor
            def _(pe):
                def qkv(j):
                    pe.wait_ge(s_xh, j + 1)
                    pe.wait_ge(s_xl, j + 1)
                    if due(4 * j - 3):
                        pe.wait_ge(s_ln1, 4 * j - 3)
                    parts = [(xt_h, wqkv_h), (xt_h, wqkv_l), (xt_l, wqkv_h)]
                    for lo, n in ((0, 512), (512, 256)):
                        for i, (x, w) in enumerate(parts):
                            for c in range(HC):
                                mm = pe.matmul(pa[:, lo:lo + n], x[:, c, :], w[:, c, lo:lo + n],
                                               start=(i == 0 and c == 0), stop=(i == 2 and c == HC - 1))
                    mm.then_inc(s_qkv, 1)

                def turn_qk(j):
                    pe.wait_ge(s_rope, 4 * j + 4)
                    if due(j):
                        pe.wait_ge(s_ot, j)
                    for r in range(REP):
                        pe.transpose(pa[:, 1024 + 128 * r:1152 + 128 * r],
                                     qk_cos[:, :, :, :].rearrange("p a b c -> p (a b c)")[:, 128 * r:128 * r + 128], ident[:])
                    pe.wait_ge(s_vbd, 4 * j + 4)
                    pe.transpose(pa[:, 768:896],
                                 qk_cos[:, :, :, :].rearrange("p a b c -> p (a b c)")[:, H:H + NKV], ident[:]).then_inc(s_qkt, 1)

                def scores(j, b):
                    if b == 0:
                        pe.wait_ge(s_qts, j + 1)
                        pe.wait_ge(s_kbd, j + 1)
                    else:
                        pe.wait_ge(s_asub, 2 * j + 1)
                    for rp in range(2):
                        out = pa[:, 512 * rp:512 * rp + 512]
                        pe.matmul(out, mask_q[:], mask_k[:].rearrange("p g m -> p (g m)"), start=True, stop=False)
                        mm = pe.matmul(out, q_t[:, b, 2 * rp:2 * rp + 2, :].rearrange("p r q -> p (r q)"),
                                       kbd[:, b].rearrange("p g m -> p (g m)"), start=False, stop=True)
                    mm.then_inc(s_sc, 1)

                PT_BANK = [1024, 1024, 0, 512]

                def turn_prob(j, t):
                    b, half = t // 2, t % 2
                    pe.wait_ge(s_anorm, 2 * j + b + 1)
                    if t == 1:
                        pe.wait_ge(s_pts, 4 * j + 1)
                    if t == 2:
                        pe.wait_ge(s_asub, 2 * j + 2)
                    for g in range(2):
                        gp = 2 * half + g
                        for rp in range(2):
                            lo = PT_BANK[t] + 256 * g + 128 * rp
                            mm = pe.transpose(pa[:, lo:lo + 128],
                                              prob[:, b, 8 * rp + 2 * gp:8 * rp + 2 * gp + 2, :].rearrange("p g m -> p (g m)"),
                                              ident[:])
                    mm.then_inc(s_pt, 1)

                def weigh_values(j):
                    for b in range(2):
                        pe.wait_ge(s_pts, 4 * j + 2 * b + 2)
                        for gp in range(4):
                            mm = pe.matmul(pa[32 * gp:32 * gp + 32, 1024 + 256 * b:1280 + 256 * b],
                                           vbd[:, b, gp].rearrange("p g d -> p (g d)"), prob_t[:, b, gp, :],
                                           start=True, stop=True)
                    mm.then_inc(s_pv, 1)

                def out_proj(j):
                    pe.wait_ge(s_ot, j + 1)
                    for r in range(REP):
                        mm = pe.matmul(pa[:, 0:512], o_t[:, r].rearrange("p b q -> p (b q)"), wo[:, r, :],
                                       start=(r == 0), stop=(r == REP - 1))
                    mm.then_inc(s_wo, 1)

                def attention(j):
                    qkv(j)
                    turn_qk(j)
                    scores(j, 0)
                    scores(j, 1)
                    for t in range(4):
                        turn_prob(j, t)
                    weigh_values(j)
                    out_proj(j)

                def k_product(j, u):
                    b, dt = u // 4, u % 4
                    if u == 0:
                        pe.wait_ge(s_cl, 2 * j + 2)
                    if due(8 * j + u):
                        pe.wait_ge(s_kexp, 8 * j + u)
                    pe.matmul(pk[:, 0:512], xwk_h[:, 128 * dt:128 * dt + 128], cs[:, b, :], start=True, stop=False)
                    pe.matmul(pk[:, 0:512], xwk_l[:, 128 * dt:128 * dt + 128], cs[:, b, :], start=False,
                              stop=True).then_inc(s_kmm, 1)

                def k_turn(j, u):
                    pe.wait_ge(s_kexp, 8 * j + u + 1)
                    if due(8 * j + u):
                        pe.wait_ge(s_kts, 8 * j + u)
                    if u == 0:
                        if due(j):
                            pe.wait_ge(s_mts, j)
                    for t in range(4):
                        mm = pe.transpose(pk[:, 512 + 128 * t:640 + 128 * t], k_e[:, u % 2, 128 * t:128 * t + 128], ident[:])
                    mm.then_inc(s_ktr, 1)

                def k_contract(j):
                    pe.wait_ge(s_kts, 8 * j + 8)
                    pe.wait_ge(s_ld_ct, 16 * (j + 1))
                    for t in range(4):
                        for b in range(2):
                            mm = pe.matmul(pk[64 * b:64 * b + 64, 0:512], ctxt_st[:, t, 64 * b:64 * b + 64], k_t[:, b, t, :],
                                           start=(t == 0), stop=(t == 3))
                    mm.then_inc(s_kx, 1)

                def k_matrix(j):
                    pe.wait_ge(s_kxs, j + 1)
                    for h in range(XH):
                        p = 64 * (h % 2)
                        mm = pe.matmul(pk[p:p + 64, 512 + 128 * (h // 2):640 + 128 * (h // 2)], kx[:, 64 * h:64 * h + 64],
                                       pbd[:, h].rearrange("p b o -> p (b o)"), start=True, stop=True)
                    mm.then_inc(s_m, 1)

                def q_product(j, u):
                    b, nt = u // 4, u % 4
                    if u == 0:
                        pe.wait_ge(s_x1l, 2 * j + 2)
                    if due(8 * j + u):
                        pe.wait_ge(s_qsub, 8 * j + u)
                    pe.matmul(px[:, 0:512], xs[:, b, 128 * nt:128 * nt + 128], xwq_h[:], start=True, stop=False)
                    pe.matmul(px[:, 0:512], xs[:, b, 128 * nt:128 * nt + 128], xwq_l[:], start=False,
                              stop=True).then_inc(s_qmm, 1)

                def q_turn(j, u):
                    pe.wait_ge(s_qnorm, 8 * j + u + 1)
                    if due(8 * j + u):
                        pe.wait_ge(s_xq, 8 * j + u)
                    for t in range(4):
                        mm = pe.transpose(px[:, 512 + 128 * t:640 + 128 * t], q_e[:, u % 2, 128 * t:128 * t + 128], ident[:])
                    mm.then_inc(s_qtr, 1)

                def final(j):
                    pe.wait_ge(s_mts, j + 1)
                    pe.wait_ge(s_xq, 8 * j + 8)
                    if due(j):
                        pe.wait_ge(s_score, j)
                    for t in range(4):
                        for b in range(2):
                            mm = pe.matmul(pf[64 * b:64 * b + 64, :], m_t[:, t, b, :], x_q[:, b, t, :],
                                           start=(t == 0), stop=(t == 3))
                    mm.then_inc(s_fin, 1)

                def variance(j):
                    pe.wait_ge(s_osq, j + 1)
                    pe.matmul(pf[:], onesbd[:], osq[:], start=True, stop=True).then_inc(s_var, 1)

                def turn_x2(j):
                    pe.wait_ge(s_ln2, 4 * j + 4)
                    pe.wait_ge(s_vln, j + 1)
                    for c in range(HC):
                        mm = pe.transpose(pf[:, 128 * c:128 * c + 128], x2_st[:, 128 * c:128 * c + 128], ident[:])
                    mm.then_inc(s_x2t, 1)

                def gate(j):
                    pe.wait_ge(s_xfl, j + 1)
                    pe.wait_ge(s_xfh, j + 1)
                    parts = [(xf_h, gw_h), (xf_h, gw_l), (xf_l, gw_h), (xf_l, gw_l)]
                    for i, (x, w) in enumerate(parts):
                        for c in range(HC):
                            mm = pe.matmul(pf[:, 0:E], x[:, bass.ds(j, 1), c, :].rearrange("p o t -> p (o t)"), w[:, c, :],
                                           start=(i == 0 and c == 0), stop=(i == 3 and c == HC - 1))
                    mm.then_inc(s_gate, 1)

                def end(j):
                    final(j)
                    variance(j)
                    turn_x2(j)
                    gate(j)

                def iteration(j, attend, finish):
                    k_product(j, 0)
                    q_product(j, 0)
                    if finish:
                        final(j - 1)
                    if attend:
                        qkv(j + 1)
                    k_turn(j, 0)
                    k_product(j, 1)
                    q_product(j, 1)
                    if finish:
                        variance(j - 1)
                    if attend:
                        turn_qk(j + 1)
                    for u in range(2, 8):
                        k_turn(j, u - 1)
                        q_turn(j, u - 2)
                        k_product(j, u)
                        q_product(j, u)
                        if attend:
                            if u == 2:
                                scores(j + 1, 0)
                            if u == 3:
                                scores(j + 1, 1)
                            if u >= 4:
                                turn_prob(j + 1, u - 4)
                        if finish:
                            if u == 4:
                                turn_x2(j - 1)
                            if u == 6:
                                gate(j - 1)
                    k_turn(j, 7)
                    q_turn(j, 6)
                    if attend:
                        weigh_values(j + 1)
                    k_contract(j)
                    q_turn(j, 7)
                    if attend:
                        out_proj(j + 1)
                    k_matrix(j)

                pe.wait_ge(s_wraw, 16 * len(RAW))
                for h in range(XH):
                    for b in range(2):
                        mm = pe.matmul(pf[64 * b:64 * b + 64, 64 * h:64 * h + 64], wv_in[:, h, :], wout_in[:, h, :],
                                       start=True, stop=True)
                mm.then_inc(s_setp, 1)
                pe.wait_ge(s_const, 16 * len(CONSTS))
                pe.wait_ge(s_setv, SETV)
                pe.wait_ge(s_seta, SETA)
                walk(pe, attention, iteration, end)

            @block.scalar
            def _(act):
                def split_x(j):
                    act.wait_ge(s_ld_xt, 16 * (j + 1))
                    if due(j):
                        act.wait_ge(s_qkv, j)
                    act.activation(xt_h[:], xt_st[:], ACT.Copy).then_inc(s_xh, 1)

                def values(j):
                    act.wait_ge(s_rope, 4 * j + 3)
                    if due(j):
                        act.wait_ge(s_pv, j)
                    for b in range(2):
                        for g in range(2):
                            act.activation(vbd[64 * g:64 * g + 64, b, :, g, :],
                                           pa[64 * b:64 * b + 64, 640:768].rearrange("p (a g d) -> p a g d", a=4, g=2)[:, :, g, :],
                                           ACT.Copy, scale=1 / WS).then_inc(s_vbd, 1)

                def q_out(j):
                    act.wait_ge(s_qkt, j + 1)
                    if due(2 * j):
                        act.wait_ge(s_sc, 2 * j)
                    act.activation(q_t[:].rearrange("p b r q -> p r b q"),
                                   pa[:, 1024:1536].rearrange("p (r b q) -> p r b q", r=REP, b=2), ACT.Copy).then_inc(s_qts, 1)

                def a_exp(j, b):
                    act.wait_ge(s_asub, 2 * j + b + 1)
                    act.activation(prob[:, b], prob[:, b], ACT.Exp, scale=D ** -0.5).then_inc(s_aexp, 1)

                PT_BANK = [1024, 1024, 0, 512]

                def prob_out(j, t):
                    b, half = t // 2, t % 2
                    act.wait_ge(s_pt, 4 * j + t + 1)
                    if t == 0:
                        if due(j):
                            act.wait_ge(s_pv, j)
                    act.activation(prob_t[:, b, 2 * half:2 * half + 2, :].rearrange("p g c -> p (g c)"),
                                   pa[:, PT_BANK[t]:PT_BANK[t] + 512], ACT.Copy).then_inc(s_pts, 1)

                def o_out(j):
                    act.wait_ge(s_pv, j + 1)
                    if due(j):
                        act.wait_ge(s_wo, j)
                    act.activation(o_t[:].rearrange("p r b q -> p b r q"),
                                   pa[:, 1024:1536].rearrange("p (b r q) -> p b r q", r=REP, b=2), ACT.Copy).then_inc(s_ot, 1)

                def root1(j):
                    act.wait_ge(s_ln1, 4 * j + 3)
                    act.activation(ln1[:], mv1[:, 1:2], ACT.Ln, bias=eps[:]).then_inc(s_rs1, 1)
                    act.wait_ge(s_rs1, 2 * j + 1)
                    act.activation(rstd1[:], ln1[:], ACT.Exp, scale=-0.5).then_inc(s_rs1, 1)

                def split_c(j):
                    act.wait_ge(s_ld_c, 16 * (j + 1))
                    if due(8 * j):
                        act.wait_ge(s_kmm, 8 * j)
                    for b in range(2):
                        act.activation(cs[64 * b:64 * b + 64, b, :], ctx_st[64 * b:64 * b + 64, :], ACT.Copy).then_inc(s_ch, 1)

                def split_x1(j):
                    act.wait_ge(s_ln1, 4 * j + 4)
                    if due(8 * j):
                        act.wait_ge(s_qmm, 8 * j)
                    for b in range(2):
                        act.activation(xs[64 * b:64 * b + 64, b, :],
                                       xres[64 * b:64 * b + 64, bass.ds(j, 1), :].rearrange("p o h -> p (o h)"),
                                       ACT.Copy).then_inc(s_x1h, 1)

                def k_exp(j, u):
                    b, dt = u // 4, u % 4
                    act.wait_ge(s_kneg, 8 * j + u + 1)
                    if due(8 * j + u - 1):
                        act.wait_ge(s_ktr, 8 * j + u - 1)
                    if u == 0:
                        if due(j):
                            act.wait_ge(s_krec, j)
                    act.activation(k_e[:, u % 2, :], pk[:, 0:512], ACT.Exp, bias=kng[:, u:u + 1], scale=1 / WS,
                                   accum_out=ksum[:, dt, b:b + 1]).then_inc(s_kexp, 1)

                def k_out(j, u):
                    b, dt = u // 4, u % 4
                    act.wait_ge(s_ktr, 8 * j + u + 1)
                    if u == 0:
                        if due(j):
                            act.wait_ge(s_kx, j)
                    act.activation(k_t[:, b, :, 128 * dt:128 * dt + 128],
                                   pk[:, 512:1024].rearrange("p (t c) -> p t c", t=4), ACT.Copy).then_inc(s_kts, 1)

                def kx_out(j):
                    act.wait_ge(s_kx, j + 1)
                    if due(j):
                        act.wait_ge(s_m, j)
                    act.activation(kx[:], pk[:, 0:512], ACT.Copy).then_inc(s_kxs, 1)

                def q_exp(j, u):
                    act.wait_ge(s_qsub, 8 * j + u + 1)
                    act.activation(q_e[:, u % 2, :], q_e[:, u % 2, :], ACT.Exp, scale=1 / WS).then_inc(s_qexp, 1)

                def q_tout(j, u):
                    b, nt = u // 4, u % 4
                    act.wait_ge(s_qtr, 8 * j + u + 1)
                    if u == 0:
                        if due(j):
                            act.wait_ge(s_fin, j)
                    act.activation(x_q[:, b, :, 128 * nt:128 * nt + 128],
                                   px[:, 512:1024].rearrange("p (t c) -> p t c", t=4), ACT.Copy).then_inc(s_xq, 1)

                def centre(j):
                    act.wait_ge(s_fin, j + 1)
                    if due(4 * j - 3):
                        act.wait_ge(s_ln2, 4 * j - 3)
                    act.activation(oc[:], pf[:], ACT.Identity, bias=bc[:]).then_inc(s_oc, 1)
                    act.wait_ge(s_oc, j + 1)
                    act.activation(osq[:], oc[:], ACT.Square).then_inc(s_osq, 1)

                def root_o(j):
                    act.wait_ge(s_var, j + 1)
                    act.activation(ort[:], pf[:], ACT.Ln, bias=eps[:]).then_inc(s_vln, 1)
                    act.wait_ge(s_vln, j + 1)
                    act.activation(ort[:], ort[:], ACT.Exp, scale=-0.5).then_inc(s_rst, 1)

                def root2(j):
                    act.wait_ge(s_ln2, 4 * j + 3)
                    act.activation(ln2[:], mv2[:, 1:2], ACT.Ln, bias=eps[:]).then_inc(s_rs2, 1)
                    act.wait_ge(s_rs2, 2 * j + 1)
                    act.activation(rstd2[:], ln2[:], ACT.Exp, scale=-0.5).then_inc(s_rs2, 1)

                def x2t_hi(j):
                    act.wait_ge(s_x2t, j + 1)
                    act.activation(xf_h[:, bass.ds(j, 1)].rearrange("p o c t -> p (o c t)"), pf[:], ACT.Copy).then_inc(s_xfh, 1)

                def score_out(j):
                    act.wait_ge(s_gate, j + 1)
                    act.activation(score[:, bass.ds(j, 1), :].rearrange("p o e -> p (o e)"), pf[:, 0:E], ACT.Exp,
                                   scale=-1 / WS).then_inc(s_score, 1)

                def attention(j):
                    split_x(j)
                    values(j)
                    q_out(j)
                    a_exp(j, 0)
                    a_exp(j, 1)
                    for t in range(4):
                        prob_out(j, t)
                    o_out(j)
                    root1(j)
                    split_c(j)
                    split_x1(j)

                def end(j):
                    centre(j)
                    root_o(j)
                    root2(j)
                    x2t_hi(j)
                    score_out(j)

                def iteration(j, attend, finish):
                    if attend:
                        split_x(j + 1)
                    k_exp(j, 0)
                    if finish:
                        centre(j - 1)
                    if attend:
                        values(j + 1)
                    q_exp(j, 0)
                    k_out(j, 0)
                    k_exp(j, 1)
                    q_exp(j, 1)
                    if finish:
                        root_o(j - 1)
                    if attend:
                        q_out(j + 1)
                    for u in range(2, 8):
                        k_out(j, u - 1)
                        q_tout(j, u - 2)
                        if finish and u == 3:
                            root2(j - 1)
                        k_exp(j, u)
                        q_exp(j, u)
                        if attend:
                            if u in (3, 4):
                                a_exp(j + 1, u - 3)
                            if u >= 5:
                                prob_out(j + 1, u - 5)
                        if finish:
                            if u == 5:
                                x2t_hi(j - 1)
                            if u == 6:
                                score_out(j - 1)
                    k_out(j, 7)
                    q_tout(j, 6)
                    if attend:
                        prob_out(j + 1, 3)
                        o_out(j + 1)
                    q_tout(j, 7)
                    kx_out(j)
                    if attend:
                        root1(j + 1)
                        split_c(j + 1)
                        split_x1(j + 1)

                act.preload_act_table_set("natural_log_exp_and_others")
                act.wait_ge(s_wraw, 16 * len(RAW))
                for lo in range(0, HC, 2):
                    act.activation(wqkv_h[:, lo:lo + 2, :], w_in[:, lo:lo + 2, :], ACT.Copy, scale=WS).then_inc(s_seta, 1)
                act.activation(xwq_h[:], xw_in[:, 0, :], ACT.Copy, scale=WS).then_inc(s_seta, 1)
                act.activation(xwk_h[:], xw_in[:, 1, :], ACT.Copy, scale=WS).then_inc(s_seta, 1)
                act.activation(gw_h[:], gw_in[:], ACT.Copy, scale=WS).then_inc(s_seta, 1)
                act.wait_ge(s_setv, SETV)
                walk(act, attention, iteration, end)


            @block.vector
            def _(dve):
                def split_x(j):
                    dve.wait_ge(s_ld_xt, 16 * (j + 1))
                    dve.wait_ge(s_xh, j + 1)
                    if due(j):
                        dve.wait_ge(s_qkv, j)
                    dve.tensor_tensor(xt_l[:], xt_st[:], xt_h[:], ALU.subtract).then_inc(s_xl, 1)

                def rotate(j):
                    dve.wait_ge(s_qkv, j + 1)
                    if due(j):
                        dve.wait_ge(s_qkt, j)
                    qk = pa[:, 0:H + NKV].rearrange("p (a b c) -> p a b c", b=2, c=8)
                    n = NHQ + NHKV
                    dve.tensor_tensor(qk_cos[:].rearrange("p a b c -> p a (b c)"), qk.rearrange("p a b c -> p a (b c)"),
                                      rope[:, 0, :].unsqueeze(1).to_broadcast([128, n, 16]), ALU.mult).then_inc(s_rope, 1)
                    for half in range(2):
                        dve.tensor_tensor(qk_sin[:, :, half, :], qk[:, :, 1 - half, :],
                                          rope[:, 1, 8 * half:8 * half + 8].unsqueeze(1).to_broadcast([128, n, 8]),
                                          ALU.mult).then_inc(s_rope, 1)
                    dve.wait_ge(s_rope, 4 * j + 3)
                    dve.tensor_tensor(qk_cos[:], qk_cos[:], qk_sin[:], ALU.add).then_inc(s_rope, 1)

                def key_blocks(j):
                    dve.wait_ge(s_qkt, j + 1)
                    if due(2 * j):
                        dve.wait_ge(s_sc, 2 * j)
                    dve.tensor_tensor(kbd[:],
                                      pa[:, 768:896].rearrange("p (b m) -> p b m", b=2).unsqueeze(2).to_broadcast([128, 2, NHKV, S]),
                                      kmask[:].unsqueeze(1).unsqueeze(3).to_broadcast([128, 2, NHKV, S]), ALU.mult).then_inc(s_kbd, 1)

                def a_softmax(j, b):
                    sc = pa[:, 0:1024].rearrange("p (g m) -> p g m", m=S)
                    dve.wait_ge(s_sc, 2 * j + b + 1)
                    dve.tensor_reduce(amax[:, b, :], sc, AX.X, ALU.max).then_inc(s_amax, 1)
                    dve.wait_ge(s_amax, 2 * j + b + 1)
                    if due(4 * j - 2 + 2 * b):
                        dve.wait_ge(s_pt, 4 * j - 2 + 2 * b)
                    dve.tensor_tensor(prob[:, b], sc, amax[:, b, :].unsqueeze(2).to_broadcast([128, 16, S]),
                                      ALU.subtract).then_inc(s_asub, 1)

                def a_total(j, b):
                    dve.wait_ge(s_aexp, 2 * j + b + 1)
                    dve.tensor_reduce(asum[:, b, :], prob[:, b], AX.X, ALU.add).then_inc(s_asum, 1)
                    dve.wait_ge(s_asum, 2 * j + b + 1)
                    if due(2 * j - 1 + b):
                        dve.wait_ge(s_anorm, 2 * j - 1 + b)
                    dve.reciprocal(arec[:, b, :], asum[:, b, :]).then_inc(s_arec, 1)

                def norm1_stats(j):
                    dve.wait_ge(s_wo, j + 1)
                    dve.wait_ge(s_ld_x, 16 * (j + 1))
                    dve.tensor_tensor(y1[:], pa[:, 0:512], x_st[:], ALU.add).then_inc(s_ln1, 1)
                    dve.wait_ge(s_ln1, 4 * j + 1)
                    dve.bn_stats(st1[:], y1[:]).then_inc(s_ln1, 1)
                    dve.wait_ge(s_ln1, 4 * j + 2)
                    dve.memset(pause[:], 0.0)
                    dve.bn_aggr(mv1[:], st1[:]).then_inc(s_ln1, 1)

                def norm1(j):
                    dve.wait_ge(s_rs1, 2 * j + 2)
                    dve.tensor_scalar(xres[:, bass.ds(j, 1), :].rearrange("p o h -> p (o h)"), y1[:], mv1[:, 0:1], rstd1[:],
                                      ALU.subtract, ALU.mult).then_inc(s_ln1, 1)

                def split_c(j):
                    dve.wait_ge(s_ch, 2 * j + 2)
                    if due(8 * j):
                        dve.wait_ge(s_kmm, 8 * j)
                    for b in range(2):
                        dve.tensor_tensor(cs[64 - 64 * b:128 - 64 * b, b, :], ctx_st[64 * b:64 * b + 64, :],
                                          cs[64 * b:64 * b + 64, b, :], ALU.subtract).then_inc(s_cl, 1)

                def split_x1(j):
                    dve.wait_ge(s_x1h, 2 * j + 2)
                    if due(8 * j):
                        dve.wait_ge(s_qmm, 8 * j)
                    for b in range(2):
                        dve.tensor_tensor(xs[64 - 64 * b:128 - 64 * b, b, :],
                                          xres[64 * b:64 * b + 64, bass.ds(j, 1), :].rearrange("p o h -> p (o h)"),
                                          xs[64 * b:64 * b + 64, b, :], ALU.subtract).then_inc(s_x1l, 1)

                def k_max(j, u):
                    dve.wait_ge(s_kmm, 8 * j + u + 1)
                    dve.tensor_reduce(kmx[:, u:u + 1], pk[:, 0:512], AX.X, ALU.max).then_inc(s_kmax, 1)
                    dve.wait_ge(s_kmax, 8 * j + u + 1)
                    if due(8 * j - 7 + u):
                        dve.wait_ge(s_kexp, 8 * j - 7 + u)
                    dve.tensor_scalar(kng[:, u:u + 1], kmx[:, u:u + 1], -1 / WS, None, ALU.mult).then_inc(s_kneg, 1)

                def q_max(j, u):
                    q = px[:, 0:512].rearrange("p (h d) -> p h d", d=XD)
                    dve.wait_ge(s_qmm, 8 * j + u + 1)
                    dve.tensor_reduce(qmx[:, u, :], q, AX.X, ALU.max).then_inc(s_qmax, 1)
                    dve.wait_ge(s_qmax, 8 * j + u + 1)
                    if due(8 * j + u - 1):
                        dve.wait_ge(s_qtr, 8 * j + u - 1)
                    dve.tensor_tensor(q_e[:, u % 2, :].rearrange("p (h d) -> p h d", d=XD), q,
                                      qmx[:, u, :].unsqueeze(2).to_broadcast([128, XH, XD]), ALU.subtract).then_inc(s_qsub, 1)

                def q_total(j, u):
                    dve.wait_ge(s_qexp, 8 * j + u + 1)
                    dve.tensor_reduce(qsum[:, u, :], q_e[:, u % 2, :].rearrange("p (h d) -> p h d", d=XD), AX.X,
                                      ALU.add).then_inc(s_qsum, 1)
                    dve.wait_ge(s_qsum, 8 * j + u + 1)
                    if due(8 * j - 7 + u):
                        dve.wait_ge(s_qnorm, 8 * j - 7 + u)
                    dve.reciprocal(qrec[:, u, :], qsum[:, u, :]).then_inc(s_qrec, 1)

                def k_sums(j):
                    dve.wait_ge(s_kexp, 8 * j + 8)
                    if due(j):
                        dve.wait_ge(s_mts, j)
                    dve.reciprocal(krec[:], ksum[:]).then_inc(s_krec, 1)

                def m_out(j):
                    dve.wait_ge(s_m, j + 1)
                    dve.wait_ge(s_krec, j + 1)
                    if due(j):
                        dve.wait_ge(s_fin, j)
                    dve.scalar_tensor_tensor(m_t[:].rearrange("p t b o -> p (t b) o"),
                                             pk[:, 512:1024].rearrange("p (g o) -> p g o", o=XD), XD ** -0.5,
                                             krec[:].rearrange("p t b -> p (t b)").unsqueeze(2).to_broadcast([128, 8, XD]),
                                             ALU.mult, ALU.mult).then_inc(s_mts, 1)

                def norm2_stats(j):
                    dve.wait_ge(s_rst, j + 1)
                    dve.scalar_tensor_tensor(y2[:], oc[:], xvec[:, 1:2], ort[:], ALU.mult, ALU.mult).then_inc(s_ln2, 1)
                    dve.wait_ge(s_ln2, 4 * j + 1)
                    dve.tensor_tensor(y2[:], y2[:], xres[:, bass.ds(j, 1), :].rearrange("p o h -> p (o h)"),
                                      ALU.add).then_inc(s_y2, 1)
                    dve.wait_ge(s_y2, j + 1)
                    dve.bn_stats(st2[:], y2[:]).then_inc(s_ln2, 1)
                    dve.wait_ge(s_ln2, 4 * j + 2)
                    dve.memset(pause[:], 0.0)
                    dve.bn_aggr(mv2[:], st2[:]).then_inc(s_ln2, 1)

                def norm2(j):
                    dve.wait_ge(s_rs2, 2 * j + 2)
                    if due(j):
                        dve.wait_ge(s_x2st, j)
                    dve.tensor_scalar(x2_st[:], y2[:], mv2[:, 0:1], rstd2[:], ALU.subtract, ALU.mult).then_inc(s_ln2, 1)

                def x2t_lo(j):
                    dve.wait_ge(s_xfh, j + 1)
                    dve.tensor_tensor(xf_l[:, bass.ds(j, 1)].rearrange("p o c t -> p (o c t)"), pf[:],
                                      xf_h[:, bass.ds(j, 1)].rearrange("p o c t -> p (o c t)"), ALU.subtract).then_inc(s_xfl, 1)

                def attention(j):
                    split_x(j)
                    rotate(j)
                    key_blocks(j)
                    for b in range(2):
                        a_softmax(j, b)
                    for b in range(2):
                        a_total(j, b)
                    norm1_stats(j)
                    norm1(j)
                    split_c(j)
                    split_x1(j)

                def end(j):
                    norm2_stats(j)
                    norm2(j)
                    x2t_lo(j)

                def iteration(j, attend, finish):
                    if attend:
                        split_x(j + 1)
                    k_max(j, 0)
                    q_max(j, 0)
                    if attend:
                        rotate(j + 1)
                    k_max(j, 1)
                    q_max(j, 1)
                    q_total(j, 0)
                    if attend:
                        key_blocks(j + 1)
                    for u in range(2, 8):
                        k_max(j, u)
                        q_max(j, u)
                        q_total(j, u - 1)
                        if finish and u == 2:
                            norm2_stats(j - 1)
                        if finish and u == 3:
                            norm2(j - 1)
                        if finish and u == 5:
                            x2t_lo(j - 1)
                        if attend:
                            if u == 2:
                                a_softmax(j + 1, 0)
                            if u == 3:
                                a_softmax(j + 1, 1)
                            if u == 4:
                                a_total(j + 1, 0)
                            if u == 5:
                                a_total(j + 1, 1)
                    q_total(j, 7)
                    k_sums(j)
                    if attend:
                        norm1_stats(j + 1)
                    m_out(j)
                    if attend:
                        norm1(j + 1)
                        split_c(j + 1)
                        split_x1(j + 1)

                dve.memset(vbd[:], 0.0).then_inc(s_setv, 1)
                dve.memset(pbd[:], 0.0).then_inc(s_setv, 1)
                dve.memset(eps[:], EPS).then_inc(s_setv, 1)
                dve.wait_ge(s_wraw, 16 * len(RAW))
                dve.wait_ge(s_const, 16 * len(CONSTS))
                dve.wait_ge(s_seta, SETA)
                for raw, hi, lo in ((w_in[:], wqkv_h[:], wqkv_l[:]), (xw_in[:, 0, :], xwq_h[:], xwq_l[:]),
                                    (xw_in[:, 1, :], xwk_h[:], xwk_l[:]), (gw_in[:], gw_h[:], gw_l[:])):
                    dve.scalar_tensor_tensor(lo, raw, WS, hi, ALU.mult, ALU.subtract).then_inc(s_setv, 1)
                dve.tensor_reduce(bmean[:], xvec[:, 2:2 + XD], AX.X, ALU.add).then_inc(s_setv, 1)
                dve.wait_ge(s_setp, 1)
                dve.tensor_reduce(pmean[:], pf[:].rearrange("p (h o) -> p h o", o=XD), AX.X, ALU.add).then_inc(s_setv, 1)
                dve.wait_ge(s_setv, 9)
                dve.scalar_tensor_tensor(bc[:], bmean[:], -1 / XD, xvec[:, 0:1], ALU.mult, ALU.add).then_inc(s_setv, 1)
                dve.tensor_scalar(pmean[:], pmean[:], 1 / XD, None, ALU.mult).then_inc(s_setv, 1)
                dve.wait_ge(s_setv, 11)
                for b in range(2):
                    rows = slice(64 * b, 64 * b + 64)
                    dve.tensor_tensor(pbd[rows, :, b, :], pf[rows, :].rearrange("p (h o) -> p h o", o=XD),
                                      pmean[rows, :].unsqueeze(2).to_broadcast([64, XH, XD]), ALU.subtract).then_inc(s_setv, 1)
                dve.tensor_copy(mask_q[:], mask_q_in).then_inc(s_setv, 1)
                dve.tensor_copy(mask_k[:], mask_k_in).then_inc(s_setv, 1)
                walk(dve, attention, iteration, end)

            @block.gpsimd
            def _(pool):
                def a_norm(j, b):
                    pool.wait_ge(s_arec, 2 * j + b + 1)
                    pool.tensor_tensor(prob[:, b], prob[:, b], arec[:, b, :].unsqueeze(2).to_broadcast([128, 16, S]),
                                       ALU.mult).then_inc(s_anorm, 1)

                def q_norm(j, u):
                    pool.wait_ge(s_qrec, 8 * j + u + 1)
                    q = q_e[:, u % 2, :].rearrange("p (h d) -> p h d", d=XD)
                    pool.tensor_tensor(q, q, qrec[:, u, :].unsqueeze(2).to_broadcast([128, XH, XD]),
                                       ALU.mult).then_inc(s_qnorm, 1)

                def keep_x2(j):
                    pool.wait_ge(s_ln2, 4 * j + 4)
                    pool.wait_ge(s_x2t, j + 1)
                    pool.tensor_copy(xres[:, bass.ds(j, 1), :].rearrange("p o h -> p (o h)"), x2_st[:]).then_inc(s_x2st, 1)

                def attention(j):
                    a_norm(j, 0)
                    a_norm(j, 1)

                def iteration(j, attend, finish):
                    for u in range(8):
                        q_norm(j, u)
                        if attend and u == 3:
                            a_norm(j + 1, 0)
                        if attend and u == 4:
                            a_norm(j + 1, 1)
                        if finish and u == 6:
                            keep_x2(j - 1)

                walk(pool, attention, iteration, keep_x2)

        pairs_stack.close()
        w_h = sb("w_h", [128, 2, WEXP], F16)
        w_l = sb("w_l", [128, 2, WEXP], F16)
        sg = sb("sg", [128, 2, I])
        z = sb("z", [128, 2, I])
        z_h = sb("z_h", [128, 2, 128], F16)
        z_l = sb("z_l", [128, 2, 128], F16)
        sig = sb("sig", [128, PAIRS, E])
        rank = sb("rank", [128, PAIRS, E])
        total = sb("total", [128, PAIRS])
        st3 = sb("st3", [128, PAIRS, 6])
        mv3 = sb("mv3", [128, PAIRS, 2])
        ln3 = sb("ln3", [128, PAIRS, 1])
        rstd3 = sb("rstd3", [128, PAIRS, 1])
        y3 = sb("y3", [128, 2, H])
        cmp_gt = sb("cmp_gt", [128, PAIRS, E, E])
        cmp_eq = sb("cmp_eq", [128, PAIRS, E, E])

        def experts(eng, one):
            for par in range(2):
                one(par, par, 0)
            with eng.Fori(1, E // 2) as p:
                for par in range(2):
                    one(2 * p + par, par, p)
            one(E, 0, E // 2)

        with nc.Block() as block:
            @block.sync
            def _(sp):
                def one(e, par, p):
                    if due(e - 1):
                        sp.wait_ge(s_wlo, e - 1)
                    sp.dma_start(w_raw[:, par], d["wexp"][bass.ds(e, 1)].rearrange("o p c -> (o p) c")).then_inc(s_ldw[par], 16)

                experts(sp, one)
                for i in range(PAIRS):
                    sp.wait_ge(s_norm3, i + 1)
                    sp.dma_start(d["out"][i], y3[:, i % 2]).then_inc(s_out[i % 2], 16)
                for sent in s_out:
                    sp.wait_ge(sent, 16 * (PAIRS // 2))

            @block.tensor
            def _(pe):
                def one(e, par, p):
                    pe.wait_ge(s_whi, e + 1)
                    pe.wait_ge(s_wlo, e + 1)
                    for i in range(PAIRS + 1):
                        if i < PAIRS:
                            if due(8 * e + i - 1):
                                pe.wait_ge(s_z, 8 * e + i - 1)
                            for n, (x, w) in enumerate(((xf_h, w_h), (xf_h, w_l), (xf_l, w_h))):
                                for c in range(HC):
                                    mm = pe.matmul(pgu[:, i % 2, :], x[:, i, c, :], w[:, par, 512 * c:512 * c + 512],
                                                   start=(n == 0 and c == 0), stop=(n == 2 and c == HC - 1))
                            mm.then_inc(s_gu, 1)
                        if i >= 1:
                            t = i - 1
                            pe.wait_ge(s_z, 8 * e + t + 1)
                            if due(8 * e + t):
                                pe.wait_ge(s_zl, 8 * e + t)
                            for c in range(2):
                                mm = pe.transpose(pzt[:, 128 * c:128 * c + 128], z[:, t % 2, 128 * c:128 * c + 128], ident[:])
                            mm.then_inc(s_zt, 1)
                            pe.wait_ge(s_zl, 8 * e + t + 1)
                            if due(8 * e + t - 1):
                                pe.wait_ge(s_acc, 8 * e + t - 1)
                            for n, (x, w) in enumerate(((z_h, w_h), (z_h, w_l), (z_l, w_h))):
                                for c in range(2):
                                    mm = pe.matmul(py[:, t % 2, :], x[:, c, :], w[:, par, 2048 + 512 * c:2560 + 512 * c],
                                                   start=(n == 0 and c == 0), stop=(n == 2 and c == 1))
                            mm.then_inc(s_y, 1)

                experts(pe, one)

            @block.scalar
            def _(act):
                def one(e, par, p):
                    act.wait_ge(s_ldw[par], 16 * (p + 1))
                    if due(8 * e - 8):
                        act.wait_ge(s_y, 8 * e - 8)
                    act.activation(w_h[:, par], w_raw[:, par], ACT.Copy, scale=WS).then_inc(s_whi, 1)
                    for i in range(PAIRS + 1):
                        if i < PAIRS:
                            act.wait_ge(s_gu, 8 * e + i + 1)
                            if due(8 * e + i - 1):
                                act.wait_ge(s_z, 8 * e + i - 1)
                            act.activation(sg[:, i % 2, :], pgu[:, i % 2, 0:I], ACT.Silu, scale=1 / WS).then_inc(s_sg, 1)
                        if i >= 1:
                            t = i - 1
                            act.wait_ge(s_zt, 8 * e + t + 1)
                            if due(8 * e + t):
                                act.wait_ge(s_y, 8 * e + t)
                            act.activation(z_h[:].rearrange("p c t -> p (c t)"), pzt[:], ACT.Copy).then_inc(s_zh, 1)

                experts(act, one)
                for i in range(PAIRS):
                    act.wait_ge(s_stat3, 2 * i + 2)
                    act.activation(ln3[:, i, :], mv3[:, i, 1:2], ACT.Ln, bias=eps[:]).then_inc(s_rs3, 1)
                    act.wait_ge(s_rs3, 2 * i + 1)
                    act.activation(rstd3[:, i, :], ln3[:, i, :], ACT.Exp, scale=-0.5).then_inc(s_rs3, 1)

            @block.vector
            def _(dve):
                steps = 0

                def step(ins):
                    nonlocal steps
                    ins.then_inc(s_route, 1)
                    steps += 1
                    dve.wait_ge(s_route, steps)

                def by_expert(a):
                    return a.unsqueeze(2).to_broadcast([128, PAIRS, E, E])

                step(dve.memset(cw[:, :, E:E + 1], ZS / WS))
                step(dve.tensor_scalar(sig[:], score[:], 1.0, None, ALU.add))
                step(dve.reciprocal(sig[:], sig[:]))
                step(dve.tensor_tensor(sig[:], sig[:], gbias[:].unsqueeze(1).to_broadcast([128, PAIRS, E]), ALU.add))
                other, own = sig[:].unsqueeze(2).to_broadcast([128, PAIRS, E, E]), sig[:].unsqueeze(3).to_broadcast([128, PAIRS, E, E])
                step(dve.tensor_tensor(cmp_gt[:], other, own, ALU.is_gt))
                step(dve.tensor_tensor(cmp_eq[:], other, own, ALU.is_equal))
                step(dve.tensor_tensor(cmp_eq[:], cmp_eq[:], before[:].unsqueeze(1).to_broadcast([128, PAIRS, E, E]), ALU.mult))
                step(dve.tensor_tensor(cmp_gt[:], cmp_gt[:], cmp_eq[:], ALU.add))
                step(dve.tensor_reduce(rank[:], cmp_gt[:], AX.X, ALU.add))
                step(dve.tensor_scalar(rank[:], rank[:], TOPK - 0.5, None, ALU.is_lt))
                step(dve.tensor_tensor(sig[:], sig[:], rank[:], ALU.mult))
                step(dve.tensor_reduce(total[:], sig[:], AX.X, ALU.add))
                step(dve.tensor_scalar(total[:], total[:], 1e-20, None, ALU.add))
                step(dve.reciprocal(total[:], total[:]))
                step(dve.tensor_scalar(total[:], total[:], ZS / WS, None, ALU.mult))
                step(dve.tensor_tensor(cw[:, :, 0:E], sig[:], total[:].unsqueeze(2).to_broadcast([128, PAIRS, E]), ALU.mult))

                def one(e, par, p):
                    dve.wait_ge(s_whi, e + 1)
                    if due(8 * e - 8):
                        dve.wait_ge(s_y, 8 * e - 8)
                    dve.scalar_tensor_tensor(w_l[:, par], w_raw[:, par], WS, w_h[:, par], ALU.mult, ALU.subtract).then_inc(s_wlo, 1)
                    for i in range(PAIRS + 2):
                        if i < PAIRS:
                            dve.wait_ge(s_sg, 8 * e + i + 1)
                            if due(8 * e + i - 1):
                                dve.wait_ge(s_zt, 8 * e + i - 1)
                            dve.scalar_tensor_tensor(z[:, i % 2, :], pgu[:, i % 2, I:2 * I],
                                                     cw[:, i, bass.ds(e, 1)], sg[:, i % 2, :],
                                                     ALU.mult, ALU.mult).then_inc(s_z, 1)
                        if 1 <= i <= PAIRS:
                            t = i - 1
                            dve.wait_ge(s_zh, 8 * e + t + 1)
                            dve.tensor_tensor(z_l[:].rearrange("p c t -> p (c t)"), pzt[:],
                                              z_h[:].rearrange("p c t -> p (c t)"), ALU.subtract).then_inc(s_zl, 1)
                        if i >= 2:
                            t = i - 2
                            dve.wait_ge(s_y, 8 * e + t + 1)
                            if due(8 * e + t - 7):
                                dve.wait_ge(s_acc, 8 * e + t - 7)
                            dve.scalar_tensor_tensor(xres[:, t, :], py[:, t % 2, :], 1 / (WS * ZS), xres[:, t, :],
                                                     ALU.mult, ALU.add).then_inc(s_acc, 1)

                experts(dve, one)
                for i in range(PAIRS):
                    dve.wait_ge(s_acc, 8 * E + i + 1)
                    dve.bn_stats(st3[:, i, :], xres[:, i, :]).then_inc(s_stat3, 1)
                    dve.wait_ge(s_stat3, 2 * i + 1)
                    dve.bn_aggr(mv3[:, i, :], st3[:, i, :]).then_inc(s_stat3, 1)
                for i in range(PAIRS):
                    dve.wait_ge(s_rs3, 2 * i + 2)
                    if due(16 * (i // 2)):
                        dve.wait_ge(s_out[i % 2], 16 * (i // 2))
                    dve.tensor_scalar(y3[:, i % 2], xres[:, i, :], mv3[:, i, 0:1], rstd3[:, i, :],
                                      ALU.subtract, ALU.mult).then_inc(s_norm3, 1)



def layouts(i):
    c = np.ascontiguousarray
    x = i["x"].reshape(PAIRS, 128, H)
    cx = i["ctx_4096"].reshape(PAIRS, 128, H)
    wq = i["L0_attn_Wq"].reshape(H, NHKV, REP, D).transpose(0, 2, 1, 3).reshape(H, H)
    wo = i["L0_attn_Wo"].reshape(NHKV, REP, D, H).transpose(1, 0, 2, 3).reshape(REP, 128, H)
    wqkv = np.concatenate([wq, i["L0_attn_Wk"], i["L0_attn_Wv"]], 1)
    xwkv = i["L0_xattn_Wkv"]
    dup = lambda w: np.concatenate([w, w], 0)
    b, g = i["L0_xattn_b_out"], i["L0_xattn_g"].reshape(XD)
    inv = (1.0 / np.float32(10000.0) ** (np.arange(0, D, 2, dtype=np.float32) / D)).astype(np.float32)
    ang = (np.arange(S, dtype=np.float32)[:, None] * inv[None, :]).astype(np.float32)
    cos, sin = np.cos(ang) / np.float32(WS), np.sin(ang) / np.float32(WS)
    rope = np.stack([np.concatenate([cos, cos], 1), np.concatenate([-sin, sin], 1)], 1)
    q = np.arange(S)
    mask_k = np.where(q[None, :] > q[:, None], np.float32(NEG), np.float32(0))[:, None, :].repeat(NHKV, 1)
    mask_q = np.tile(np.eye(S, dtype=np.float32), (1, 2))
    mask_q, mask_k = (np.concatenate([m, np.zeros_like(m)], 0) for m in (mask_q, mask_k))
    wg, wu, wd = (np.concatenate([i["L0_ffn_W" + n], i["L0_ffn_S" + n][None]], 0) for n in "gud")
    gu = np.stack([wg, wu], 1).transpose(0, 3, 1, 2).reshape(E + 1, HC, 128, 2 * I).transpose(0, 2, 1, 3)
    down = wd.transpose(0, 2, 1).reshape(E + 1, I // 128, 128, H).transpose(0, 2, 1, 3)
    wexp = np.concatenate([gu.reshape(E + 1, 128, -1), down.reshape(E + 1, 128, -1)], 2)
    return {
        "wexp": c(wexp), "before": c(np.broadcast_to(np.tril(np.ones((E, E), np.float32), -1), (128, E, E))),
        "x": c(x), "xt": c(x.reshape(PAIRS, 128, HC, 128).transpose(0, 3, 2, 1)),
        "ctx": c(cx), "ctxt": c(cx.reshape(PAIRS, 128, 4, 128).transpose(0, 3, 2, 1)),
        "wqkv": c(wqkv.reshape(HC, 128, 768).transpose(1, 0, 2)), "wo": c(wo.transpose(1, 0, 2)),
        "xw": c(np.stack([dup(i["L0_xattn_Wq"].T), dup(xwkv[:H].T)], 1)),
        "wv": c(xwkv[H:].reshape(XH, XD, XD).transpose(1, 0, 2)),
        "wout": c(i["L0_xattn_Wout"].T.reshape(XH, XD, XD).transpose(1, 0, 2)),
        "xvec": c(np.concatenate([dup(b[:, None]), dup(g[:, None]), np.broadcast_to(b, (128, XD))], 1)),
        "gw": c(i["L0_ffn_gate_w"].T.reshape(HC, 128, E).transpose(1, 0, 2)),
        "gbias": c(np.broadcast_to(i["L0_ffn_bias"], (128, E))),
        "ident": np.eye(128, dtype=np.float32), "rope": c(dup(rope)),
        "kmask": c(np.repeat(np.eye(NHKV, dtype=np.float32), D, 0)),
        "mask_q": c(mask_q), "mask_k": c(mask_k),
        "onesbd": c(np.kron(np.eye(2, dtype=np.float32), np.full((S, S), 1 / S, np.float32))),
    }


def kernel(**inputs):
    import concourse.bacc as bacc
    from concourse.bass_utils import run_bass_kernel_spmd

    arrays = {f"{n}_dram": a for n, a in layouts({n: np.asarray(a) for n, a in inputs.items()}).items()}
    nc = bacc.Bacc("TRN2", target_bir_lowering=False, num_devices=1)
    d = {n[:-5]: nc.dram_tensor(n, a.shape, mybir.dt.from_np(a.dtype), kind="ExternalInput").ap() for n, a in arrays.items()}
    d["out"] = nc.dram_tensor("out_dram", (PAIRS, 128, H), F32, kind="ExternalOutput").ap()
    decoder_layer(nc, d)
    r = run_bass_kernel_spmd(nc, [arrays], core_ids=[0])
    return r.results[0]["out_dram"].reshape(B, S, H)
```

```python
from contextlib import ExitStack

import concourse.bass as bass
import concourse.mybir as mybir
import numpy as np

F32, F16, BF16, U32 = mybir.dt.float32, mybir.dt.float16, mybir.dt.bfloat16, mybir.dt.uint32
ALU = mybir.AluOpType
ACT = mybir.ActivationFunctionType
AX = mybir.AxisListType

B, S, H = 16, 64, 512
PAIRS = B // 2
HC = H // 128
NHQ, NHKV, D = 32, 8, 16
REP = NHQ // NHKV
NKV = NHKV * D
XH, XD = 8, 64
E, TOPK, I = 16, 4, 256
EPS = 1e-5
WS = 64.0
NEG = -1e30
BLOCKS = B * S * TOPK // 256 + E
TILES = 2 * BLOCKS
SEL_STEP, PAIRS_STEP, ROWS_STEP, TABLES_STEP = 9, 24, 28, 43
WEXP = 2 * I * HC + H * I // 128
ZS = 16.0


def due(count):
    return not isinstance(count, int) or count > 0


def decoder_layer(nc, d):
    ctx = ExitStack()
    with ctx:
        def sb(name, shape, dt=F32):
            return ctx.enter_context(nc.sbuf_tensor(name, shape, dt))

        pairs_stack = ExitStack()

        def sb_pairs(name, shape, dt=F32):
            return pairs_stack.enter_context(nc.sbuf_tensor(name, shape, dt))

        def sem(name):
            return ctx.enter_context(nc.semaphore(name))

        ident = sb("ident", [128, 128])
        eps = sb("eps", [128, 1])
        gbias = sb("gbias", [128, E])
        xres = sb("xres", [128, PAIRS, H])
        xf_h = sb("xf_h", [128, PAIRS, HC, 128], F16)
        xf_l = sb("xf_l", [128, PAIRS, HC, 128], F16)
        score = sb("score", [128, PAIRS, E])
        sh_raw_t = sb("sh_raw", [128, WEXP])
        before = sb("before", [128, E, E])

        rope = sb_pairs("rope", [128, 2, 16])
        kmask = sb_pairs("kmask", [128, NHKV])
        mask_q = sb_pairs("mask_q", [128, 128], BF16)
        mask_k = sb_pairs("mask_k", [128, NHKV, S], BF16)
        onesbd = sb_pairs("onesbd", [128, 128])
        wqkv_h = sb_pairs("wqkv_h", [128, HC, 768], F16)
        wqkv_l = sb_pairs("wqkv_l", [128, HC, 768], F16)
        wo = sb_pairs("wo", [128, REP, H])
        xwq_h = sb_pairs("xwq_h", [128, H], F16)
        xwq_l = sb_pairs("xwq_l", [128, H], F16)
        xwk_h = sb_pairs("xwk_h", [128, H], F16)
        xwk_l = sb_pairs("xwk_l", [128, H], F16)
        wv_in = sb_pairs("wv_in", [XD, XH, XD])
        wout_in = sb_pairs("wout_in", [XD, XH, XD])
        pbd = sb_pairs("pbd", [128, XH, 2, XD])
        pmean = sb_pairs("pmean", [128, XH])
        xvec = sb_pairs("xvec", [128, 2 + XD])
        bmean = sb_pairs("bmean", [128, 1])
        bc = sb_pairs("bc", [128, 1])
        pause = sb_pairs("pause", [128, 1])
        gw_in = sb_pairs("gw_in", [128, HC, E])
        gw_h = sb_pairs("gw_h", [128, HC, E], F16)
        gw_l = sb_pairs("gw_l", [128, HC, E], F16)

        x_st = sb_pairs("x_st", [128, H])
        xt_st = sb_pairs("xt_st", [128, HC, 128])
        xt_h = sb_pairs("xt_h", [128, HC, 128], F16)
        xt_l = sb_pairs("xt_l", [128, HC, 128], F16)
        qk_cos = sb_pairs("qk_cos", [128, NHQ + NHKV, 2, 8])
        qk_sin = sb_pairs("qk_sin", [128, NHQ + NHKV, 2, 8])
        vbd = sb_pairs("vbd", [128, 2, 4, 2, D])
        q_t = sb_pairs("q_t", [128, 2, REP, S])
        kbd = sb_pairs("kbd", [128, 2, NHKV, S])
        prob = sb_pairs("prob", [128, 2, 16, S])
        amax = sb_pairs("amax", [128, 2, 16])
        asum = sb_pairs("asum", [128, 2, 16])
        arec = sb_pairs("arec", [128, 2, 16])
        prob_t = sb_pairs("prob_t", [128, 2, 4, 256])
        o_t = sb_pairs("o_t", [128, REP, 2, S])
        y1 = sb_pairs("y1", [128, H])
        st1 = sb_pairs("st1", [128, 6])
        mv1 = sb_pairs("mv1", [128, 2])
        ln1 = sb_pairs("ln1", [128, 1])
        rstd1 = sb_pairs("rstd1", [128, 1])

        ctx_st = sb_pairs("ctx_st", [128, H])
        ctxt_st = sb_pairs("ctxt_st", [128, 4, 128])
        cs = sb_pairs("cs", [128, 2, H], F16)
        xs = sb_pairs("xs", [128, 2, H], F16)
        kmx = sb_pairs("kmx", [128, 8])
        kng = sb_pairs("kng", [128, 8])
        ksum = sb_pairs("ksum", [128, 4, 2])
        krec = sb_pairs("krec", [128, 4, 2])
        k_e = sb_pairs("k_e", [128, 2, H])
        k_t = sb_pairs("k_t", [128, 2, 4, H])
        kx = sb_pairs("kx", [128, H])
        m_t = sb_pairs("m_t", [128, 4, 2, XD])
        qmx = sb_pairs("qmx", [128, 8, XH])
        qsum = sb_pairs("qsum", [128, 8, XH])
        qrec = sb_pairs("qrec", [128, 8, XH])
        q_e = sb_pairs("q_e", [128, 2, H])
        x_q = sb_pairs("x_q", [128, 2, 4, H])
        mask_q_in = prob[:].rearrange("p b g m -> p (b g m)")[:, 0:128]
        mask_k_in = prob[:, 1, 0:NHKV, :]
        zero = sb_pairs("zero", [128, H])
        w_in = k_t[:].rearrange("p b t c -> p (b t c)")[:, 0:HC * 768].rearrange("p (c n) -> p c n", c=HC)
        xw_in = x_q[:].rearrange("p b t c -> p (b t c)")[:, 0:2 * H].rearrange("p (c n) -> p c n", c=2)
        oc = sb_pairs("oc", [128, H])
        osq = sb_pairs("osq", [128, H])
        ort = sb_pairs("ort", [128, H])
        y2 = sb_pairs("y2", [128, H])
        st2 = sb_pairs("st2", [128, 6])
        mv2 = sb_pairs("mv2", [128, 2])
        ln2 = sb_pairs("ln2", [128, 1])
        rstd2 = sb_pairs("rstd2", [128, 1])
        x2_st = sb_pairs("x2_st", [128, H])

        sh_raw = sh_raw_t[:]

        x2_rows = nc.dram_tensor("x2_rows", (B * S, H), F32, kind="Internal").ap()
        y_rows = nc.dram_tensor("y_rows", (TILES * 128, H), F32, kind="Internal").ap()

        pa = ctx.enter_context(nc.psum_tensor("pa", [128, 1536], F32))
        pf = ctx.enter_context(nc.psum_tensor("pf", [128, 512], F32))
        pk = ctx.enter_context(nc.psum_tensor("pk", [128, 1024], F32))
        px = ctx.enter_context(nc.psum_tensor("px", [128, 1024], F32))

        pgu = pk[:].rearrange("p (i c) -> p i c", i=2)
        py = px[:].rearrange("p (i c) -> p i c", i=2)
        pzt = pf[:, 0:256]

        s_const, s_wraw, s_wqkv, s_wh, s_wl = (sem(n) for n in ("s_const", "s_wraw", "s_wqkv", "s_wh", "s_wl"))
        s_setv, s_setp, s_seta = sem("s_setv"), sem("s_setp"), sem("s_seta")
        s_ld_xt, s_ld_x, s_ld_c, s_ld_ct = (sem(n) for n in ("s_ld_xt", "s_ld_x", "s_ld_c", "s_ld_ct"))
        s_xh, s_xl, s_qkv, s_rope, s_vbd = (sem(n) for n in ("s_xh", "s_xl", "s_qkv", "s_rope", "s_vbd"))
        s_qkt, s_qts, s_kbd, s_sc = (sem(n) for n in ("s_qkt", "s_qts", "s_kbd", "s_sc"))
        s_amax, s_asub, s_aexp, s_asum, s_arec = (sem(n) for n in ("s_amax", "s_asub", "s_aexp", "s_asum", "s_arec"))
        s_anorm, s_pt, s_pts, s_pv, s_ot, s_wo = (sem(n) for n in ("s_anorm", "s_pt", "s_pts", "s_pv", "s_ot", "s_wo"))
        s_ln1, s_rs1 = sem("s_ln1"), sem("s_rs1")
        s_ch, s_cl, s_x1h, s_x1l = (sem(n) for n in ("s_ch", "s_cl", "s_x1h", "s_x1l"))
        s_kmm, s_kmax, s_kneg, s_kexp, s_ktr, s_kts = (sem(n) for n in ("s_kmm", "s_kmax", "s_kneg", "s_kexp", "s_ktr", "s_kts"))
        s_kx, s_kxs, s_m, s_krec, s_mts = (sem(n) for n in ("s_kx", "s_kxs", "s_m", "s_krec", "s_mts"))
        s_qmm, s_qmax, s_qsub, s_qexp, s_qsum, s_qrec = (sem(n) for n in ("s_qmm", "s_qmax", "s_qsub", "s_qexp", "s_qsum", "s_qrec"))
        s_qnorm, s_qtr, s_xq = (sem(n) for n in ("s_qnorm", "s_qtr", "s_xq"))
        s_fin, s_oc, s_osq, s_var, s_vln, s_rst = (sem(n) for n in ("s_fin", "s_oc", "s_osq", "s_var", "s_vln", "s_rst"))
        s_ln2, s_rs2, s_x2st, s_x2t, s_xfh, s_xfl, s_gate, s_score = (
            sem(n) for n in ("s_ln2", "s_rs2", "s_x2st", "s_x2t", "s_xfh", "s_xfl", "s_gate", "s_score"))
        s_y2 = sem("s_y2")
        s_zero, s_ldsh, s_x2w = sem("s_zero"), sem("s_ldsh"), sem("s_x2w")
        s_out = [sem(f"s_out{i}") for i in range(4)]
        s_route, s_gu, s_sg, s_z, s_zt, s_zh, s_zl, s_y, s_acc = (
            sem(n) for n in ("s_route", "s_gu", "s_sg", "s_z", "s_zt", "s_zh", "s_zl", "s_y", "s_acc"))
        s_stat3, s_rs3, s_norm3 = sem("s_stat3"), sem("s_rs3"), sem("s_norm3")


        SETA, SETV, SETM = 3, 15, 10

        def walk(eng, attention, iteration):
            attention(0)
            iteration(0, True, True, False)
            iteration(1, True, True, True)
            with eng.Fori(2, PAIRS - 1) as j:
                iteration(j, True, True, True)
            iteration(PAIRS - 1, False, True, True)
            iteration(PAIRS, False, False, True)

        def q_tile(j, u, lag):
            v = u - 2 - lag
            return (j, v) if v >= 0 else (j - 1, v + 8)

        def q_runs(j, u, lag, keys, prev):
            return keys if u - 2 - lag >= 0 else prev

        def k_tile(j, u):
            return (j, u - 1) if u >= 1 else (j - 1, 7)

        def k_runs(u, keys, prev):
            return keys if u >= 1 else prev

        CONSTS = [("ident", ident), ("rope", rope), ("kmask", kmask), ("mask_q", mask_q_in), ("mask_k", mask_k_in),
                  ("onesbd", onesbd)]
        RAW = [("wo", wo), ("xw", xw_in), ("wv", wv_in), ("wout", wout_in), ("xvec", xvec),
               ("gw", gw_in), ("gbias", gbias), ("before", before)]

        with nc.Block() as block:
            @block.sync
            def _(sp):
                def load_xt(j):
                    if due(j):
                        sp.wait_ge(s_xl, j)
                    sp.dma_start(xt_st[:], d["xt"][bass.ds(j, 1)].rearrange("o p c t -> (o p) c t")).then_inc(s_ld_xt, 16)

                def load_x(j):
                    if due(4 * j - 3):
                        sp.wait_ge(s_ln1, 4 * j - 3)
                    sp.dma_start(x_st[:], d["x"][bass.ds(j, 1)].rearrange("o p h -> (o p) h")).then_inc(s_ld_x, 16)

                def load_c(j):
                    if due(2 * j):
                        sp.wait_ge(s_cl, 2 * j)
                    sp.dma_start(ctx_st[:], d["ctx"][bass.ds(j, 1)].rearrange("o p h -> (o p) h")).then_inc(s_ld_c, 16)

                def load_ct(j):
                    if due(j):
                        sp.wait_ge(s_kx, j)
                    sp.dma_start(ctxt_st[:], d["ctxt"][bass.ds(j, 1)].rearrange("o p c t -> (o p) c t")).then_inc(s_ld_ct, 16)

                def iteration(j, last):
                    if last < 2:
                        load_xt(j + 2)
                    load_ct(j)
                    if last < 3:
                        load_x(j + 1)
                        load_c(j + 1)

                def store_x2(j):
                    sp.wait_ge(s_x2st, j + 1)
                    if due(16 * j):
                        sp.wait_ge(s_x2w, 16 * j)
                    sp.dma_start(x2_rows[bass.ds(128 * j, 128)], xres[:, bass.ds(j, 1), :].rearrange("p o h -> p (o h)")).then_inc(s_x2w, 16)

                sp.dma_start(w_in[:], d["wqkv"]).then_inc(s_wqkv, 16)
                load_xt(0)
                for name, tile in CONSTS:
                    sp.dma_start(tile[:], d[name]).then_inc(s_const, 16)
                for name, tile in RAW:
                    sp.dma_start(tile[:], d[name]).then_inc(s_wraw, 16)
                load_c(0)
                load_x(0)
                load_xt(1)
                iteration(0, 1)
                iteration(1, 1)
                with sp.Fori(2, PAIRS - 2) as j:
                    iteration(j, 1)
                    store_x2(j - 2)
                sp.dma_start(y_rows[128 * TILES // 2:].rearrange("(t p) h -> p t h", p=128),
                             zero[:].unsqueeze(1).to_broadcast([128, TILES // 2, H])).then_inc(s_zero, 16)
                iteration(PAIRS - 2, 2)
                store_x2(PAIRS - 4)
                iteration(PAIRS - 1, 3)
                store_x2(PAIRS - 3)
                sp.dma_start(sh_raw, d["wsh"]).then_inc(s_ldsh, 16)
                store_x2(PAIRS - 2)
                store_x2(PAIRS - 1)
                sp.wait_ge(s_zero, 16)

            @block.tensor
            def _(pe):
                def qkv(j):
                    pe.wait_ge(s_xh, j + 1)
                    pe.wait_ge(s_xl, j + 1)
                    if due(j):
                        pe.wait_ge(s_ot, j)
                    if due(4 * j - 3):
                        pe.wait_ge(s_ln1, 4 * j - 3)
                    parts = [(xt_h, wqkv_h), (xt_h, wqkv_l), (xt_l, wqkv_h)]
                    for lo, n in ((0, 512), (512, 256)):
                        for i, (x, w) in enumerate(parts):
                            for c in range(HC):
                                mm = pe.matmul(pa[:, lo:lo + n], x[:, c, :], w[:, c, lo:lo + n],
                                               start=(i == 0 and c == 0), stop=(i == 2 and c == HC - 1))
                    mm.then_inc(s_qkv, 1)

                def turn_qk(j):
                    pe.wait_ge(s_rope, 4 * j + 4)
                    for r in range(REP):
                        pe.transpose(pa[:, 1024 + 128 * r:1152 + 128 * r],
                                     qk_cos[:, :, :, :].rearrange("p a b c -> p (a b c)")[:, 128 * r:128 * r + 128], ident[:])
                    pe.wait_ge(s_vbd, 4 * j + 4)
                    pe.transpose(pa[:, 768:896],
                                 qk_cos[:, :, :, :].rearrange("p a b c -> p (a b c)")[:, H:H + NKV], ident[:]).then_inc(s_qkt, 1)

                def scores(j, b):
                    if b == 0:
                        pe.wait_ge(s_qts, j + 1)
                        pe.wait_ge(s_kbd, j + 1)
                    else:
                        pe.wait_ge(s_asub, 2 * j + 1)
                    for rp in range(2):
                        out = pa[:, 512 * rp:512 * rp + 512]
                        pe.matmul(out, mask_q[:], mask_k[:].rearrange("p g m -> p (g m)"), start=True, stop=False)
                        mm = pe.matmul(out, q_t[:, b, 2 * rp:2 * rp + 2, :].rearrange("p r q -> p (r q)"),
                                       kbd[:, b].rearrange("p g m -> p (g m)"), start=False, stop=True)
                    mm.then_inc(s_sc, 1)

                PT_BANK = [1024, 0, 512, 1024]

                def turn_prob(j, t):
                    b, half = t // 2, t % 2
                    pe.wait_ge(s_anorm, 2 * j + b + 1)
                    if t == 1:
                        pe.wait_ge(s_asub, 2 * j + 2)
                    if t == 3:
                        pe.wait_ge(s_pts, 4 * j + 1)
                    for g in range(2):
                        gp = 2 * half + g
                        for rp in range(2):
                            lo = PT_BANK[t] + 256 * g + 128 * rp
                            mm = pe.transpose(pa[:, lo:lo + 128],
                                              prob[:, b, 8 * rp + 2 * gp:8 * rp + 2 * gp + 2, :].rearrange("p g m -> p (g m)"),
                                              ident[:])
                    mm.then_inc(s_pt, 1)

                def weigh_values(j):
                    for b in range(2):
                        pe.wait_ge(s_pts, 4 * j + 2 * b + 2)
                        for gp in range(4):
                            mm = pe.matmul(pa[32 * gp:32 * gp + 32, 256 * b:256 * b + 256],
                                           vbd[:, b, gp].rearrange("p g d -> p (g d)"), prob_t[:, b, gp, :],
                                           start=True, stop=True)
                    mm.then_inc(s_pv, 1)

                def out_proj(j):
                    pe.wait_ge(s_ot, j + 1)
                    for r in range(REP):
                        mm = pe.matmul(pa[:, 512:1024], o_t[:, r].rearrange("p b q -> p (b q)"), wo[:, r, :],
                                       start=(r == 0), stop=(r == REP - 1))
                    mm.then_inc(s_wo, 1)

                def setup():
                    pe.wait_ge(s_wraw, 16 * len(RAW))
                    for h in range(XH):
                        for b in range(2):
                            mm = pe.matmul(pf[64 * b:64 * b + 64, 64 * h:64 * h + 64], wv_in[:, h, :], wout_in[:, h, :],
                                           start=True, stop=True)
                    mm.then_inc(s_setp, 1)

                def attention(j):
                    pe.wait_ge(s_wl, 2)
                    qkv(j)
                    setup()
                    pe.wait_ge(s_const, 16 * len(CONSTS))
                    turn_qk(j)
                    pe.wait_ge(s_setv, SETM)
                    scores(j, 0)
                    scores(j, 1)
                    for t in range(4):
                        turn_prob(j, t)
                    weigh_values(j)
                    out_proj(j)
                    pe.wait_ge(s_setv, SETV)
                    pe.wait_ge(s_seta, SETA)

                def k_product(j, u):
                    b, dt = u // 4, u % 4
                    if dt == 0:
                        pe.wait_ge(s_cl, 2 * j + b + 1)
                    if due(8 * j + u):
                        pe.wait_ge(s_kexp, 8 * j + u)
                    pe.matmul(pk[:, 0:512], xwk_h[:, 128 * dt:128 * dt + 128], cs[:, b, :], start=True, stop=False)
                    pe.matmul(pk[:, 0:512], xwk_l[:, 128 * dt:128 * dt + 128], cs[:, b, :], start=False,
                              stop=True).then_inc(s_kmm, 1)

                def k_turn(j, u):
                    pe.wait_ge(s_kexp, 8 * j + u + 1)
                    if due(8 * j + u):
                        pe.wait_ge(s_kts, 8 * j + u)
                    for t in range(4):
                        mm = pe.transpose(pk[:, 512 + 128 * t:640 + 128 * t], k_e[:, u % 2, 128 * t:128 * t + 128], ident[:])
                    mm.then_inc(s_ktr, 1)

                def k_contract(j):
                    pe.wait_ge(s_kts, 8 * j + 8)
                    pe.wait_ge(s_ld_ct, 16 * (j + 1))
                    if due(j):
                        pe.wait_ge(s_score, j)
                    for t in range(4):
                        for b in range(2):
                            mm = pe.matmul(pf[64 * b:64 * b + 64, :], ctxt_st[:, t, 64 * b:64 * b + 64], k_t[:, b, t, :],
                                           start=(t == 0), stop=(t == 3))
                    mm.then_inc(s_kx, 1)

                def k_matrix(j):
                    pe.wait_ge(s_kxs, j + 1)
                    for h in range(XH):
                        p = 64 * (h % 2)
                        mm = pe.matmul(pf[p:p + 64, 128 * (h // 2):128 * (h // 2) + 128], kx[:, 64 * h:64 * h + 64],
                                       pbd[:, h].rearrange("p b o -> p (b o)"), start=True, stop=True)
                    mm.then_inc(s_m, 1)

                def q_product(j, u):
                    b, nt = u // 4, u % 4
                    if nt == 0:
                        pe.wait_ge(s_x1l, 2 * j + b + 1)
                    if due(8 * j + u):
                        pe.wait_ge(s_qsub, 8 * j + u)
                    pe.matmul(px[:, 0:512], xs[:, b, 128 * nt:128 * nt + 128], xwq_h[:], start=True, stop=False)
                    pe.matmul(px[:, 0:512], xs[:, b, 128 * nt:128 * nt + 128], xwq_l[:], start=False,
                              stop=True).then_inc(s_qmm, 1)

                def q_turn(j, u):
                    pe.wait_ge(s_qnorm, 8 * j + u + 1)
                    if due(8 * j + u):
                        pe.wait_ge(s_xq, 8 * j + u)
                    for t in range(4):
                        mm = pe.transpose(px[:, 512 + 128 * t:640 + 128 * t], q_e[:, u % 2, 128 * t:128 * t + 128], ident[:])
                    mm.then_inc(s_qtr, 1)

                def final(j):
                    pe.wait_ge(s_mts, j + 1)
                    pe.wait_ge(s_xq, 8 * j + 8)
                    for t in range(4):
                        for b in range(2):
                            mm = pe.matmul(pf[64 * b:64 * b + 64, :], m_t[:, t, b, :], x_q[:, b, t, :],
                                           start=(t == 0), stop=(t == 3))
                    mm.then_inc(s_fin, 1)

                def variance(j):
                    pe.wait_ge(s_osq, j + 1)
                    pe.matmul(pf[:], onesbd[:], osq[:], start=True, stop=True).then_inc(s_var, 1)

                def turn_x2(j):
                    pe.wait_ge(s_ln2, 4 * j + 4)
                    pe.wait_ge(s_vln, j + 1)
                    for c in range(HC):
                        mm = pe.transpose(pf[:, 128 * c:128 * c + 128], x2_st[:, 128 * c:128 * c + 128], ident[:])
                    mm.then_inc(s_x2t, 1)

                def gate(j):
                    pe.wait_ge(s_xfl, j + 1)
                    pe.wait_ge(s_xfh, j + 1)
                    parts = [(xf_h, gw_h), (xf_h, gw_l), (xf_l, gw_h), (xf_l, gw_l)]
                    for i, (x, w) in enumerate(parts):
                        for c in range(HC):
                            mm = pe.matmul(pf[:, 0:E], x[:, bass.ds(j, 1), c, :].rearrange("p o t -> p (o t)"), w[:, c, :],
                                           start=(i == 0 and c == 0), stop=(i == 3 and c == HC - 1))
                    mm.then_inc(s_gate, 1)

                def iteration(j, attend, keys, prev):
                    for u in range(8):
                        qj, qu = q_tile(j, u, 0)
                        tj, tu = q_tile(j, u, 2)
                        if q_runs(j, u, 2, keys, prev):
                            q_turn(tj, tu)
                        if keys:
                            k_product(j, u)
                        if k_runs(u, keys, prev):
                            k_turn(*k_tile(j, u))
                        if q_runs(j, u, 0, keys, prev):
                            q_product(qj, qu)
                        if prev and u == 5:
                            variance(j - 1)
                        if prev:
                            if u == 0:
                                k_contract(j - 1)
                            if u == 2:
                                k_matrix(j - 1)
                            if u == 4:
                                final(j - 1)
                        if attend:
                            if u == 1:
                                qkv(j + 1)
                            if u == 2:
                                turn_qk(j + 1)
                            if u == 3:
                                scores(j + 1, 0)
                            if u == 4:
                                scores(j + 1, 1)
                            if u == 5:
                                turn_prob(j + 1, 0)
                                turn_prob(j + 1, 1)
                            if u == 6:
                                turn_prob(j + 1, 2)
                                turn_prob(j + 1, 3)
                            if u == 7:
                                weigh_values(j + 1)
                        if prev:
                            if u == 6:
                                turn_x2(j - 1)
                            if u == 7:
                                gate(j - 1)
                        if attend and u == 7:
                            out_proj(j + 1)

                walk(pe, attention, iteration)

            @block.scalar
            def _(act):
                def split_x(j):
                    act.wait_ge(s_ld_xt, 16 * (j + 1))
                    if due(j):
                        act.wait_ge(s_qkv, j)
                    act.activation(xt_h[:], xt_st[:], ACT.Copy).then_inc(s_xh, 1)

                def values(j):
                    act.wait_ge(s_rope, 4 * j + 3)
                    if due(j):
                        act.wait_ge(s_pv, j)
                    for b in range(2):
                        for g in range(2):
                            act.activation(vbd[64 * g:64 * g + 64, b, :, g, :],
                                           pa[64 * b:64 * b + 64, 640:768].rearrange("p (a g d) -> p a g d", a=4, g=2)[:, :, g, :],
                                           ACT.Copy, scale=1 / WS).then_inc(s_vbd, 1)

                def q_out(j):
                    act.wait_ge(s_qkt, j + 1)
                    if due(2 * j):
                        act.wait_ge(s_sc, 2 * j)
                    act.activation(q_t[:].rearrange("p b r q -> p r b q"),
                                   pa[:, 1024:1536].rearrange("p (r b q) -> p r b q", r=REP, b=2), ACT.Copy).then_inc(s_qts, 1)

                def a_exp(j, b):
                    act.wait_ge(s_asub, 2 * j + b + 1)
                    act.activation(prob[:, b], prob[:, b], ACT.Exp, scale=D ** -0.5).then_inc(s_aexp, 1)

                PT_BANK = [1024, 0, 512, 1024]

                def prob_out(j, t):
                    b, half = t // 2, t % 2
                    act.wait_ge(s_pt, 4 * j + t + 1)
                    if t == 0:
                        if due(j):
                            act.wait_ge(s_pv, j)
                    act.activation(prob_t[:, b, 2 * half:2 * half + 2, :].rearrange("p g c -> p (g c)"),
                                   pa[:, PT_BANK[t]:PT_BANK[t] + 512], ACT.Copy).then_inc(s_pts, 1)

                def o_out(j):
                    act.wait_ge(s_pv, j + 1)
                    if due(j):
                        act.wait_ge(s_wo, j)
                    act.activation(o_t[:].rearrange("p r b q -> p b r q"),
                                   pa[:, 0:512].rearrange("p (b r q) -> p b r q", r=REP, b=2), ACT.Copy).then_inc(s_ot, 1)

                def root1(j):
                    act.wait_ge(s_ln1, 4 * j + 3)
                    act.activation(ln1[:], mv1[:, 1:2], ACT.Ln, bias=eps[:]).then_inc(s_rs1, 1)
                    act.wait_ge(s_rs1, 2 * j + 1)
                    act.activation(rstd1[:], ln1[:], ACT.Exp, scale=-0.5).then_inc(s_rs1, 1)

                def split_c(j, b):
                    act.wait_ge(s_ld_c, 16 * (j + 1))
                    if due(8 * j - 4 + 4 * b):
                        act.wait_ge(s_kmm, 8 * j - 4 + 4 * b)
                    act.activation(cs[64 * b:64 * b + 64, b, :], ctx_st[64 * b:64 * b + 64, :], ACT.Copy).then_inc(s_ch, 1)

                def split_x1(j, b):
                    act.wait_ge(s_ln1, 4 * j + 4)
                    if due(8 * j - 4 + 4 * b):
                        act.wait_ge(s_qmm, 8 * j - 4 + 4 * b)
                    act.activation(xs[64 * b:64 * b + 64, b, :],
                                   xres[64 * b:64 * b + 64, bass.ds(j, 1), :].rearrange("p o h -> p (o h)"),
                                   ACT.Copy).then_inc(s_x1h, 1)

                def k_exp(j, u):
                    b, dt = u // 4, u % 4
                    act.wait_ge(s_kmax, 8 * j + u + 1)
                    if due(8 * j + u - 1):
                        act.wait_ge(s_ktr, 8 * j + u - 1)
                    if u == 0:
                        if due(j):
                            act.wait_ge(s_krec, j)
                    act.activation(k_e[:, u % 2, :], pk[:, 0:512], ACT.Exp, bias=kmx[:, u:u + 1], scale=-1.0,
                                   accum_out=ksum[:, dt, b:b + 1]).then_inc(s_kexp, 1)

                def k_out(j, u):
                    b, dt = u // 4, u % 4
                    act.wait_ge(s_ktr, 8 * j + u + 1)
                    if u == 0:
                        if due(j):
                            act.wait_ge(s_kx, j)
                    act.activation(k_t[:, b, :, 128 * dt:128 * dt + 128],
                                   pk[:, 512:1024].rearrange("p (t c) -> p t c", t=4), ACT.Copy).then_inc(s_kts, 1)

                def kx_out(j):
                    act.wait_ge(s_kx, j + 1)
                    if due(j):
                        act.wait_ge(s_m, j)
                    act.activation(kx[:], pf[:], ACT.Copy).then_inc(s_kxs, 1)

                def q_exp(j, u):
                    act.wait_ge(s_qsub, 8 * j + u + 1)
                    act.activation(q_e[:, u % 2, :], q_e[:, u % 2, :], ACT.Exp, scale=1 / WS).then_inc(s_qexp, 1)

                def q_tout(j, u):
                    b, nt = u // 4, u % 4
                    act.wait_ge(s_qtr, 8 * j + u + 1)
                    if u == 0:
                        if due(j):
                            act.wait_ge(s_fin, j)
                    act.activation(x_q[:, b, :, 128 * nt:128 * nt + 128],
                                   px[:, 512:1024].rearrange("p (t c) -> p t c", t=4), ACT.Copy).then_inc(s_xq, 1)

                def centre(j):
                    act.wait_ge(s_fin, j + 1)
                    if due(4 * j - 3):
                        act.wait_ge(s_ln2, 4 * j - 3)
                    act.activation(oc[:], pf[:], ACT.Identity, bias=bc[:]).then_inc(s_oc, 1)
                    act.wait_ge(s_oc, j + 1)
                    act.activation(osq[:], oc[:], ACT.Square).then_inc(s_osq, 1)

                def root_o(j):
                    act.wait_ge(s_var, j + 1)
                    act.activation(ort[:], pf[:], ACT.Ln, bias=eps[:]).then_inc(s_vln, 1)
                    act.wait_ge(s_vln, j + 1)
                    act.activation(ort[:], ort[:], ACT.Exp, scale=-0.5).then_inc(s_rst, 1)

                def root2(j):
                    act.wait_ge(s_ln2, 4 * j + 3)
                    act.activation(ln2[:], mv2[:, 1:2], ACT.Ln, bias=eps[:]).then_inc(s_rs2, 1)
                    act.wait_ge(s_rs2, 2 * j + 1)
                    act.activation(rstd2[:], ln2[:], ACT.Exp, scale=-0.5).then_inc(s_rs2, 1)

                def x2t_hi(j):
                    act.wait_ge(s_x2t, j + 1)
                    act.activation(xf_h[:, bass.ds(j, 1)].rearrange("p o c t -> p (o c t)"), pf[:], ACT.Copy).then_inc(s_xfh, 1)

                def score_out(j):
                    act.wait_ge(s_gate, j + 1)
                    act.activation(score[:, bass.ds(j, 1), :].rearrange("p o e -> p (o e)"), pf[:, 0:E], ACT.Copy,
                                   scale=-1 / WS).then_inc(s_score, 1)

                def setup():
                    act.wait_ge(s_wraw, 16 * len(RAW))
                    act.activation(xwq_h[:], xw_in[:, 0, :], ACT.Copy, scale=WS).then_inc(s_seta, 1)
                    act.activation(xwk_h[:], xw_in[:, 1, :], ACT.Copy, scale=-1.0).then_inc(s_seta, 1)
                    act.activation(gw_h[:], gw_in[:], ACT.Copy, scale=WS).then_inc(s_seta, 1)

                def attention(j):
                    split_x(j)
                    setup()
                    act.wait_ge(s_setv, SETM)
                    values(j)
                    q_out(j)
                    a_exp(j, 0)
                    a_exp(j, 1)
                    for t in range(4):
                        prob_out(j, t)
                    o_out(j)
                    split_c(j, 0)
                    split_c(j, 1)
                    root1(j)
                    split_x1(j, 0)
                    split_x1(j, 1)
                    act.wait_ge(s_setv, SETV)

                def iteration(j, attend, keys, prev):
                    for u in range(8):
                        qj, qu = q_tile(j, u, 0)
                        tj, tu = q_tile(j, u, 2)
                        if attend and u == 0:
                            split_x(j + 1)
                        if attend and u == 7:
                            o_out(j + 1)
                        if q_runs(j, u, 2, keys, prev):
                            q_tout(tj, tu)
                        if k_runs(u, keys, prev):
                            k_out(*k_tile(j, u))
                        if prev:
                            if u == 1:
                                kx_out(j - 1)
                            if u == 5:
                                root_o(j - 1)
                        if keys:
                            k_exp(j, u)
                        if q_runs(j, u, 0, keys, prev):
                            q_exp(qj, qu)
                        if keys and prev:
                            if u == 0:
                                split_c(j, 1)
                                root1(j)
                            if u in (1, 2):
                                split_x1(j, u - 1)
                        if prev:
                            if u == 4:
                                centre(j - 1)
                            if u == 5:
                                root2(j - 1)
                            if u == 6:
                                x2t_hi(j - 1)
                            if u == 7:
                                score_out(j - 1)
                        if attend:
                            if u == 1:
                                values(j + 1)
                            if u == 2:
                                q_out(j + 1)
                            if u in (3, 4):
                                a_exp(j + 1, u - 3)
                            if u == 5:
                                prob_out(j + 1, 0)
                                prob_out(j + 1, 1)
                            if u == 6:
                                split_c(j + 1, 0)
                                prob_out(j + 1, 2)
                                prob_out(j + 1, 3)

                act.preload_act_table_set("natural_log_exp_and_others")
                act.wait_ge(s_wqkv, 16)
                for c in range(0, HC, 2):
                    act.activation(wqkv_h[:, c:c + 2, :], w_in[:, c:c + 2, :], ACT.Copy, scale=WS).then_inc(s_wh, 1)
                walk(act, attention, iteration)


            @block.vector
            def _(dve):
                def rotate(j):
                    dve.wait_ge(s_qkv, j + 1)
                    if due(j):
                        dve.wait_ge(s_qkt, j)
                    qk = pa[:, 0:H + NKV].rearrange("p (a b c) -> p a b c", b=2, c=8)
                    n = NHQ + NHKV
                    dve.tensor_tensor(qk_cos[:].rearrange("p a b c -> p a (b c)"), qk.rearrange("p a b c -> p a (b c)"),
                                      rope[:, 0, :].unsqueeze(1).to_broadcast([128, n, 16]), ALU.mult).then_inc(s_rope, 1)
                    for half in range(2):
                        dve.tensor_tensor(qk_sin[:, :, half, :], qk[:, :, 1 - half, :],
                                          rope[:, 1, 8 * half:8 * half + 8].unsqueeze(1).to_broadcast([128, n, 8]),
                                          ALU.mult).then_inc(s_rope, 1)
                    dve.wait_ge(s_rope, 4 * j + 3)
                    dve.tensor_tensor(qk_cos[:], qk_cos[:], qk_sin[:], ALU.add).then_inc(s_rope, 1)

                def key_blocks(j):
                    dve.wait_ge(s_qkt, j + 1)
                    if due(2 * j):
                        dve.wait_ge(s_sc, 2 * j)
                    dve.tensor_tensor(kbd[:],
                                      pa[:, 768:896].rearrange("p (b m) -> p b m", b=2).unsqueeze(2).to_broadcast([128, 2, NHKV, S]),
                                      kmask[:].unsqueeze(1).unsqueeze(3).to_broadcast([128, 2, NHKV, S]), ALU.mult).then_inc(s_kbd, 1)

                def a_softmax(j, b):
                    sc = pa[:, 0:1024].rearrange("p (g m) -> p g m", m=S)
                    dve.wait_ge(s_sc, 2 * j + b + 1)
                    dve.tensor_reduce(amax[:, b, :], sc, AX.X, ALU.max).then_inc(s_amax, 1)
                    dve.wait_ge(s_amax, 2 * j + b + 1)
                    if due(4 * j - 2 + 2 * b):
                        dve.wait_ge(s_pt, 4 * j - 2 + 2 * b)
                    dve.tensor_tensor(prob[:, b], sc, amax[:, b, :].unsqueeze(2).to_broadcast([128, 16, S]),
                                      ALU.subtract).then_inc(s_asub, 1)

                def a_total(j, b):
                    dve.wait_ge(s_aexp, 2 * j + b + 1)
                    dve.tensor_reduce(asum[:, b, :], prob[:, b], AX.X, ALU.add).then_inc(s_asum, 1)
                    dve.wait_ge(s_asum, 2 * j + b + 1)
                    if due(2 * j - 1 + b):
                        dve.wait_ge(s_anorm, 2 * j - 1 + b)
                    dve.reciprocal(arec[:, b, :], asum[:, b, :]).then_inc(s_arec, 1)

                def norm1_stats(j):
                    dve.wait_ge(s_wo, j + 1)
                    dve.wait_ge(s_ld_x, 16 * (j + 1))
                    dve.tensor_tensor(y1[:], pa[:, 512:1024], x_st[:], ALU.add).then_inc(s_ln1, 1)
                    dve.wait_ge(s_ln1, 4 * j + 1)
                    dve.bn_stats(st1[:], y1[:]).then_inc(s_ln1, 1)
                    dve.wait_ge(s_ln1, 4 * j + 2)
                    dve.memset(pause[:], 0.0)
                    dve.bn_aggr(mv1[:], st1[:]).then_inc(s_ln1, 1)

                def norm1(j):
                    dve.wait_ge(s_rs1, 2 * j + 2)
                    dve.tensor_scalar(xres[:, bass.ds(j, 1), :].rearrange("p o h -> p (o h)"), y1[:], mv1[:, 0:1], rstd1[:],
                                      ALU.subtract, ALU.mult).then_inc(s_ln1, 1)

                def k_max(j, u):
                    dve.wait_ge(s_kmm, 8 * j + u + 1)
                    if due(8 * j - 7 + u):
                        dve.wait_ge(s_kexp, 8 * j - 7 + u)
                    dve.tensor_reduce(kmx[:, u:u + 1], pk[:, 0:512], AX.X, ALU.min).then_inc(s_kmax, 1)

                def q_max(j, u):
                    q = px[:, 0:512].rearrange("p (h d) -> p h d", d=XD)
                    dve.wait_ge(s_qmm, 8 * j + u + 1)
                    dve.tensor_reduce(qmx[:, u, :], q, AX.X, ALU.max).then_inc(s_qmax, 1)
                    dve.wait_ge(s_qmax, 8 * j + u + 1)
                    if due(8 * j + u - 1):
                        dve.wait_ge(s_qtr, 8 * j + u - 1)
                    dve.tensor_tensor(q_e[:, u % 2, :].rearrange("p (h d) -> p h d", d=XD), q,
                                      qmx[:, u, :].unsqueeze(2).to_broadcast([128, XH, XD]), ALU.subtract).then_inc(s_qsub, 1)

                def q_total(j, u):
                    dve.wait_ge(s_qexp, 8 * j + u + 1)
                    dve.tensor_reduce(qsum[:, u, :], q_e[:, u % 2, :].rearrange("p (h d) -> p h d", d=XD), AX.X,
                                      ALU.add).then_inc(s_qsum, 1)
                    dve.wait_ge(s_qsum, 8 * j + u + 1)
                    if due(8 * j - 7 + u):
                        dve.wait_ge(s_qnorm, 8 * j - 7 + u)
                    dve.reciprocal(qrec[:, u, :], qsum[:, u, :]).then_inc(s_qrec, 1)

                def k_sums(j):
                    dve.wait_ge(s_kexp, 8 * j + 8)
                    if due(j):
                        dve.wait_ge(s_mts, j)
                    dve.reciprocal(krec[:], ksum[:]).then_inc(s_krec, 1)

                def m_out(j):
                    dve.wait_ge(s_m, j + 1)
                    dve.wait_ge(s_krec, j + 1)
                    if due(j):
                        dve.wait_ge(s_fin, j)
                    dve.scalar_tensor_tensor(m_t[:].rearrange("p t b o -> p (t b) o"),
                                             pf[:].rearrange("p (g o) -> p g o", o=XD), XD ** -0.5,
                                             krec[:].rearrange("p t b -> p (t b)").unsqueeze(2).to_broadcast([128, 8, XD]),
                                             ALU.mult, ALU.mult).then_inc(s_mts, 1)

                def norm2_stats(j):
                    dve.wait_ge(s_rst, j + 1)
                    dve.scalar_tensor_tensor(y2[:], oc[:], xvec[:, 1:2], ort[:], ALU.mult, ALU.mult).then_inc(s_ln2, 1)
                    dve.wait_ge(s_ln2, 4 * j + 1)
                    dve.tensor_tensor(y2[:], y2[:], xres[:, bass.ds(j, 1), :].rearrange("p o h -> p (o h)"),
                                      ALU.add).then_inc(s_y2, 1)
                    dve.wait_ge(s_y2, j + 1)
                    dve.bn_stats(st2[:], y2[:]).then_inc(s_ln2, 1)
                    dve.wait_ge(s_ln2, 4 * j + 2)
                    dve.memset(pause[:], 0.0)
                    dve.bn_aggr(mv2[:], st2[:]).then_inc(s_ln2, 1)

                def norm2(j):
                    dve.wait_ge(s_rs2, 2 * j + 2)
                    if due(j):
                        dve.wait_ge(s_x2st, j)
                    dve.tensor_scalar(x2_st[:], y2[:], mv2[:, 0:1], rstd2[:], ALU.subtract, ALU.mult).then_inc(s_ln2, 1)

                def x2t_lo(j):
                    dve.wait_ge(s_xfh, j + 1)
                    dve.tensor_tensor(xf_l[:, bass.ds(j, 1)].rearrange("p o c t -> p (o c t)"), pf[:],
                                      xf_h[:, bass.ds(j, 1)].rearrange("p o c t -> p (o c t)"), ALU.subtract).then_inc(s_xfl, 1)

                def setup():
                    dve.wait_ge(s_const, 16 * len(CONSTS))
                    dve.tensor_copy(mask_q[:], mask_q_in).then_inc(s_setv, 1)
                    dve.tensor_copy(mask_k[:], mask_k_in).then_inc(s_setv, 1)
                    dve.wait_ge(s_wraw, 16 * len(RAW))
                    dve.tensor_reduce(bmean[:], xvec[:, 2:2 + XD], AX.X, ALU.add).then_inc(s_setv, 1)
                    dve.wait_ge(s_seta, SETA)
                    for raw, hi, lo in ((xw_in[:, 0, :], xwq_h[:], xwq_l[:]), (gw_in[:], gw_h[:], gw_l[:])):
                        dve.scalar_tensor_tensor(lo, raw, WS, hi, ALU.mult, ALU.subtract).then_inc(s_setv, 1)
                    dve.scalar_tensor_tensor(xwk_l[:], xw_in[:, 1, :], -1.0, xwk_h[:], ALU.mult, ALU.subtract).then_inc(s_setv, 1)

                def setup_values():
                    dve.wait_ge(s_setp, 1)
                    dve.tensor_reduce(pmean[:], pf[:].rearrange("p (h o) -> p h o", o=XD), AX.X, ALU.add).then_inc(s_setv, 1)
                    dve.scalar_tensor_tensor(bc[:], bmean[:], -1 / XD, xvec[:, 0:1], ALU.mult, ALU.add).then_inc(s_setv, 1)
                    dve.wait_ge(s_setv, 11)
                    dve.tensor_scalar(pmean[:], pmean[:], 1 / XD, None, ALU.mult).then_inc(s_setv, 1)
                    dve.wait_ge(s_setv, 13)
                    for b in range(2):
                        rows = slice(64 * b, 64 * b + 64)
                        dve.tensor_tensor(pbd[rows, :, b, :], pf[rows, :].rearrange("p (h o) -> p h o", o=XD),
                                          pmean[rows, :].unsqueeze(2).to_broadcast([64, XH, XD]), ALU.subtract).then_inc(s_setv, 1)

                def attention(j):
                    setup()
                    rotate(j)
                    key_blocks(j)
                    setup_values()
                    dve.wait_ge(s_setv, SETM)
                    for b in range(2):
                        a_softmax(j, b)
                    for b in range(2):
                        a_total(j, b)
                    norm1_stats(j)
                    norm1(j)

                def iteration(j, attend, keys, prev):
                    for u in range(8):
                        qj, qu = q_tile(j, u, 0)
                        tj, tu = q_tile(j, u, 1)
                        if u == 0 and prev:
                            k_sums(j - 1)
                        if u == 0 and prev and keys:
                            norm1_stats(j)
                        if u == 1 and prev and keys:
                            norm1(j)
                        if prev:
                            if u == 6:
                                norm2(j - 1)
                            if u == 7:
                                x2t_lo(j - 1)
                        if q_runs(j, u, 1, keys, prev):
                            q_total(tj, tu)
                        if keys:
                            k_max(j, u)
                        if q_runs(j, u, 0, keys, prev):
                            q_max(qj, qu)
                        if prev and u == 2:
                            m_out(j - 1)
                        if attend:
                            if u == 1:
                                rotate(j + 1)
                            if u == 2:
                                key_blocks(j + 1)
                            if u == 3:
                                a_softmax(j + 1, 0)
                            if u == 4:
                                a_total(j + 1, 0)
                                a_softmax(j + 1, 1)
                            if u == 5:
                                a_total(j + 1, 1)
                        if prev and u == 5:
                            norm2_stats(j - 1)

                dve.memset(vbd[:], 0.0).then_inc(s_setv, 1)
                dve.memset(zero[:], 0.0).then_inc(s_setv, 1)
                dve.memset(pbd[:], 0.0).then_inc(s_setv, 1)
                dve.memset(eps[:], EPS).then_inc(s_setv, 1)
                for c in range(0, HC, 2):
                    dve.wait_ge(s_wh, c // 2 + 1)
                    dve.scalar_tensor_tensor(wqkv_l[:, c:c + 2, :], w_in[:, c:c + 2, :], WS, wqkv_h[:, c:c + 2, :],
                                             ALU.mult, ALU.subtract).then_inc(s_wl, 1)
                walk(dve, attention, iteration)

            @block.gpsimd
            def _(pool):
                def a_norm(j, b):
                    pool.wait_ge(s_arec, 2 * j + b + 1)
                    pool.tensor_tensor(prob[:, b], prob[:, b], arec[:, b, :].unsqueeze(2).to_broadcast([128, 16, S]),
                                       ALU.mult).then_inc(s_anorm, 1)

                def q_norm(j, u):
                    pool.wait_ge(s_qrec, 8 * j + u + 1)
                    q = q_e[:, u % 2, :].rearrange("p (h d) -> p h d", d=XD)
                    pool.tensor_tensor(q, q, qrec[:, u, :].unsqueeze(2).to_broadcast([128, XH, XD]),
                                       ALU.mult).then_inc(s_qnorm, 1)

                def keep_x2(j):
                    pool.wait_ge(s_ln2, 4 * j + 4)
                    pool.wait_ge(s_x2t, j + 1)
                    pool.tensor_copy(xres[:, bass.ds(j, 1), :].rearrange("p o h -> p (o h)"), x2_st[:]).then_inc(s_x2st, 1)

                def split_x(j):
                    pool.wait_ge(s_ld_xt, 16 * (j + 1))
                    pool.wait_ge(s_xh, j + 1)
                    if due(j):
                        pool.wait_ge(s_qkv, j)
                    pool.tensor_tensor(xt_l[:], xt_st[:], xt_h[:], ALU.subtract).then_inc(s_xl, 1)

                def split_c(j, b):
                    pool.wait_ge(s_ch, 2 * j + b + 1)
                    if due(8 * j - 4 + 4 * b):
                        pool.wait_ge(s_kmm, 8 * j - 4 + 4 * b)
                    pool.tensor_tensor(cs[64 - 64 * b:128 - 64 * b, b, :], ctx_st[64 * b:64 * b + 64, :],
                                       cs[64 * b:64 * b + 64, b, :], ALU.subtract).then_inc(s_cl, 1)

                def split_x1(j, b):
                    pool.wait_ge(s_x1h, 2 * j + b + 1)
                    if due(8 * j - 4 + 4 * b):
                        pool.wait_ge(s_qmm, 8 * j - 4 + 4 * b)
                    pool.tensor_tensor(xs[64 - 64 * b:128 - 64 * b, b, :],
                                       xres[64 * b:64 * b + 64, bass.ds(j, 1), :].rearrange("p o h -> p (o h)"),
                                       xs[64 * b:64 * b + 64, b, :], ALU.subtract).then_inc(s_x1l, 1)

                def attention(j):
                    split_x(j)
                    a_norm(j, 0)
                    a_norm(j, 1)
                    pool.wait_ge(s_anorm, 2 * j + 2)
                    split_c(j, 0)
                    pool.wait_ge(s_cl, 2 * j + 1)
                    split_c(j, 1)
                    pool.wait_ge(s_cl, 2 * j + 2)
                    split_x1(j, 0)
                    pool.wait_ge(s_x1l, 2 * j + 1)
                    split_x1(j, 1)
                    pool.wait_ge(s_x1l, 2 * j + 2)

                def iteration(j, attend, keys, prev):
                    for u in range(8):
                        tj, tu = q_tile(j, u, 1)
                        if attend and u == 0:
                            split_x(j + 1)
                        if keys and prev:
                            if u == 1:
                                pool.wait_ge(s_cl, 2 * j + 2)
                            if u in (2, 3):
                                if due(2 * j + u - 1):
                                    pool.wait_ge(s_x1l, 2 * j + u - 1)
                        if attend and u == 7:
                            pool.wait_ge(s_cl, 2 * j + 3)
                        if q_runs(j, u, 1, keys, prev):
                            q_norm(tj, tu)
                        if keys and prev:
                            if u < 3:
                                if due(8 * j + u - 2):
                                    pool.wait_ge(s_qnorm, 8 * j + u - 2)
                            if u == 0:
                                split_c(j, 1)
                            if u in (1, 2):
                                split_x1(j, u - 1)
                        if attend:
                            if u in (4, 5):
                                a_norm(j + 1, u - 4)
                            if u == 6:
                                if due(8 * j + u - 2):
                                    pool.wait_ge(s_qnorm, 8 * j + u - 2)
                                split_c(j + 1, 0)
                        if prev and u == 7:
                            keep_x2(j - 1)

                walk(pool, attention, iteration)


        pairs_stack.close()
        w_h = sb("w_h", [128, 2, WEXP], F16)
        w_l = sb("w_l", [128, 2, WEXP], F16)
        sg = sb("sg", [128, 2, I])
        z = sb("z", [128, 2, I])
        z_h = sb("z_h", [128, 2, 2, 128], F16)
        z_l = sb("z_l", [128, 2, 2, 128], F16)
        sig = sb("sig", [128, PAIRS, E])
        total = sb("total", [128, PAIRS])
        st3 = sb("st3", [128, PAIRS, 6])
        mv3 = sb("mv3", [128, PAIRS, 2])
        ln3 = sb("ln3", [128, PAIRS, 1])
        rstd3 = sb("rstd3", [128, PAIRS, 1])
        y3 = sb("y3", [128, 4, H])

        SLOT, GUC = WEXP // 6, 4 * I * HC // 2
        gu_raw = sb("gu_raw", [128, 2, GUC])
        dn_raw = sb("dn_raw", [128, 2, WEXP - GUC])
        sh_h = sb("sh_h", [128, WEXP], F16)
        sh_l = sb("sh_l", [128, WEXP], F16)
        tri = sb("tri", [128, 128], F16)
        count = sb("count", [128, 128])
        token = sb("token", [128, PAIRS])
        ones = sb("ones", [128, 128], F16)
        sel = sb("sel", [128, PAIRS, E], F16)
        mask = sb("mask", [128, PAIRS, TOPK, E])
        top = sb("top", [128, PAIRS, 8])
        top_e = sb("top_e", [128, PAIRS, 8], U32)
        top_f = sb("top_f", [128, PAIRS, 8])
        count_h = sb("count_h", [128, 128], F16)
        pick = sb("pick", [128, PAIRS, TOPK, E])
        blocks = sb("blocks", [128, E])
        begin = sb("begin", [128, E])
        end = sb("end", [128, E])
        by_pair = sb("by_pair", [128, E])
        pairs_f = sb("pairs_f", [128, 1])
        pairs_i = sb("pairs_i", [128, 1], mybir.dt.int32)
        wk = sb("wk", [128, PAIRS, TOPK])
        posk = sb("posk", [128, PAIRS, TOPK])
        basek = sb("basek", [128, PAIRS, TOPK])
        tile_in = sb("tile_in", [128, PAIRS, TOPK])
        lane = sb("lane", [128, PAIRS, TOPK])
        slot_i = sb("slot_i", [128, PAIRS * TOPK], U32)
        at_lane = sb("at_lane", [128, PAIRS * TOPK, 128], F16)
        at_tile = sb("at_tile", [128, PAIRS * TOPK, TILES], F16)
        neg = sb("neg", [128, PAIRS, 1])
        owner = sb("owner", [128, BLOCKS, E])
        earlier = sb("earlier", [128, E, E])
        row_f = sb("row_f", [128, BLOCKS])
        row_i = sb("row_i", [128, BLOCKS], U32)
        ids = sb("ids", [128, TILES], U32)
        at_w = sb("at_w", [128, 4], U32)
        at_x = sb("at_x", [128, 4], U32)
        xg = sb("xg", [128, 4, H])
        xg_h = sb("xg_h", [128, 2, HC, 128], F16)
        xg_l = sb("xg_l", [128, 2, HC, 128], F16)
        ysb = sb("ysb", [128, 2, H])
        yg = sb("yg", [128, 8, H])

        s_tab, s_sco, s_shh, s_shl, s_pos, s_ids = (
            sem(n) for n in ("s_tab", "s_sco", "s_shh", "s_shl", "s_pos", "s_ids"))
        h_gu, h_sg, h_z, h_zt, h_zh, h_zl, h_y = (sem(n) for n in ("h_gu", "h_sg", "h_z", "h_zt", "h_zh", "h_zl", "h_y"))
        s_xt, s_gxh, s_gxl, s_guh, s_gul, s_dnh, s_dnl, s_stage, s_yo, s_add = (
            sem(n) for n in ("s_xt", "s_gxh", "s_gxl", "s_guh", "s_gul", "s_dnh", "s_dnl", "s_stage", "s_yo", "s_add"))
        s_ldgu, s_lddn, s_sty = ([sem(f"{n}{i}") for i in range(2)] for n in ("s_ldgu", "s_lddn", "s_sty"))
        s_neg = sem("s_neg")
        s_max, s_put, s_put_act = (sem(n) for n in ("s_max", "s_put", "s_put_act"))
        s_passed = sem("s_passed")
        s_ldx = [sem(f"s_ldx{i}") for i in range(4)]
        s_yg = [sem(f"s_yg{i}") for i in range(8)]

        EARLY, LATE = range(0, PAIRS // 2), range(PAIRS // 2, PAIRS)
        LATE_SLOTS = ((4, 5), (6, 7), (8,), (9,))
        SHARED = [(1024 * c, 1024 * (c + 1)) for c in range(3)]
        PIECES = [(0, 512), (512, GUC)]
        XT = [slice(0, 512), slice(512, 1024)]

        def pairs_of_blocks(eng):
            return eng.value_load(pairs_i[0:1, 0:1], min_val=0, max_val=BLOCKS // 4) + BLOCKS // 4

        with nc.Block() as block:
            @block.sync
            def _(sp):
                for name, tile in (("tri", tri), ("count", count), ("token", token)):
                    sp.dma_start(tile[:], d[name]).then_inc(s_tab, 16)
                sp.wait_ge(s_route, PAIRS_STEP)
                n = pairs_of_blocks(sp)
                with sp.Fori(0, n) as p:
                    for q in range(4):
                        sp.wait_ge(s_yo, 4 * p + q + 1)
                        sp.dma_start(y_rows[bass.ds(512 * p + 128 * q, 128)], ysb[:, q % 2]).then_inc(s_sty[q % 2], 16)
                for i in range(PAIRS):
                    sp.wait_ge(s_norm3, i + 1)
                    sp.dma_start(d["out"][i], y3[:, i % 4]).then_inc(s_out[i % 4], 16)
                for sent in s_out:
                    sp.wait_ge(sent, 16 * (PAIRS // 4))

            @block.tensor
            def _(pe):
                def shared(tiles):
                    first, behind = tiles[0], tiles[-1] + 1
                    for i in range(first, behind + 2):
                        if i < behind:
                            if i >= 2:
                                pe.wait_ge(h_z, i - 1)
                            for n, (x, w) in enumerate(((xf_h, sh_h), (xf_h, sh_l), (xf_l, sh_h))):
                                for c in range(HC):
                                    mm = pe.matmul(pgu[:, i % 2, :], x[:, i, c, :], w[:, 512 * c:512 * c + 512],
                                                   start=(n == 0 and c == 0), stop=(n == 2 and c == HC - 1))
                            mm.then_inc(h_gu, 1)
                        if first < i <= behind:
                            pe.wait_ge(h_z, i)
                            if i >= 2:
                                pe.wait_ge(h_zl, i - 1)
                            for c in range(2):
                                mm = pe.transpose(pzt[:, 128 * c:128 * c + 128], z[:, (i - 1) % 2, 128 * c:128 * c + 128], ident[:])
                            mm.then_inc(h_zt, 1)
                        if i >= first + 2:
                            pe.wait_ge(h_zl, i - 1)
                            if i >= 4:
                                pe.wait_ge(s_acc, i - 3)
                            for n, (x, w) in enumerate(((z_h, sh_h), (z_h, sh_l), (z_l, sh_h))):
                                for c in range(2):
                                    mm = pe.matmul(py[:, i % 2, :], x[:, i % 2, c, :], w[:, 2048 + 512 * c:2560 + 512 * c],
                                                   start=(n == 0 and c == 0), stop=(n == 2 and c == 1))
                            mm.then_inc(h_y, 1)

                pe.wait_ge(s_tab, 48)
                pe.wait_ge(s_route, SEL_STEP)
                pe.matmul(pa[:, 0:128], tri[:], sel[:].rearrange("p i e -> p (i e)"), start=True, stop=False)
                for k in range(1, PAIRS):
                    pe.matmul(pa[:, 16 * k:128], ones[:], sel[:, 0:PAIRS - k, :].rearrange("p i e -> p (i e)"),
                              start=False, stop=(k == PAIRS - 1))
                for k in range(PAIRS):
                    mm = pe.matmul(pa[:, 512:512 + E], ones[:], sel[:, k, :], start=(k == 0), stop=(k == PAIRS - 1))
                mm.then_inc(s_pos, 1)
                pe.wait_ge(s_shl, 3)
                shared(EARLY)

                for k in range(PAIRS * TOPK):
                    if k % (PAIRS * TOPK // 2) == 0:
                        pe.wait_ge(s_put, 2 + k // (PAIRS * TOPK // 2))
                    if k % TOPK == 0:
                        pe.wait_ge(s_put_act, k // TOPK + 1)
                    mm = pe.matmul(pa[:, 1024:1024 + TILES], at_lane[:, k, :], at_tile[:, k, :],
                                   start=(k == 0), stop=(k == PAIRS * TOPK - 1))
                mm.then_inc(s_ids, 1)

                def turn_x(t, bank):
                    for c in range(HC):
                        mm = pe.transpose(pa[:, 512 * bank + 128 * c:512 * bank + 128 * c + 128],
                                          xg[:, t, 128 * c:128 * c + 128], ident[:])
                    mm.then_inc(s_xt, 1)

                def turn_z(q):
                    for c in range(2):
                        mm = pe.transpose(pzt[:, 128 * c:128 * c + 128], z[:, (q + 1) % 2, 128 * c:128 * c + 128], ident[:])
                    mm.then_inc(s_zt, 1)

                def project(q):
                    own = (q - 2) % 4 // 2
                    for n, (x, w) in enumerate(((z_h, w_h), (z_h, w_l), (z_l, w_h))):
                        for c in range(2):
                            mm = pe.matmul(py[:, q % 2, :], x[:, q % 2, c, :], w[:, own, 2048 + 512 * c:2560 + 512 * c],
                                           start=(n == 0 and c == 0), stop=(n == 2 and c == 1))
                    mm.then_inc(s_y, 1)

                def pair(p, first, last):
                    for q in range(4):
                        if not (last and q == 3):
                            if q < 3:
                                pe.wait_ge(s_ldx[q + 1], 16 * p + 16)
                            else:
                                pe.wait_ge(s_ldx[0], 16 * p + 32)
                            if not (first and q == 0):
                                pe.wait_ge(s_gxl, 4 * p + q)
                            turn_x((q + 1) % 4, (q + 1) % 2)
                        pe.wait_ge(s_gxl, 4 * p + q + 1)
                        if q % 2 == 0:
                            pe.wait_ge(s_gul, 4 * p + q + 2)
                        if not (first and q < 2):
                            pe.wait_ge(s_z, 4 * p + q - 1)
                        for n, (x, w) in enumerate(((xg_h, w_h), (xg_h, w_l), (xg_l, w_h))):
                            for c in range(HC):
                                mm = pe.matmul(pgu[:, q % 2, :], x[:, q % 2, c, :], w[:, q // 2, 512 * c:512 * c + 512],
                                               start=(n == 0 and c == 0), stop=(n == 2 and c == HC - 1))
                        mm.then_inc(s_gu, 1)
                        if not (first and q < 1):
                            pe.wait_ge(s_z, 4 * p + q)
                            if not (first and q < 2):
                                pe.wait_ge(s_zl, 4 * p + q - 1)
                            turn_z(q)
                        if not (first and q < 2):
                            pe.wait_ge(s_zl, 4 * p + q - 1)
                            if q % 2 == 0:
                                pe.wait_ge(s_dnl, 2 * p + q // 2)
                            if not (first and q < 4):
                                pe.wait_ge(s_yo, 4 * p + q - 3)
                            project(q)

                pe.wait_ge(s_route, PAIRS_STEP)
                n = pairs_of_blocks(pe)
                pe.wait_ge(s_route, TABLES_STEP)
                pe.wait_ge(s_acc, len(EARLY))
                pe.wait_ge(s_ldx[0], 16)
                turn_x(0, 0)
                pair(0, True, False)
                with pe.Fori(1, n - 1) as p:
                    pair(p, False, False)
                pair(n - 1, False, True)
                pe.wait_ge(s_z, 4 * n)
                pe.wait_ge(s_zl, 4 * n - 1)
                turn_z(0)
                pe.wait_ge(s_dnl, 2 * n)
                pe.wait_ge(s_yo, 4 * n - 3)
                project(0)
                pe.wait_ge(s_zl, 4 * n)
                pe.wait_ge(s_yo, 4 * n - 2)
                project(1)
                pe.wait_ge(s_yo, 4 * n)
                shared(LATE)

            @block.scalar
            def _(act):
                act.wait_ge(s_route, 2)
                act.activation(score[:], score[:], ACT.Exp).then_inc(s_sco, 1)
                act.wait_ge(s_ldsh, 16)
                for lo, hi in SHARED:
                    act.activation(sh_h[:, lo:hi], sh_raw[:, lo:hi], ACT.Copy, scale=WS).then_inc(s_shh, 1)
                def shared(tiles):
                    first, behind = tiles[0], tiles[-1] + 1
                    for i in range(first, behind + 1):
                        if i < behind:
                            act.wait_ge(h_gu, i + 1)
                            if i >= 2:
                                act.wait_ge(h_z, i - 1)
                            act.activation(sg[:, i % 2, :], pgu[:, i % 2, 0:I], ACT.Silu, scale=1 / WS).then_inc(h_sg, 1)
                        if i > first:
                            act.wait_ge(h_zt, i)
                            if i >= 3:
                                act.wait_ge(h_y, i - 2)
                            act.activation(z_h[:, (i - 1) % 2].rearrange("p c t -> p (c t)"), pzt[:], ACT.Copy).then_inc(h_zh, 1)

                shared(EARLY)
                act.wait_ge(s_put, 1)
                for i in range(PAIRS):
                    part = at_tile[:, TOPK * i:TOPK * i + TOPK].rearrange("p k t -> p (k t)")
                    act.activation(part, part, ACT.Copy, scale=token[:, i:i + 1]).then_inc(s_put_act, 1)

                def split_gu(s, piece):
                    lo, hi = PIECES[piece]
                    act.activation(w_h[:, s, lo:hi], gu_raw[:, s, lo:hi], ACT.Copy, scale=WS).then_inc(s_guh, 1)

                def split_dn(s):
                    act.activation(w_h[:, s, GUC:WEXP], dn_raw[:, s], ACT.Copy, scale=WS).then_inc(s_dnh, 1)

                def split_x(q):
                    act.activation(xg_h[:, q % 2].rearrange("p c t -> p (c t)"), pa[:, XT[q % 2]], ACT.Copy).then_inc(s_gxh, 1)

                def turned(q):
                    act.activation(z_h[:, (q + 1) % 2].rearrange("p c t -> p (c t)"), pzt[:], ACT.Copy).then_inc(s_zh, 1)

                def out(q):
                    act.activation(ysb[:, (q + 1) % 2], py[:, (q + 1) % 2, :], ACT.Copy, scale=1 / (WS * ZS)).then_inc(s_yo, 1)

                def pair(p, first, last):
                    for q in range(4):
                        s = q // 2
                        if not (first and q < 3):
                            act.wait_ge(s_y, 4 * p + q - 2)
                            if not (first and q < 5):
                                if q == 0:
                                    act.wait_ge(s_sty[1], 32 * p - 32)
                                elif q == 1:
                                    act.wait_ge(s_sty[0], 32 * p - 16)
                                elif q == 2:
                                    act.wait_ge(s_sty[1], 32 * p - 16)
                                else:
                                    act.wait_ge(s_sty[0], 32 * p)
                            out(q)
                        if not (last and q == 3):
                            act.wait_ge(s_xt, 4 * p + q + 2)
                            if not (first and q == 0):
                                act.wait_ge(s_gu, 4 * p + q)
                            split_x(q + 1)
                        if q % 2 == 0:
                            act.wait_ge(s_lddn[s], 16 * p + 16)
                            if not first:
                                act.wait_ge(s_y, 4 * p + q - 2)
                            split_dn(s)
                        if not (last and q >= 2):
                            if q == 0:
                                act.wait_ge(s_ldgu[1], 16 * p + 16)
                            if q == 2:
                                act.wait_ge(s_ldgu[0], 16 * p + 32)
                            if q % 2 == 0 and not (first and q == 0):
                                act.wait_ge(s_gu, 4 * p + q)
                            split_gu(1 - s, q % 2)
                        act.wait_ge(s_gu, 4 * p + q + 1)
                        if not (first and q < 2):
                            act.wait_ge(s_z, 4 * p + q - 1)
                        act.activation(sg[:, q % 2, :], pgu[:, q % 2, 0:I], ACT.Silu, scale=1 / WS).then_inc(s_sg, 1)
                        if not (first and q < 1):
                            act.wait_ge(s_zt, 4 * p + q)
                            if not (first and q < 3):
                                act.wait_ge(s_y, 4 * p + q - 2)
                            turned(q)

                act.wait_ge(s_route, PAIRS_STEP)
                n = pairs_of_blocks(act)
                act.wait_ge(h_z, len(EARLY))
                act.wait_ge(h_y, len(EARLY))
                act.wait_ge(s_ldgu[0], 16)
                split_gu(0, 0)
                split_gu(0, 1)
                act.wait_ge(s_xt, 1)
                split_x(0)
                pair(0, True, False)
                with act.Fori(1, n - 1) as p:
                    pair(p, False, False)
                pair(n - 1, False, True)
                act.wait_ge(s_zt, 4 * n)
                act.wait_ge(s_y, 4 * n - 2)
                turned(0)
                act.wait_ge(s_sty[1], 32 * n - 32)
                out(0)
                act.wait_ge(s_y, 4 * n - 1)
                act.wait_ge(s_sty[0], 32 * n - 16)
                out(1)
                act.wait_ge(s_y, 4 * n)
                act.wait_ge(s_sty[1], 32 * n - 16)
                out(2)
                shared(LATE)
                act.preload_act_table_set("natural_log_exp_and_others")
                def roots3(t):
                    act.wait_ge(s_stat3, t // 2 * 4 + 3 + t % 2)
                    act.activation(ln3[:, t, :], mv3[:, t, 1:2], ACT.Ln, bias=eps[:]).then_inc(s_rs3, 1)
                    act.wait_ge(s_rs3, 2 * t + 1)
                    act.activation(rstd3[:, t, :], ln3[:, t, :], ACT.Exp, scale=-0.5).then_inc(s_rs3, 1)

                for t in range(4):
                    roots3(t)
                for i in range(PAIRS // 2):
                    for t in (2 * i, 2 * i + 1):
                        if i >= 2:
                            roots3(t)
                    for t in (2 * i, 2 * i + 1):
                        act.wait_ge(s_neg, t + 1)
                        if t >= 4:
                            act.wait_ge(s_out[t % 4], 16)
                        act.activation(y3[:, t % 4], xres[:, t, :], ACT.Identity, bias=neg[:, t], scale=rstd3[:, t, :]).then_inc(s_norm3, 1)

            @block.vector
            def _(dve):
                steps = 0

                def step(ins):
                    nonlocal steps
                    ins.then_inc(s_route, 1)
                    steps += 1
                    dve.wait_ge(s_route, steps)

                choices = [128, PAIRS, TOPK, E]

                def route(part):
                    if part == 0:
                        step(dve.tensor_scalar(score[:], score[:], 88.0, None, ALU.min))
                        dve.wait_ge(s_sco, 1)
                        step(dve.tensor_scalar(sig[:], score[:], 1.0, None, ALU.add))
                        step(dve.reciprocal(sig[:], sig[:]))
                        step(dve.tensor_tensor(sig[:], sig[:], gbias[:].unsqueeze(1).to_broadcast([128, PAIRS, E]), ALU.add))
                        for i in range(PAIRS):
                            dve.max(top[:, i], sig[:, i]).then_inc(s_max, 1)
                        for i in range(PAIRS):
                            dve.wait_ge(s_max, i + 1)
                            dve.max_index(top_e[:, i], top[:, i], sig[:, i]).then_inc(s_max, 1)
                        dve.wait_ge(s_max, 2 * PAIRS)
                        step(dve.tensor_copy(top_f[:], top_e[:]))
                        dve.wait_ge(s_tab, 48)
                        step(dve.tensor_tensor(mask[:], top_f[:, :, 0:TOPK].unsqueeze(3).to_broadcast(choices),
                                               count[:, 0:E].unsqueeze(1).unsqueeze(2).to_broadcast(choices), ALU.is_equal))
                        step(dve.tensor_tensor(pick[:, :, 0:2, :], mask[:, :, 0:2, :], mask[:, :, 2:4, :], ALU.add))
                        step(dve.tensor_tensor(sel[:], pick[:, :, 0, :], pick[:, :, 1, :], ALU.add))
                        assert steps == SEL_STEP
                    if part == 1:
                        step(dve.tensor_reduce(total[:], top[:, :, 0:TOPK], AX.X, ALU.add))
                        step(dve.tensor_scalar(total[:], total[:], 1e-20, None, ALU.add))
                        step(dve.reciprocal(total[:], total[:]))
                        step(dve.tensor_tensor(wk[:], top[:, :, 0:TOPK], total[:].unsqueeze(2).to_broadcast([128, PAIRS, TOPK]), ALU.mult))
                        step(dve.tensor_copy(count_h[:], count[:]))
                        dve.wait_ge(s_pos, 1)
                        step(dve.tensor_scalar(blocks[:], pa[:, 512:512 + E], 0.5, None, ALU.is_gt))
                        for k in range(1, B * S // 256):
                            step(dve.scalar_tensor_tensor(blocks[:], pa[:, 512:512 + E], 256.0 * k + 0.5, blocks[:], ALU.is_gt, ALU.add))
                        step(dve.tensor_tensor(earlier[:], before[:], blocks[:].unsqueeze(1).to_broadcast([128, E, E]), ALU.mult))
                        step(dve.tensor_reduce(begin[:], earlier[:], AX.X, ALU.add))
                        step(dve.tensor_tensor(end[:], begin[:], blocks[:], ALU.add))
                        step(dve.tensor_scalar(by_pair[:], count[:, 0:E], 2.0, end[:, E - 1:E], ALU.mult, ALU.is_lt))
                        step(dve.tensor_reduce(pairs_f[:], by_pair[:], AX.X, ALU.add))
                        step(dve.tensor_scalar(pairs_i[:], pairs_f[:], -BLOCKS / 4, None, ALU.add))
                        assert steps == PAIRS_STEP
                        step(dve.tensor_tensor(owner[:], end[:].unsqueeze(1).to_broadcast([128, BLOCKS, E]),
                                               count[:, 0:BLOCKS].unsqueeze(2).to_broadcast([128, BLOCKS, E]), ALU.is_le))
                        step(dve.tensor_reduce(row_f[:], owner[:], AX.X, ALU.add))
                        step(dve.tensor_scalar(row_f[:], row_f[:], E - 1.0, 128.0, ALU.min, ALU.mult))
                        step(dve.tensor_scalar(row_i[:], row_f[:], token[:, 0:1], None, ALU.add))
                        assert steps == ROWS_STEP
                    if part == 2:
                        step(dve.tensor_tensor(pick[:], mask[:], pa[:, 0:128].rearrange("p (i e) -> p i e", e=E).unsqueeze(2).to_broadcast(choices), ALU.mult))
                        step(dve.tensor_reduce(posk[:], pick[:], AX.X, ALU.add))
                        step(dve.tensor_tensor(pick[:], mask[:], begin[:].unsqueeze(1).unsqueeze(2).to_broadcast(choices), ALU.mult))
                        step(dve.tensor_reduce(basek[:], pick[:], AX.X, ALU.add))
                    if part == 3:
                        step(dve.scalar_tensor_tensor(slot_i[:].rearrange("p (i k) -> p i k", k=TOPK), basek[:], 256.0, posk[:], ALU.mult, ALU.add))
                        step(dve.tensor_scalar(tile_in[:], posk[:], 127.5, None, ALU.is_gt))
                        for k in range(2, PAIRS):
                            step(dve.scalar_tensor_tensor(tile_in[:], posk[:], 128.0 * k - 0.5, tile_in[:], ALU.is_gt, ALU.add))
                        step(dve.scalar_tensor_tensor(lane[:], tile_in[:], -128.0, posk[:], ALU.mult, ALU.add))
                        step(dve.scalar_tensor_tensor(tile_in[:], basek[:], 2.0, tile_in[:], ALU.mult, ALU.add))
                    if part == 4:
                        n = PAIRS * TOPK
                        dve.tensor_tensor(at_tile[:], count_h[:, 0:TILES].unsqueeze(1).to_broadcast([128, n, TILES]),
                                          tile_in[:].rearrange("p i k -> p (i k)").unsqueeze(2).to_broadcast([128, n, TILES]),
                                          ALU.is_equal).then_inc(s_put, 1)
                    if part == 5:
                        for half in range(2):
                            a, b = PAIRS // 2 * half, PAIRS // 2 * (half + 1)
                            m = PAIRS // 2 * TOPK
                            dve.tensor_tensor(at_lane[:, TOPK * a:TOPK * b], count_h[:].unsqueeze(1).to_broadcast([128, m, 128]),
                                              lane[:, a:b].rearrange("p i k -> p (i k)").unsqueeze(2).to_broadcast([128, m, 128]),
                                              ALU.is_equal).then_inc(s_put, 1)

                step(dve.memset(ones[:], 1.0))
                route(0)
                for c, (lo, hi) in enumerate(SHARED):
                    dve.wait_ge(s_shh, c + 1)
                    dve.scalar_tensor_tensor(sh_l[:, lo:hi], sh_raw[:, lo:hi], WS, sh_h[:, lo:hi],
                                             ALU.mult, ALU.subtract).then_inc(s_shl, 1)

                def shared(i, first, behind):
                    if i < behind:
                        dve.wait_ge(h_sg, i + 1)
                        if i >= 2:
                            dve.wait_ge(h_zt, i - 1)
                        dve.scalar_tensor_tensor(z[:, i % 2, :], pgu[:, i % 2, I:2 * I], ZS / WS, sg[:, i % 2, :],
                                                 ALU.mult, ALU.mult).then_inc(h_z, 1)
                    if first < i <= behind:
                        dve.wait_ge(h_zh, i)
                        dve.tensor_tensor(z_l[:, (i - 1) % 2].rearrange("p c t -> p (c t)"), pzt[:],
                                          z_h[:, (i - 1) % 2].rearrange("p c t -> p (c t)"), ALU.subtract).then_inc(h_zl, 1)
                    if i >= first + 2:
                        dve.wait_ge(h_y, i - 1)
                        dve.scalar_tensor_tensor(xres[:, i - 2, :], py[:, i % 2, :], 1 / (WS * ZS), xres[:, i - 2, :],
                                                 ALU.mult, ALU.add).then_inc(s_acc, 1)

                route(1)
                for part in range(len(EARLY) + 2):
                    shared(part, 0, len(EARLY))
                    if part < 3:
                        route(2 + part)
                    if part == 4:
                        route(5)

                dve.wait_ge(s_ids, 1)
                assert steps == TABLES_STEP - 1
                step(dve.tensor_copy(ids[:], pa[:, 1024:1024 + TILES]))
                assert steps == TABLES_STEP

                def split_gu(s, piece):
                    lo, hi = PIECES[piece]
                    dve.scalar_tensor_tensor(w_l[:, s, lo:hi], gu_raw[:, s, lo:hi], WS, w_h[:, s, lo:hi],
                                             ALU.mult, ALU.subtract).then_inc(s_gul, 1)

                def split_x(q):
                    dve.tensor_tensor(xg_l[:, q % 2].rearrange("p c t -> p (c t)"), pa[:, XT[q % 2]],
                                      xg_h[:, q % 2].rearrange("p c t -> p (c t)"), ALU.subtract).then_inc(s_gxl, 1)

                def turned(q):
                    dve.tensor_tensor(z_l[:, (q + 1) % 2].rearrange("p c t -> p (c t)"), pzt[:],
                                      z_h[:, (q + 1) % 2].rearrange("p c t -> p (c t)"), ALU.subtract).then_inc(s_zl, 1)

                def pair(p, first, last):
                    for q in range(4):
                        s = q // 2
                        if not (last and q == 3):
                            dve.wait_ge(s_gxh, 4 * p + q + 2)
                            split_x(q + 1)
                        if q % 2 == 0:
                            dve.wait_ge(s_dnh, 2 * p + s + 1)
                            dve.scalar_tensor_tensor(w_l[:, s, GUC:WEXP], dn_raw[:, s], WS, w_h[:, s, GUC:WEXP],
                                                     ALU.mult, ALU.subtract).then_inc(s_dnl, 1)
                        if not (last and q >= 2):
                            dve.wait_ge(s_guh, 4 * p + q + 3)
                            split_gu(1 - s, q % 2)
                        dve.wait_ge(s_sg, 4 * p + q + 1)
                        if not (first and q < 2):
                            dve.wait_ge(s_zt, 4 * p + q - 1)
                        dve.scalar_tensor_tensor(z[:, q % 2, :], pgu[:, q % 2, I:2 * I], ZS / WS, sg[:, q % 2, :],
                                                 ALU.mult, ALU.mult).then_inc(s_z, 1)
                        if not (first and q < 1):
                            dve.wait_ge(s_zh, 4 * p + q)
                            turned(q)

                n = pairs_of_blocks(dve)
                for piece in range(2):
                    dve.wait_ge(s_guh, piece + 1)
                    split_gu(0, piece)
                dve.wait_ge(s_gxh, 1)
                split_x(0)
                pair(0, True, False)
                with dve.Fori(1, n - 1) as p:
                    pair(p, False, False)
                pair(n - 1, False, True)
                dve.wait_ge(s_zh, 4 * n)
                turned(0)

                def centre3(t):
                    dve.wait_ge(s_rs3, 2 * t + 2)
                    dve.tensor_scalar(neg[:, t], mv3[:, t, 0:1], rstd3[:, t, :], -1.0, ALU.mult, ALU.mult).then_inc(s_neg, 1)

                for i in range(PAIRS // 2):
                    for late in LATE_SLOTS[i]:
                        shared(late, len(EARLY), PAIRS)
                    if i == 2:
                        for t in range(4):
                            centre3(t)
                    for k in range(TOPK):
                        if i == 3 and k == 2:
                            centre3(4)
                            centre3(5)
                        for t in (2 * i, 2 * i + 1):
                            m = 8 * i + 2 * k + t % 2
                            dve.wait_ge(s_yg[m % 8], 16 * i + 16)
                            if k == 0:
                                dve.wait_ge(s_acc, t + 1)
                            else:
                                dve.wait_ge(s_add, m - 1)
                            dve.scalar_tensor_tensor(xres[:, t, :], yg[:, m % 8], wk[:, t, k:k + 1], xres[:, t, :],
                                                     ALU.mult, ALU.add).then_inc(s_add, 1)
                    for t in (2 * i, 2 * i + 1):
                        dve.wait_ge(s_add, 8 * i + 7 + t % 2)
                        dve.bn_stats(st3[:, t, :], xres[:, t, :]).then_inc(s_stat3, 1)
                    for t in (2 * i, 2 * i + 1):
                        dve.wait_ge(s_stat3, 4 * i + 1 + t % 2)
                        dve.bn_aggr(mv3[:, t, :], st3[:, t, :]).then_inc(s_stat3, 1)
                centre3(6)
                centre3(7)

            @block.gpsimd
            def _(pool):
                def load_x(t, q, count):
                    pool.tensor_copy(at_x[:, q:q + 1], ids[:, bass.ds(t, 1)]).then_inc(s_stage, 1)
                    pool.wait_ge(s_stage, count + 1)
                    pool.sem_inc(s_passed, 1)
                    pool.indirect_dma_start(xg[:, q], None, x2_rows, bass.IndirectOffsetOnAxis(ap=at_x[:, q:q + 1], axis=0)).then_inc(s_ldx[q], 16)

                def load_gu(b, s, count):
                    pool.tensor_copy(at_w[:, s:s + 1], row_i[:, bass.ds(b, 1)]).then_inc(s_stage, 1)
                    pool.wait_ge(s_stage, count + 1)
                    pool.sem_inc(s_passed, 1)
                    pool.indirect_dma_start(gu_raw[:, s], None, d["wgu"], bass.IndirectOffsetOnAxis(ap=at_w[:, s:s + 1], axis=0)).then_inc(s_ldgu[s], 16)

                def load_dn(b, s, count):
                    pool.tensor_copy(at_w[:, 2 + s:3 + s], row_i[:, bass.ds(b, 1)]).then_inc(s_stage, 1)
                    pool.wait_ge(s_stage, count + 1)
                    pool.sem_inc(s_passed, 1)
                    pool.indirect_dma_start(dn_raw[:, s], None, d["wdn"], bass.IndirectOffsetOnAxis(ap=at_w[:, 2 + s:3 + s], axis=0)).then_inc(s_lddn[s], 16)

                pool.wait_ge(s_route, ROWS_STEP)
                load_gu(0, 0, 0)
                load_dn(0, 0, 1)
                load_gu(1, 1, 2)
                pool.wait_ge(s_x2w, 16 * PAIRS)
                pool.wait_ge(s_route, TABLES_STEP)
                load_x(0, 0, 3)
                load_x(1, 1, 4)
                load_x(2, 2, 5)
                load_dn(1, 1, 6)

                def pair(p, first):
                    pool.wait_ge(s_gul, 4 * p + 2)
                    pool.sem_inc(s_passed, 1)
                    load_gu(2 * p + 2, 0, 8 * p + 7)
                    if not first:
                        pool.wait_ge(s_xt, 4 * p)
                        pool.sem_inc(s_passed, 1)
                    load_x(4 * p + 3, 3, 8 * p + 8)
                    pool.wait_ge(s_dnl, 2 * p + 1)
                    pool.sem_inc(s_passed, 1)
                    load_dn(2 * p + 2, 0, 8 * p + 9)
                    pool.wait_ge(s_xt, 4 * p + 1)
                    pool.sem_inc(s_passed, 1)
                    load_x(4 * p + 4, 0, 8 * p + 10)
                    pool.wait_ge(s_gul, 4 * p + 4)
                    pool.sem_inc(s_passed, 1)
                    load_gu(2 * p + 3, 1, 8 * p + 11)
                    pool.wait_ge(s_xt, 4 * p + 2)
                    pool.sem_inc(s_passed, 1)
                    load_x(4 * p + 5, 1, 8 * p + 12)
                    pool.wait_ge(s_dnl, 2 * p + 2)
                    pool.sem_inc(s_passed, 1)
                    load_dn(2 * p + 3, 1, 8 * p + 13)
                    pool.wait_ge(s_xt, 4 * p + 3)
                    pool.sem_inc(s_passed, 1)
                    load_x(4 * p + 6, 2, 8 * p + 14)

                n = pairs_of_blocks(pool)
                pair(0, True)
                with pool.Fori(1, n - 1) as p:
                    pair(p, False)
                pool.wait_ge(s_xt, 4 * n - 4)
                pool.sem_inc(s_passed, 1)
                load_x(4 * n - 1, 3, 8 * n - 1)
                for sent in s_sty:
                    pool.wait_ge(sent, 32 * n)
                    pool.sem_inc(s_passed, 1)
                for m in range(PAIRS * TOPK):
                    c = TOPK * (m // 8 * 2 + m % 2) + m % 8 // 2
                    if m >= 8:
                        pool.wait_ge(s_add, m - 7)
                    pool.indirect_dma_start(yg[:, m % 8], None, y_rows,
                                            bass.IndirectOffsetOnAxis(ap=slot_i[:, c:c + 1], axis=0)).then_inc(s_yg[m % 8], 16)



def layouts(i):
    c = np.ascontiguousarray
    x = i["x"].reshape(PAIRS, 128, H)
    cx = i["ctx_4096"].reshape(PAIRS, 128, H)
    wq = i["L0_attn_Wq"].reshape(H, NHKV, REP, D).transpose(0, 2, 1, 3).reshape(H, H)
    wo = i["L0_attn_Wo"].reshape(NHKV, REP, D, H).transpose(1, 0, 2, 3).reshape(REP, 128, H)
    wqkv = np.concatenate([wq, i["L0_attn_Wk"], i["L0_attn_Wv"]], 1)
    xwkv = i["L0_xattn_Wkv"]
    dup = lambda w: np.concatenate([w, w], 0)
    b, g = i["L0_xattn_b_out"], i["L0_xattn_g"].reshape(XD)
    inv = (1.0 / np.float32(10000.0) ** (np.arange(0, D, 2, dtype=np.float32) / D)).astype(np.float32)
    ang = (np.arange(S, dtype=np.float32)[:, None] * inv[None, :]).astype(np.float32)
    cos, sin = np.cos(ang) / np.float32(WS), np.sin(ang) / np.float32(WS)
    rope = np.stack([np.concatenate([cos, cos], 1), np.concatenate([-sin, sin], 1)], 1)
    q = np.arange(S)
    mask_k = np.where(q[None, :] > q[:, None], np.float32(NEG), np.float32(0))[:, None, :].repeat(NHKV, 1)
    mask_q = np.tile(np.eye(S, dtype=np.float32), (1, 2))
    mask_q, mask_k = (np.concatenate([m, np.zeros_like(m)], 0) for m in (mask_q, mask_k))
    wg, wu, wd = (np.concatenate([i["L0_ffn_S" + n][None], i["L0_ffn_W" + n]], 0) for n in "gud")
    gu = np.stack([wg, wu], 1).transpose(0, 3, 1, 2).reshape(E + 1, HC, 128, 2 * I).transpose(0, 2, 1, 3)
    down = wd.transpose(0, 2, 1).reshape(E + 1, I // 128, 128, H).transpose(0, 2, 1, 3)
    gu, down = gu.reshape(E + 1, 128, -1), down.reshape(E + 1, 128, -1)
    return {
        "wgu": c(gu[1:].reshape(E * 128, -1)), "wdn": c(down[1:].reshape(E * 128, -1)), "wsh": c(np.concatenate([gu[0], down[0]], 1)),
        "tri": np.triu(np.ones((128, 128), np.float16), 1),
        "count": c(np.broadcast_to(np.arange(128, dtype=np.float32), (128, 128))),
        "token": c(np.arange(B * S, dtype=np.float32).reshape(PAIRS, 128).T),
        "before": c(np.broadcast_to(np.tril(np.ones((E, E), np.float32), -1), (128, E, E))),
        "x": c(x), "xt": c(x.reshape(PAIRS, 128, HC, 128).transpose(0, 3, 2, 1)),
        "ctx": c(cx), "ctxt": c(cx.reshape(PAIRS, 128, 4, 128).transpose(0, 3, 2, 1)),
        "wqkv": c(wqkv.reshape(HC, 128, 768).transpose(1, 0, 2)), "wo": c(wo.transpose(1, 0, 2)),
        "xw": c(np.stack([dup(i["L0_xattn_Wq"].T), dup(xwkv[:H].T)], 1)),
        "wv": c(xwkv[H:].reshape(XH, XD, XD).transpose(1, 0, 2)),
        "wout": c(i["L0_xattn_Wout"].T.reshape(XH, XD, XD).transpose(1, 0, 2)),
        "xvec": c(np.concatenate([dup(b[:, None]), dup(g[:, None]), np.broadcast_to(b, (128, XD))], 1)),
        "gw": c(i["L0_ffn_gate_w"].T.reshape(HC, 128, E).transpose(1, 0, 2)),
        "gbias": c(np.broadcast_to(i["L0_ffn_bias"], (128, E))),
        "ident": np.eye(128, dtype=np.float32), "rope": c(dup(rope)),
        "kmask": c(np.repeat(np.eye(NHKV, dtype=np.float32), D, 0)),
        "mask_q": c(mask_q), "mask_k": c(mask_k),
        "onesbd": c(np.kron(np.eye(2, dtype=np.float32), np.full((S, S), 1 / S, np.float32))),
    }


def kernel(**inputs):
    import concourse.bacc as bacc
    from concourse.bass_utils import run_bass_kernel_spmd

    arrays = {f"{n}_dram": a for n, a in layouts({n: np.asarray(a) for n, a in inputs.items()}).items()}
    nc = bacc.Bacc("TRN2", target_bir_lowering=False, num_devices=1)
    d = {n[:-5]: nc.dram_tensor(n, a.shape, mybir.dt.from_np(a.dtype), kind="ExternalInput").ap() for n, a in arrays.items()}
    d["out"] = nc.dram_tensor("out_dram", (PAIRS, 128, H), F32, kind="ExternalOutput").ap()
    decoder_layer(nc, d)
    r = run_bass_kernel_spmd(nc, [arrays], core_ids=[0])
    return r.results[0]["out_dram"].reshape(B, S, H)
```

```python
from contextlib import ExitStack

import concourse.bass as bass
import concourse.mybir as mybir
import numpy as np

F32, F16, BF16, U32 = mybir.dt.float32, mybir.dt.float16, mybir.dt.bfloat16, mybir.dt.uint32
ALU = mybir.AluOpType
ACT = mybir.ActivationFunctionType
AX = mybir.AxisListType

B, S, H = 16, 64, 512
PAIRS = B // 2
HC = H // 128
NHQ, NHKV, D = 32, 8, 16
REP = NHQ // NHKV
NKV = NHKV * D
XH, XD = 8, 64
E, TOPK, I = 16, 4, 256
EPS = 1e-5
WS = 64.0
NEG = -1e30
LANES, SUBS = 96, 2
BLOCK = LANES * SUBS
BLOCKS = -(-((B * S * TOPK + E * (BLOCK - 1)) // BLOCK) // 2) * 2
TILES = SUBS * BLOCKS
LEAST = -(-B * S * TOPK // (2 * BLOCK))
SEL_STEP, PAIRS_STEP, ROWS_STEP, TABLES_STEP = 9, 23, 27, 36
WEXP = 2 * I * HC + H * I // 128
ROUND = 1.5 * 2.0 ** 23
ZS = 16.0


def due(count):
    return not isinstance(count, int) or count > 0


def decoder_layer(nc, d):
    ctx = ExitStack()
    with ctx:
        def sb(name, shape, dt=F32):
            return ctx.enter_context(nc.sbuf_tensor(name, shape, dt))

        pairs_stack = ExitStack()

        def sb_pairs(name, shape, dt=F32):
            return pairs_stack.enter_context(nc.sbuf_tensor(name, shape, dt))

        def sem(name):
            return ctx.enter_context(nc.semaphore(name))

        ident = sb("ident", [128, 128])
        eps = sb("eps", [128, 1])
        gbias = sb("gbias", [128, E])
        xres = sb("xres", [128, PAIRS, H])
        xf_h = sb("xf_h", [128, PAIRS, HC, 128], F16)
        xf_l = sb("xf_l", [128, PAIRS, HC, 128], F16)
        score = sb("score", [128, PAIRS, E])
        sh_raw_t = sb("sh_raw", [128, WEXP])
        before = sb("before", [128, E, E])

        rope = sb_pairs("rope", [128, 2, 16])
        kmask = sb_pairs("kmask", [128, NHKV])
        mask_q = sb_pairs("mask_q", [128, 128], BF16)
        mask_k = sb_pairs("mask_k", [128, NHKV, S], BF16)
        onesbd = sb_pairs("onesbd", [128, 128])
        wqkv_h = sb_pairs("wqkv_h", [128, HC, 768], F16)
        wqkv_l = sb_pairs("wqkv_l", [128, HC, 768], F16)
        wo = sb_pairs("wo", [128, REP, H])
        xwq_h = sb_pairs("xwq_h", [128, H], F16)
        xwq_l = sb_pairs("xwq_l", [128, H], F16)
        xwk_h = sb_pairs("xwk_h", [128, H], F16)
        xwk_l = sb_pairs("xwk_l", [128, H], F16)
        wv_in = sb_pairs("wv_in", [XD, XH, XD])
        wout_in = sb_pairs("wout_in", [XD, XH, XD])
        pbd = sb_pairs("pbd", [128, XH, 2, XD])
        pmean = sb_pairs("pmean", [128, XH])
        xvec = sb_pairs("xvec", [128, 2 + XD])
        bmean = sb_pairs("bmean", [128, 1])
        bc = sb_pairs("bc", [128, 1])
        pause = sb_pairs("pause", [128, 1])
        gw_in = sb_pairs("gw_in", [128, HC, E])
        gw_h = sb_pairs("gw_h", [128, HC, E], F16)
        gw_l = sb_pairs("gw_l", [128, HC, E], F16)

        x_st = sb_pairs("x_st", [128, H])
        xt_st = sb_pairs("xt_st", [128, HC, 128])
        xt_h = sb_pairs("xt_h", [128, HC, 128], F16)
        xt_l = sb_pairs("xt_l", [128, HC, 128], F16)
        qk_cos = sb_pairs("qk_cos", [128, NHQ + NHKV, 2, 8])
        qk_sin = sb_pairs("qk_sin", [128, NHQ + NHKV, 2, 8])
        vbd = sb_pairs("vbd", [128, 2, 4, 2, D])
        q_t = sb_pairs("q_t", [128, 2, REP, S])
        kbd = sb_pairs("kbd", [128, 2, NHKV, S])
        prob = sb_pairs("prob", [128, 2, 16, S])
        amax = sb_pairs("amax", [128, 2, 16])
        asum = sb_pairs("asum", [128, 2, 16])
        arec = sb_pairs("arec", [128, 2, 16])
        prob_t = sb_pairs("prob_t", [128, 2, 4, 256])
        o_t = sb_pairs("o_t", [128, REP, 2, S])
        y1 = sb_pairs("y1", [128, H])
        st1 = sb_pairs("st1", [128, 6])
        mv1 = sb_pairs("mv1", [128, 2])
        ln1 = sb_pairs("ln1", [128, 1])
        rstd1 = sb_pairs("rstd1", [128, 1])

        ctx_st = sb_pairs("ctx_st", [128, H])
        ctxt_st = sb_pairs("ctxt_st", [128, 4, 128])
        cs = sb_pairs("cs", [128, 2, H], F16)
        xs = sb_pairs("xs", [128, 2, H], F16)
        kmx = sb_pairs("kmx", [128, 8])
        ksum = sb_pairs("ksum", [128, 4, 2])
        krec = sb_pairs("krec", [128, 4, 2])
        k_e = sb_pairs("k_e", [128, 2, H])
        k_t = sb_pairs("k_t", [128, 2, 4, H])
        kx = sb_pairs("kx", [128, H])
        m_t = sb_pairs("m_t", [128, 4, 2, XD])
        qmx = sb_pairs("qmx", [128, 8, XH])
        qsum = sb_pairs("qsum", [128, 8, XH])
        qrec = sb_pairs("qrec", [128, 8, XH])
        q_e = sb_pairs("q_e", [128, 2, H])
        x_q = sb_pairs("x_q", [128, 2, 4, H])
        mask_q_in = prob[:].rearrange("p b g m -> p (b g m)")[:, 0:128]
        mask_k_in = prob[:, 1, 0:NHKV, :]
        zero = sb_pairs("zero", [128, H])
        w_in = k_t[:].rearrange("p b t c -> p (b t c)")[:, 0:HC * 768].rearrange("p (c n) -> p c n", c=HC)
        xw_in = x_q[:].rearrange("p b t c -> p (b t c)")[:, 0:2 * H].rearrange("p (c n) -> p c n", c=2)
        oc = sb_pairs("oc", [128, H])
        osq = sb_pairs("osq", [128, H])
        ort = sb_pairs("ort", [128, H])
        y2 = sb_pairs("y2", [128, H])
        st2 = sb_pairs("st2", [128, 6])
        mv2 = sb_pairs("mv2", [128, 2])
        ln2 = sb_pairs("ln2", [128, 1])
        rstd2 = sb_pairs("rstd2", [128, 1])
        x2_st = sb_pairs("x2_st", [128, H])

        sh_raw = sh_raw_t[:]

        x2_rows = nc.dram_tensor("x2_rows", (B * S, H), F32, kind="Internal").ap()
        y_rows = nc.dram_tensor("y_rows", (TILES * LANES, H), F32, kind="Internal").ap()

        pa = ctx.enter_context(nc.psum_tensor("pa", [128, 1536], F32))
        pf = ctx.enter_context(nc.psum_tensor("pf", [128, 512], F32))
        pk = ctx.enter_context(nc.psum_tensor("pk", [128, 1024], F32))
        px = ctx.enter_context(nc.psum_tensor("px", [128, 1024], F32))

        pgu = pk[:].rearrange("p (i c) -> p i c", i=2)
        py = px[:].rearrange("p (i c) -> p i c", i=2)
        pzt = pf[:, 0:256]

        s_const, s_wraw, s_wqkv, s_wh, s_wl = (sem(n) for n in ("s_const", "s_wraw", "s_wqkv", "s_wh", "s_wl"))
        s_setv, s_setp, s_seta = sem("s_setv"), sem("s_setp"), sem("s_seta")
        s_ld_xt, s_ld_x, s_ld_c, s_ld_ct = (sem(n) for n in ("s_ld_xt", "s_ld_x", "s_ld_c", "s_ld_ct"))
        s_xh, s_xl, s_qkv, s_rope, s_vbd = (sem(n) for n in ("s_xh", "s_xl", "s_qkv", "s_rope", "s_vbd"))
        s_qkt, s_qts, s_kbd, s_sc = (sem(n) for n in ("s_qkt", "s_qts", "s_kbd", "s_sc"))
        s_amax, s_asub, s_aexp, s_asum, s_arec = (sem(n) for n in ("s_amax", "s_asub", "s_aexp", "s_asum", "s_arec"))
        s_anorm, s_pt, s_pts, s_pv, s_ot, s_wo = (sem(n) for n in ("s_anorm", "s_pt", "s_pts", "s_pv", "s_ot", "s_wo"))
        s_ln1, s_rs1 = sem("s_ln1"), sem("s_rs1")
        s_ch, s_cl, s_x1h, s_x1l = (sem(n) for n in ("s_ch", "s_cl", "s_x1h", "s_x1l"))
        s_kmm, s_kmax, s_kexp, s_ktr, s_kts = (sem(n) for n in ("s_kmm", "s_kmax", "s_kexp", "s_ktr", "s_kts"))
        s_kx, s_kxs, s_m, s_krec, s_mts = (sem(n) for n in ("s_kx", "s_kxs", "s_m", "s_krec", "s_mts"))
        s_qmm, s_qmax, s_qsub, s_qexp, s_qsum, s_qrec = (sem(n) for n in ("s_qmm", "s_qmax", "s_qsub", "s_qexp", "s_qsum", "s_qrec"))
        s_qnorm, s_qtr, s_xq = (sem(n) for n in ("s_qnorm", "s_qtr", "s_xq"))
        s_fin, s_oc, s_osq, s_var, s_vln, s_rst = (sem(n) for n in ("s_fin", "s_oc", "s_osq", "s_var", "s_vln", "s_rst"))
        s_ln2, s_rs2, s_x2st, s_x2t, s_xfh, s_xfl, s_gate, s_score = (
            sem(n) for n in ("s_ln2", "s_rs2", "s_x2st", "s_x2t", "s_xfh", "s_xfl", "s_gate", "s_score"))
        s_y2 = sem("s_y2")
        s_zero, s_ldsh, s_x2w = sem("s_zero"), sem("s_ldsh"), sem("s_x2w")
        s_out = [sem(f"s_out{i}") for i in range(4)]
        s_route, s_gu, s_sg, s_z, s_zh, s_zl, s_y, s_acc = (
            sem(n) for n in ("s_route", "s_gu", "s_sg", "s_z", "s_zh", "s_zl", "s_y", "s_acc"))
        s_stat3, s_rs3, s_norm3 = sem("s_stat3"), sem("s_rs3"), sem("s_norm3")


        SETA, SETV, SETM = 3, 15, 10

        def walk(eng, attention, iteration):
            attention(0)
            iteration(0, True, True, False)
            iteration(1, True, True, True)
            with eng.Fori(2, PAIRS - 1) as j:
                iteration(j, True, True, True)
            iteration(PAIRS - 1, False, True, True)
            iteration(PAIRS, False, False, True)

        def q_tile(j, u, lag):
            v = u - 2 - lag
            return (j, v) if v >= 0 else (j - 1, v + 8)

        def q_runs(j, u, lag, keys, prev):
            return keys if u - 2 - lag >= 0 else prev

        def k_tile(j, u):
            return (j, u - 1) if u >= 1 else (j - 1, 7)

        def k_runs(u, keys, prev):
            return keys if u >= 1 else prev

        CONSTS = [("ident", ident), ("rope", rope), ("kmask", kmask), ("mask_q", mask_q_in), ("mask_k", mask_k_in),
                  ("onesbd", onesbd)]
        RAW = [("wo", wo), ("xw", xw_in), ("wv", wv_in), ("wout", wout_in), ("xvec", xvec),
               ("gw", gw_in), ("gbias", gbias), ("before", before)]

        with nc.Block() as block:
            @block.sync
            def _(sp):
                def load_xt(j):
                    if due(j):
                        sp.wait_ge(s_xl, j)
                    sp.dma_start(xt_st[:], d["xt"][bass.ds(j, 1)].rearrange("o p c t -> (o p) c t")).then_inc(s_ld_xt, 16)

                def load_x(j):
                    if due(4 * j - 3):
                        sp.wait_ge(s_ln1, 4 * j - 3)
                    sp.dma_start(x_st[:], d["x"][bass.ds(j, 1)].rearrange("o p h -> (o p) h")).then_inc(s_ld_x, 16)

                def load_c(j):
                    if due(2 * j):
                        sp.wait_ge(s_cl, 2 * j)
                    sp.dma_start(ctx_st[:], d["ctx"][bass.ds(j, 1)].rearrange("o p h -> (o p) h")).then_inc(s_ld_c, 16)

                def load_ct(j):
                    if due(j):
                        sp.wait_ge(s_kx, j)
                    sp.dma_start(ctxt_st[:], d["ctxt"][bass.ds(j, 1)].rearrange("o p c t -> (o p) c t")).then_inc(s_ld_ct, 16)

                def iteration(j, last):
                    if last < 2:
                        load_xt(j + 2)
                    load_ct(j)
                    if last < 3:
                        load_x(j + 1)
                        load_c(j + 1)

                def store_x2(j):
                    sp.wait_ge(s_x2st, j + 1)
                    if due(16 * j):
                        sp.wait_ge(s_x2w, 16 * j)
                    sp.dma_start(x2_rows[bass.ds(128 * j, 128)], xres[:, bass.ds(j, 1), :].rearrange("p o h -> p (o h)")).then_inc(s_x2w, 16)

                sp.dma_start(w_in[:], d["wqkv"]).then_inc(s_wqkv, 16)
                load_xt(0)
                for name, tile in CONSTS:
                    sp.dma_start(tile[:], d[name]).then_inc(s_const, 16)
                for name, tile in RAW:
                    sp.dma_start(tile[:], d[name]).then_inc(s_wraw, 16)
                load_c(0)
                load_x(0)
                load_xt(1)
                iteration(0, 1)
                iteration(1, 1)
                with sp.Fori(2, PAIRS - 2) as j:
                    iteration(j, 1)
                    store_x2(j - 2)
                sp.dma_start(y_rows[2 * BLOCK * LEAST:].rearrange("(t p) h -> p t h", p=LANES),
                             zero[0:LANES].unsqueeze(1).to_broadcast([LANES, TILES - 2 * SUBS * LEAST, H])).then_inc(s_zero, 16)
                iteration(PAIRS - 2, 2)
                store_x2(PAIRS - 4)
                iteration(PAIRS - 1, 3)
                store_x2(PAIRS - 3)
                sp.dma_start(sh_raw, d["wsh"]).then_inc(s_ldsh, 16)
                store_x2(PAIRS - 2)
                store_x2(PAIRS - 1)
                sp.wait_ge(s_zero, 16)

            @block.tensor
            def _(pe):
                def qkv(j):
                    pe.wait_ge(s_xh, j + 1)
                    pe.wait_ge(s_xl, j + 1)
                    if due(j):
                        pe.wait_ge(s_ot, j)
                    if due(4 * j - 3):
                        pe.wait_ge(s_ln1, 4 * j - 3)
                    parts = [(xt_h, wqkv_h), (xt_h, wqkv_l), (xt_l, wqkv_h)]
                    for lo, n in ((0, 512), (512, 256)):
                        for i, (x, w) in enumerate(parts):
                            for c in range(HC):
                                mm = pe.matmul(pa[:, lo:lo + n], x[:, c, :], w[:, c, lo:lo + n],
                                               start=(i == 0 and c == 0), stop=(i == 2 and c == HC - 1))
                    mm.then_inc(s_qkv, 1)

                def turn_qk(j):
                    pe.wait_ge(s_rope, 4 * j + 4)
                    for r in range(REP):
                        pe.transpose(pa[:, 1024 + 128 * r:1152 + 128 * r],
                                     qk_cos[:, :, :, :].rearrange("p a b c -> p (a b c)")[:, 128 * r:128 * r + 128], ident[:])
                    pe.wait_ge(s_vbd, 4 * j + 4)
                    pe.transpose(pa[:, 768:896],
                                 qk_cos[:, :, :, :].rearrange("p a b c -> p (a b c)")[:, H:H + NKV], ident[:]).then_inc(s_qkt, 1)

                def scores(j, b):
                    if b == 0:
                        pe.wait_ge(s_qts, j + 1)
                        pe.wait_ge(s_kbd, j + 1)
                    else:
                        pe.wait_ge(s_asub, 2 * j + 1)
                    for rp in range(2):
                        out = pa[:, 512 * rp:512 * rp + 512]
                        pe.matmul(out, mask_q[:], mask_k[:].rearrange("p g m -> p (g m)"), start=True, stop=False)
                        mm = pe.matmul(out, q_t[:, b, 2 * rp:2 * rp + 2, :].rearrange("p r q -> p (r q)"),
                                       kbd[:, b].rearrange("p g m -> p (g m)"), start=False, stop=True)
                    mm.then_inc(s_sc, 1)

                PT_BANK = [1024, 0, 512, 1024]

                def turn_prob(j, t):
                    b, half = t // 2, t % 2
                    pe.wait_ge(s_anorm, 2 * j + b + 1)
                    if t == 1:
                        pe.wait_ge(s_asub, 2 * j + 2)
                    if t == 3:
                        pe.wait_ge(s_pts, 4 * j + 1)
                    for g in range(2):
                        gp = 2 * half + g
                        for rp in range(2):
                            lo = PT_BANK[t] + 256 * g + 128 * rp
                            mm = pe.transpose(pa[:, lo:lo + 128],
                                              prob[:, b, 8 * rp + 2 * gp:8 * rp + 2 * gp + 2, :].rearrange("p g m -> p (g m)"),
                                              ident[:])
                    mm.then_inc(s_pt, 1)

                def weigh_values(j):
                    for b in range(2):
                        pe.wait_ge(s_pts, 4 * j + 2 * b + 2)
                        for gp in range(4):
                            mm = pe.matmul(pa[32 * gp:32 * gp + 32, 256 * b:256 * b + 256],
                                           vbd[:, b, gp].rearrange("p g d -> p (g d)"), prob_t[:, b, gp, :],
                                           start=True, stop=True)
                    mm.then_inc(s_pv, 1)

                def out_proj(j):
                    pe.wait_ge(s_ot, j + 1)
                    for r in range(REP):
                        mm = pe.matmul(pa[:, 512:1024], o_t[:, r].rearrange("p b q -> p (b q)"), wo[:, r, :],
                                       start=(r == 0), stop=(r == REP - 1))
                    mm.then_inc(s_wo, 1)

                def setup():
                    pe.wait_ge(s_wraw, 16 * len(RAW))
                    for h in range(XH):
                        for b in range(2):
                            mm = pe.matmul(pf[64 * b:64 * b + 64, 64 * h:64 * h + 64], wv_in[:, h, :], wout_in[:, h, :],
                                           start=True, stop=True)
                    mm.then_inc(s_setp, 1)

                def attention(j):
                    pe.wait_ge(s_wl, 2)
                    qkv(j)
                    setup()
                    pe.wait_ge(s_const, 16 * len(CONSTS))
                    turn_qk(j)
                    pe.wait_ge(s_setv, SETM)
                    scores(j, 0)
                    scores(j, 1)
                    for t in range(4):
                        turn_prob(j, t)
                    weigh_values(j)
                    out_proj(j)
                    pe.wait_ge(s_setv, SETV)
                    pe.wait_ge(s_seta, SETA)

                def k_product(j, u):
                    b, dt = u // 4, u % 4
                    if dt == 0:
                        pe.wait_ge(s_cl, 2 * j + b + 1)
                    if due(8 * j + u):
                        pe.wait_ge(s_kexp, 8 * j + u)
                    pe.matmul(pk[:, 0:512], xwk_h[:, 128 * dt:128 * dt + 128], cs[:, b, :], start=True, stop=False)
                    pe.matmul(pk[:, 0:512], xwk_l[:, 128 * dt:128 * dt + 128], cs[:, b, :], start=False,
                              stop=True).then_inc(s_kmm, 1)

                def k_turn(j, u):
                    pe.wait_ge(s_kexp, 8 * j + u + 1)
                    if due(8 * j + u):
                        pe.wait_ge(s_kts, 8 * j + u)
                    for t in range(4):
                        mm = pe.transpose(pk[:, 512 + 128 * t:640 + 128 * t], k_e[:, u % 2, 128 * t:128 * t + 128], ident[:])
                    mm.then_inc(s_ktr, 1)

                def k_contract(j):
                    pe.wait_ge(s_kts, 8 * j + 8)
                    pe.wait_ge(s_ld_ct, 16 * (j + 1))
                    if due(j):
                        pe.wait_ge(s_score, j)
                    for t in range(4):
                        for b in range(2):
                            mm = pe.matmul(pf[64 * b:64 * b + 64, :], ctxt_st[:, t, 64 * b:64 * b + 64], k_t[:, b, t, :],
                                           start=(t == 0), stop=(t == 3))
                    mm.then_inc(s_kx, 1)

                def k_matrix(j):
                    pe.wait_ge(s_kxs, j + 1)
                    for h in range(XH):
                        p = 64 * (h % 2)
                        mm = pe.matmul(pf[p:p + 64, 128 * (h // 2):128 * (h // 2) + 128], kx[:, 64 * h:64 * h + 64],
                                       pbd[:, h].rearrange("p b o -> p (b o)"), start=True, stop=True)
                    mm.then_inc(s_m, 1)

                def q_product(j, u):
                    b, nt = u // 4, u % 4
                    if nt == 0:
                        pe.wait_ge(s_x1l, 2 * j + b + 1)
                    if due(8 * j + u):
                        pe.wait_ge(s_qsub, 8 * j + u)
                    pe.matmul(px[:, 0:512], xs[:, b, 128 * nt:128 * nt + 128], xwq_h[:], start=True, stop=False)
                    pe.matmul(px[:, 0:512], xs[:, b, 128 * nt:128 * nt + 128], xwq_l[:], start=False,
                              stop=True).then_inc(s_qmm, 1)

                def q_turn(j, u):
                    pe.wait_ge(s_qnorm, 8 * j + u + 1)
                    if due(8 * j + u):
                        pe.wait_ge(s_xq, 8 * j + u)
                    for t in range(4):
                        mm = pe.transpose(px[:, 512 + 128 * t:640 + 128 * t], q_e[:, u % 2, 128 * t:128 * t + 128], ident[:])
                    mm.then_inc(s_qtr, 1)

                def final(j):
                    pe.wait_ge(s_mts, j + 1)
                    pe.wait_ge(s_xq, 8 * j + 8)
                    for t in range(4):
                        for b in range(2):
                            mm = pe.matmul(pf[64 * b:64 * b + 64, :], m_t[:, t, b, :], x_q[:, b, t, :],
                                           start=(t == 0), stop=(t == 3))
                    mm.then_inc(s_fin, 1)

                def variance(j):
                    pe.wait_ge(s_osq, j + 1)
                    pe.matmul(pf[:], onesbd[:], osq[:], start=True, stop=True).then_inc(s_var, 1)

                def turn_x2(j):
                    pe.wait_ge(s_ln2, 4 * j + 4)
                    pe.wait_ge(s_vln, j + 1)
                    for c in range(HC):
                        mm = pe.transpose(pf[:, 128 * c:128 * c + 128], x2_st[:, 128 * c:128 * c + 128], ident[:])
                    mm.then_inc(s_x2t, 1)

                def gate(j):
                    pe.wait_ge(s_xfl, j + 1)
                    pe.wait_ge(s_xfh, j + 1)
                    parts = [(xf_h, gw_h), (xf_h, gw_l), (xf_l, gw_h), (xf_l, gw_l)]
                    for i, (x, w) in enumerate(parts):
                        for c in range(HC):
                            mm = pe.matmul(pf[:, 0:E], x[:, bass.ds(j, 1), c, :].rearrange("p o t -> p (o t)"), w[:, c, :],
                                           start=(i == 0 and c == 0), stop=(i == 3 and c == HC - 1))
                    mm.then_inc(s_gate, 1)

                def iteration(j, attend, keys, prev):
                    for u in range(8):
                        qj, qu = q_tile(j, u, 0)
                        tj, tu = q_tile(j, u, 2)
                        if q_runs(j, u, 2, keys, prev):
                            q_turn(tj, tu)
                        if keys:
                            k_product(j, u)
                        if k_runs(u, keys, prev):
                            k_turn(*k_tile(j, u))
                        if q_runs(j, u, 0, keys, prev):
                            q_product(qj, qu)
                        if prev and u == 5:
                            variance(j - 1)
                        if prev:
                            if u == 0:
                                k_contract(j - 1)
                            if u == 2:
                                k_matrix(j - 1)
                            if u == 4:
                                final(j - 1)
                        if attend:
                            if u == 1:
                                qkv(j + 1)
                            if u == 2:
                                turn_qk(j + 1)
                            if u == 3:
                                scores(j + 1, 0)
                            if u == 4:
                                scores(j + 1, 1)
                            if u == 5:
                                turn_prob(j + 1, 0)
                                turn_prob(j + 1, 1)
                            if u == 6:
                                turn_prob(j + 1, 2)
                                turn_prob(j + 1, 3)
                            if u == 7:
                                weigh_values(j + 1)
                        if prev:
                            if u == 6:
                                turn_x2(j - 1)
                            if u == 7:
                                gate(j - 1)
                        if attend and u == 7:
                            out_proj(j + 1)

                walk(pe, attention, iteration)

            @block.scalar
            def _(act):
                def split_x(j):
                    act.wait_ge(s_ld_xt, 16 * (j + 1))
                    if due(j):
                        act.wait_ge(s_qkv, j)
                    act.activation(xt_h[:], xt_st[:], ACT.Copy).then_inc(s_xh, 1)

                def values(j):
                    act.wait_ge(s_rope, 4 * j + 3)
                    if due(j):
                        act.wait_ge(s_pv, j)
                    for b in range(2):
                        for g in range(2):
                            act.activation(vbd[64 * g:64 * g + 64, b, :, g, :],
                                           pa[64 * b:64 * b + 64, 640:768].rearrange("p (a g d) -> p a g d", a=4, g=2)[:, :, g, :],
                                           ACT.Copy, scale=1 / WS).then_inc(s_vbd, 1)

                def q_out(j):
                    act.wait_ge(s_qkt, j + 1)
                    if due(2 * j):
                        act.wait_ge(s_sc, 2 * j)
                    act.activation(q_t[:].rearrange("p b r q -> p r b q"),
                                   pa[:, 1024:1536].rearrange("p (r b q) -> p r b q", r=REP, b=2), ACT.Copy).then_inc(s_qts, 1)

                def a_exp(j, b):
                    act.wait_ge(s_asub, 2 * j + b + 1)
                    act.activation(prob[:, b], prob[:, b], ACT.Exp, scale=D ** -0.5).then_inc(s_aexp, 1)

                PT_BANK = [1024, 0, 512, 1024]

                def prob_out(j, t):
                    b, half = t // 2, t % 2
                    act.wait_ge(s_pt, 4 * j + t + 1)
                    if t == 0:
                        if due(j):
                            act.wait_ge(s_pv, j)
                    act.activation(prob_t[:, b, 2 * half:2 * half + 2, :].rearrange("p g c -> p (g c)"),
                                   pa[:, PT_BANK[t]:PT_BANK[t] + 512], ACT.Copy).then_inc(s_pts, 1)

                def o_out(j):
                    act.wait_ge(s_pv, j + 1)
                    if due(j):
                        act.wait_ge(s_wo, j)
                    act.activation(o_t[:].rearrange("p r b q -> p b r q"),
                                   pa[:, 0:512].rearrange("p (b r q) -> p b r q", r=REP, b=2), ACT.Copy).then_inc(s_ot, 1)

                def root1(j):
                    act.wait_ge(s_ln1, 4 * j + 3)
                    act.activation(ln1[:], mv1[:, 1:2], ACT.Ln, bias=eps[:]).then_inc(s_rs1, 1)
                    act.wait_ge(s_rs1, 2 * j + 1)
                    act.activation(rstd1[:], ln1[:], ACT.Exp, scale=-0.5).then_inc(s_rs1, 1)

                def split_c(j, b):
                    act.wait_ge(s_ld_c, 16 * (j + 1))
                    if due(8 * j - 4 + 4 * b):
                        act.wait_ge(s_kmm, 8 * j - 4 + 4 * b)
                    act.activation(cs[64 * b:64 * b + 64, b, :], ctx_st[64 * b:64 * b + 64, :], ACT.Copy).then_inc(s_ch, 1)

                def split_x1(j, b):
                    act.wait_ge(s_ln1, 4 * j + 4)
                    if due(8 * j - 4 + 4 * b):
                        act.wait_ge(s_qmm, 8 * j - 4 + 4 * b)
                    act.activation(xs[64 * b:64 * b + 64, b, :],
                                   xres[64 * b:64 * b + 64, bass.ds(j, 1), :].rearrange("p o h -> p (o h)"),
                                   ACT.Copy).then_inc(s_x1h, 1)

                def k_exp(j, u):
                    b, dt = u // 4, u % 4
                    act.wait_ge(s_kmax, 8 * j + u + 1)
                    if due(8 * j + u - 1):
                        act.wait_ge(s_ktr, 8 * j + u - 1)
                    if u == 0:
                        if due(j):
                            act.wait_ge(s_krec, j)
                    act.activation(k_e[:, u % 2, :], pk[:, 0:512], ACT.Exp, bias=kmx[:, u:u + 1], scale=-1.0,
                                   accum_out=ksum[:, dt, b:b + 1]).then_inc(s_kexp, 1)

                def k_out(j, u):
                    b, dt = u // 4, u % 4
                    act.wait_ge(s_ktr, 8 * j + u + 1)
                    if u == 0:
                        if due(j):
                            act.wait_ge(s_kx, j)
                    act.activation(k_t[:, b, :, 128 * dt:128 * dt + 128],
                                   pk[:, 512:1024].rearrange("p (t c) -> p t c", t=4), ACT.Copy).then_inc(s_kts, 1)

                def kx_out(j):
                    act.wait_ge(s_kx, j + 1)
                    if due(j):
                        act.wait_ge(s_m, j)
                    act.activation(kx[:], pf[:], ACT.Copy).then_inc(s_kxs, 1)

                def q_exp(j, u):
                    act.wait_ge(s_qsub, 8 * j + u + 1)
                    act.activation(q_e[:, u % 2, :], q_e[:, u % 2, :], ACT.Exp, scale=1 / WS).then_inc(s_qexp, 1)

                def q_tout(j, u):
                    b, nt = u // 4, u % 4
                    act.wait_ge(s_qtr, 8 * j + u + 1)
                    if u == 0:
                        if due(j):
                            act.wait_ge(s_fin, j)
                    act.activation(x_q[:, b, :, 128 * nt:128 * nt + 128],
                                   px[:, 512:1024].rearrange("p (t c) -> p t c", t=4), ACT.Copy).then_inc(s_xq, 1)

                def centre(j):
                    act.wait_ge(s_fin, j + 1)
                    if due(4 * j - 3):
                        act.wait_ge(s_ln2, 4 * j - 3)
                    act.activation(oc[:], pf[:], ACT.Identity, bias=bc[:]).then_inc(s_oc, 1)
                    act.wait_ge(s_oc, j + 1)
                    act.activation(osq[:], oc[:], ACT.Square).then_inc(s_osq, 1)

                def root_o(j):
                    act.wait_ge(s_var, j + 1)
                    act.activation(ort[:], pf[:], ACT.Ln, bias=eps[:]).then_inc(s_vln, 1)
                    act.wait_ge(s_vln, j + 1)
                    act.activation(ort[:], ort[:], ACT.Exp, scale=-0.5).then_inc(s_rst, 1)

                def root2(j):
                    act.wait_ge(s_ln2, 4 * j + 3)
                    act.activation(ln2[:], mv2[:, 1:2], ACT.Ln, bias=eps[:]).then_inc(s_rs2, 1)
                    act.wait_ge(s_rs2, 2 * j + 1)
                    act.activation(rstd2[:], ln2[:], ACT.Exp, scale=-0.5).then_inc(s_rs2, 1)

                def x2t_hi(j):
                    act.wait_ge(s_x2t, j + 1)
                    act.activation(xf_h[:, bass.ds(j, 1)].rearrange("p o c t -> p (o c t)"), pf[:], ACT.Copy).then_inc(s_xfh, 1)

                def score_out(j):
                    act.wait_ge(s_gate, j + 1)
                    act.activation(score[:, bass.ds(j, 1), :].rearrange("p o e -> p (o e)"), pf[:, 0:E], ACT.Copy,
                                   scale=-1 / WS).then_inc(s_score, 1)

                def setup():
                    act.wait_ge(s_wraw, 16 * len(RAW))
                    act.activation(xwq_h[:], xw_in[:, 0, :], ACT.Copy, scale=WS).then_inc(s_seta, 1)
                    act.activation(xwk_h[:], xw_in[:, 1, :], ACT.Copy, scale=-1.0).then_inc(s_seta, 1)
                    act.activation(gw_h[:], gw_in[:], ACT.Copy, scale=WS).then_inc(s_seta, 1)

                def attention(j):
                    split_x(j)
                    setup()
                    act.wait_ge(s_setv, SETM)
                    values(j)
                    q_out(j)
                    a_exp(j, 0)
                    a_exp(j, 1)
                    for t in range(4):
                        prob_out(j, t)
                    o_out(j)
                    split_c(j, 0)
                    split_c(j, 1)
                    root1(j)
                    split_x1(j, 0)
                    split_x1(j, 1)
                    act.wait_ge(s_setv, SETV)

                def iteration(j, attend, keys, prev):
                    for u in range(8):
                        qj, qu = q_tile(j, u, 0)
                        tj, tu = q_tile(j, u, 2)
                        if attend and u == 0:
                            split_x(j + 1)
                        if attend and u == 7:
                            o_out(j + 1)
                        if q_runs(j, u, 2, keys, prev):
                            q_tout(tj, tu)
                        if k_runs(u, keys, prev):
                            k_out(*k_tile(j, u))
                        if prev:
                            if u == 1:
                                kx_out(j - 1)
                            if u == 5:
                                root_o(j - 1)
                        if keys:
                            k_exp(j, u)
                        if q_runs(j, u, 0, keys, prev):
                            q_exp(qj, qu)
                        if keys and prev:
                            if u == 0:
                                split_c(j, 1)
                                root1(j)
                            if u in (1, 2):
                                split_x1(j, u - 1)
                        if prev:
                            if u == 4:
                                centre(j - 1)
                            if u == 5:
                                root2(j - 1)
                            if u == 6:
                                x2t_hi(j - 1)
                            if u == 7:
                                score_out(j - 1)
                        if attend:
                            if u == 1:
                                values(j + 1)
                            if u == 2:
                                q_out(j + 1)
                            if u in (3, 4):
                                a_exp(j + 1, u - 3)
                            if u == 5:
                                prob_out(j + 1, 0)
                                prob_out(j + 1, 1)
                            if u == 6:
                                split_c(j + 1, 0)
                                prob_out(j + 1, 2)
                                prob_out(j + 1, 3)

                act.preload_act_table_set("natural_log_exp_and_others")
                act.wait_ge(s_wqkv, 16)
                for c in range(0, HC, 2):
                    act.activation(wqkv_h[:, c:c + 2, :], w_in[:, c:c + 2, :], ACT.Copy, scale=WS).then_inc(s_wh, 1)
                walk(act, attention, iteration)


            @block.vector
            def _(dve):
                def rotate(j):
                    dve.wait_ge(s_qkv, j + 1)
                    if due(j):
                        dve.wait_ge(s_qkt, j)
                    qk = pa[:, 0:H + NKV].rearrange("p (a b c) -> p a b c", b=2, c=8)
                    n = NHQ + NHKV
                    dve.tensor_tensor(qk_cos[:].rearrange("p a b c -> p a (b c)"), qk.rearrange("p a b c -> p a (b c)"),
                                      rope[:, 0, :].unsqueeze(1).to_broadcast([128, n, 16]), ALU.mult).then_inc(s_rope, 1)
                    for half in range(2):
                        dve.tensor_tensor(qk_sin[:, :, half, :], qk[:, :, 1 - half, :],
                                          rope[:, 1, 8 * half:8 * half + 8].unsqueeze(1).to_broadcast([128, n, 8]),
                                          ALU.mult).then_inc(s_rope, 1)
                    dve.wait_ge(s_rope, 4 * j + 3)
                    dve.tensor_tensor(qk_cos[:], qk_cos[:], qk_sin[:], ALU.add).then_inc(s_rope, 1)

                def key_blocks(j):
                    dve.wait_ge(s_qkt, j + 1)
                    if due(2 * j):
                        dve.wait_ge(s_sc, 2 * j)
                    dve.tensor_tensor(kbd[:],
                                      pa[:, 768:896].rearrange("p (b m) -> p b m", b=2).unsqueeze(2).to_broadcast([128, 2, NHKV, S]),
                                      kmask[:].unsqueeze(1).unsqueeze(3).to_broadcast([128, 2, NHKV, S]), ALU.mult).then_inc(s_kbd, 1)

                def a_softmax(j, b):
                    sc = pa[:, 0:1024].rearrange("p (g m) -> p g m", m=S)
                    dve.wait_ge(s_sc, 2 * j + b + 1)
                    dve.tensor_reduce(amax[:, b, :], sc, AX.X, ALU.max).then_inc(s_amax, 1)
                    dve.wait_ge(s_amax, 2 * j + b + 1)
                    if due(4 * j - 2 + 2 * b):
                        dve.wait_ge(s_pt, 4 * j - 2 + 2 * b)
                    dve.tensor_tensor(prob[:, b], sc, amax[:, b, :].unsqueeze(2).to_broadcast([128, 16, S]),
                                      ALU.subtract).then_inc(s_asub, 1)

                def a_total(j, b):
                    dve.wait_ge(s_aexp, 2 * j + b + 1)
                    dve.tensor_reduce(asum[:, b, :], prob[:, b], AX.X, ALU.add).then_inc(s_asum, 1)
                    dve.wait_ge(s_asum, 2 * j + b + 1)
                    if due(2 * j - 1 + b):
                        dve.wait_ge(s_anorm, 2 * j - 1 + b)
                    dve.reciprocal(arec[:, b, :], asum[:, b, :]).then_inc(s_arec, 1)

                def norm1_stats(j):
                    dve.wait_ge(s_wo, j + 1)
                    dve.wait_ge(s_ld_x, 16 * (j + 1))
                    dve.tensor_tensor(y1[:], pa[:, 512:1024], x_st[:], ALU.add).then_inc(s_ln1, 1)
                    dve.wait_ge(s_ln1, 4 * j + 1)
                    dve.bn_stats(st1[:], y1[:]).then_inc(s_ln1, 1)
                    dve.wait_ge(s_ln1, 4 * j + 2)
                    dve.memset(pause[:], 0.0)
                    dve.bn_aggr(mv1[:], st1[:]).then_inc(s_ln1, 1)

                def norm1(j):
                    dve.wait_ge(s_rs1, 2 * j + 2)
                    dve.tensor_scalar(xres[:, bass.ds(j, 1), :].rearrange("p o h -> p (o h)"), y1[:], mv1[:, 0:1], rstd1[:],
                                      ALU.subtract, ALU.mult).then_inc(s_ln1, 1)

                def k_max(j, u):
                    dve.wait_ge(s_kmm, 8 * j + u + 1)
                    if due(8 * j - 7 + u):
                        dve.wait_ge(s_kexp, 8 * j - 7 + u)
                    dve.tensor_reduce(kmx[:, u:u + 1], pk[:, 0:512], AX.X, ALU.min).then_inc(s_kmax, 1)

                def q_max(j, u):
                    q = px[:, 0:512].rearrange("p (h d) -> p h d", d=XD)
                    dve.wait_ge(s_qmm, 8 * j + u + 1)
                    dve.tensor_reduce(qmx[:, u, :], q, AX.X, ALU.max).then_inc(s_qmax, 1)
                    dve.wait_ge(s_qmax, 8 * j + u + 1)
                    if due(8 * j + u - 1):
                        dve.wait_ge(s_qtr, 8 * j + u - 1)
                    dve.tensor_tensor(q_e[:, u % 2, :].rearrange("p (h d) -> p h d", d=XD), q,
                                      qmx[:, u, :].unsqueeze(2).to_broadcast([128, XH, XD]), ALU.subtract).then_inc(s_qsub, 1)

                def q_total(j, u):
                    dve.wait_ge(s_qexp, 8 * j + u + 1)
                    dve.tensor_reduce(qsum[:, u, :], q_e[:, u % 2, :].rearrange("p (h d) -> p h d", d=XD), AX.X,
                                      ALU.add).then_inc(s_qsum, 1)
                    dve.wait_ge(s_qsum, 8 * j + u + 1)
                    if due(8 * j - 7 + u):
                        dve.wait_ge(s_qnorm, 8 * j - 7 + u)
                    dve.reciprocal(qrec[:, u, :], qsum[:, u, :]).then_inc(s_qrec, 1)

                def k_sums(j):
                    dve.wait_ge(s_kexp, 8 * j + 8)
                    if due(j):
                        dve.wait_ge(s_mts, j)
                    dve.reciprocal(krec[:], ksum[:]).then_inc(s_krec, 1)

                def m_out(j):
                    dve.wait_ge(s_m, j + 1)
                    dve.wait_ge(s_krec, j + 1)
                    if due(j):
                        dve.wait_ge(s_fin, j)
                    dve.scalar_tensor_tensor(m_t[:].rearrange("p t b o -> p (t b) o"),
                                             pf[:].rearrange("p (g o) -> p g o", o=XD), XD ** -0.5,
                                             krec[:].rearrange("p t b -> p (t b)").unsqueeze(2).to_broadcast([128, 8, XD]),
                                             ALU.mult, ALU.mult).then_inc(s_mts, 1)

                def norm2_stats(j):
                    dve.wait_ge(s_rst, j + 1)
                    dve.scalar_tensor_tensor(y2[:], oc[:], xvec[:, 1:2], ort[:], ALU.mult, ALU.mult).then_inc(s_ln2, 1)
                    dve.wait_ge(s_ln2, 4 * j + 1)
                    dve.tensor_tensor(y2[:], y2[:], xres[:, bass.ds(j, 1), :].rearrange("p o h -> p (o h)"),
                                      ALU.add).then_inc(s_y2, 1)
                    dve.wait_ge(s_y2, j + 1)
                    dve.bn_stats(st2[:], y2[:]).then_inc(s_ln2, 1)
                    dve.wait_ge(s_ln2, 4 * j + 2)
                    dve.memset(pause[:], 0.0)
                    dve.bn_aggr(mv2[:], st2[:]).then_inc(s_ln2, 1)

                def norm2(j):
                    dve.wait_ge(s_rs2, 2 * j + 2)
                    if due(j):
                        dve.wait_ge(s_x2st, j)
                    dve.tensor_scalar(x2_st[:], y2[:], mv2[:, 0:1], rstd2[:], ALU.subtract, ALU.mult).then_inc(s_ln2, 1)

                def x2t_lo(j):
                    dve.wait_ge(s_xfh, j + 1)
                    dve.tensor_tensor(xf_l[:, bass.ds(j, 1)].rearrange("p o c t -> p (o c t)"), pf[:],
                                      xf_h[:, bass.ds(j, 1)].rearrange("p o c t -> p (o c t)"), ALU.subtract).then_inc(s_xfl, 1)

                def setup():
                    dve.wait_ge(s_const, 16 * len(CONSTS))
                    dve.tensor_copy(mask_q[:], mask_q_in).then_inc(s_setv, 1)
                    dve.tensor_copy(mask_k[:], mask_k_in).then_inc(s_setv, 1)
                    dve.wait_ge(s_wraw, 16 * len(RAW))
                    dve.tensor_reduce(bmean[:], xvec[:, 2:2 + XD], AX.X, ALU.add).then_inc(s_setv, 1)
                    dve.wait_ge(s_seta, SETA)
                    for raw, hi, lo in ((xw_in[:, 0, :], xwq_h[:], xwq_l[:]), (gw_in[:], gw_h[:], gw_l[:])):
                        dve.scalar_tensor_tensor(lo, raw, WS, hi, ALU.mult, ALU.subtract).then_inc(s_setv, 1)
                    dve.scalar_tensor_tensor(xwk_l[:], xw_in[:, 1, :], -1.0, xwk_h[:], ALU.mult, ALU.subtract).then_inc(s_setv, 1)

                def setup_values():
                    dve.wait_ge(s_setp, 1)
                    dve.tensor_reduce(pmean[:], pf[:].rearrange("p (h o) -> p h o", o=XD), AX.X, ALU.add).then_inc(s_setv, 1)
                    dve.scalar_tensor_tensor(bc[:], bmean[:], -1 / XD, xvec[:, 0:1], ALU.mult, ALU.add).then_inc(s_setv, 1)
                    dve.wait_ge(s_setv, 11)
                    dve.tensor_scalar(pmean[:], pmean[:], 1 / XD, None, ALU.mult).then_inc(s_setv, 1)
                    dve.wait_ge(s_setv, 13)
                    for b in range(2):
                        rows = slice(64 * b, 64 * b + 64)
                        dve.tensor_tensor(pbd[rows, :, b, :], pf[rows, :].rearrange("p (h o) -> p h o", o=XD),
                                          pmean[rows, :].unsqueeze(2).to_broadcast([64, XH, XD]), ALU.subtract).then_inc(s_setv, 1)

                def attention(j):
                    setup()
                    rotate(j)
                    key_blocks(j)
                    setup_values()
                    dve.wait_ge(s_setv, SETM)
                    for b in range(2):
                        a_softmax(j, b)
                    for b in range(2):
                        a_total(j, b)
                    norm1_stats(j)
                    norm1(j)

                def iteration(j, attend, keys, prev):
                    for u in range(8):
                        qj, qu = q_tile(j, u, 0)
                        tj, tu = q_tile(j, u, 1)
                        if u == 0 and prev:
                            k_sums(j - 1)
                        if u == 0 and prev and keys:
                            norm1_stats(j)
                        if u == 1 and prev and keys:
                            norm1(j)
                        if prev:
                            if u == 6:
                                norm2(j - 1)
                            if u == 7:
                                x2t_lo(j - 1)
                        if q_runs(j, u, 1, keys, prev):
                            q_total(tj, tu)
                        if keys:
                            k_max(j, u)
                        if q_runs(j, u, 0, keys, prev):
                            q_max(qj, qu)
                        if prev and u == 2:
                            m_out(j - 1)
                        if attend:
                            if u == 1:
                                rotate(j + 1)
                            if u == 2:
                                key_blocks(j + 1)
                            if u == 3:
                                a_softmax(j + 1, 0)
                            if u == 4:
                                a_total(j + 1, 0)
                                a_softmax(j + 1, 1)
                            if u == 5:
                                a_total(j + 1, 1)
                        if prev and u == 5:
                            norm2_stats(j - 1)

                dve.memset(vbd[:], 0.0).then_inc(s_setv, 1)
                dve.memset(zero[:], 0.0).then_inc(s_setv, 1)
                dve.memset(pbd[:], 0.0).then_inc(s_setv, 1)
                dve.memset(eps[:], EPS).then_inc(s_setv, 1)
                for c in range(0, HC, 2):
                    dve.wait_ge(s_wh, c // 2 + 1)
                    dve.scalar_tensor_tensor(wqkv_l[:, c:c + 2, :], w_in[:, c:c + 2, :], WS, wqkv_h[:, c:c + 2, :],
                                             ALU.mult, ALU.subtract).then_inc(s_wl, 1)
                walk(dve, attention, iteration)

            @block.gpsimd
            def _(pool):
                def a_norm(j, b):
                    pool.wait_ge(s_arec, 2 * j + b + 1)
                    pool.tensor_tensor(prob[:, b], prob[:, b], arec[:, b, :].unsqueeze(2).to_broadcast([128, 16, S]),
                                       ALU.mult).then_inc(s_anorm, 1)

                def q_norm(j, u):
                    pool.wait_ge(s_qrec, 8 * j + u + 1)
                    q = q_e[:, u % 2, :].rearrange("p (h d) -> p h d", d=XD)
                    pool.tensor_tensor(q, q, qrec[:, u, :].unsqueeze(2).to_broadcast([128, XH, XD]),
                                       ALU.mult).then_inc(s_qnorm, 1)

                def keep_x2(j):
                    pool.wait_ge(s_ln2, 4 * j + 4)
                    pool.wait_ge(s_x2t, j + 1)
                    pool.tensor_copy(xres[:, bass.ds(j, 1), :].rearrange("p o h -> p (o h)"), x2_st[:]).then_inc(s_x2st, 1)

                def split_x(j):
                    pool.wait_ge(s_ld_xt, 16 * (j + 1))
                    pool.wait_ge(s_xh, j + 1)
                    if due(j):
                        pool.wait_ge(s_qkv, j)
                    pool.tensor_tensor(xt_l[:], xt_st[:], xt_h[:], ALU.subtract).then_inc(s_xl, 1)

                def split_c(j, b):
                    pool.wait_ge(s_ch, 2 * j + b + 1)
                    if due(8 * j - 4 + 4 * b):
                        pool.wait_ge(s_kmm, 8 * j - 4 + 4 * b)
                    pool.tensor_tensor(cs[64 - 64 * b:128 - 64 * b, b, :], ctx_st[64 * b:64 * b + 64, :],
                                       cs[64 * b:64 * b + 64, b, :], ALU.subtract).then_inc(s_cl, 1)

                def split_x1(j, b):
                    pool.wait_ge(s_x1h, 2 * j + b + 1)
                    if due(8 * j - 4 + 4 * b):
                        pool.wait_ge(s_qmm, 8 * j - 4 + 4 * b)
                    pool.tensor_tensor(xs[64 - 64 * b:128 - 64 * b, b, :],
                                       xres[64 * b:64 * b + 64, bass.ds(j, 1), :].rearrange("p o h -> p (o h)"),
                                       xs[64 * b:64 * b + 64, b, :], ALU.subtract).then_inc(s_x1l, 1)

                def attention(j):
                    split_x(j)
                    a_norm(j, 0)
                    a_norm(j, 1)
                    pool.wait_ge(s_anorm, 2 * j + 2)
                    split_c(j, 0)
                    pool.wait_ge(s_cl, 2 * j + 1)
                    split_c(j, 1)
                    pool.wait_ge(s_cl, 2 * j + 2)
                    split_x1(j, 0)
                    pool.wait_ge(s_x1l, 2 * j + 1)
                    split_x1(j, 1)
                    pool.wait_ge(s_x1l, 2 * j + 2)

                def iteration(j, attend, keys, prev):
                    for u in range(8):
                        tj, tu = q_tile(j, u, 1)
                        if attend and u == 0:
                            split_x(j + 1)
                        if keys and prev:
                            if u == 1:
                                pool.wait_ge(s_cl, 2 * j + 2)
                            if u in (2, 3):
                                if due(2 * j + u - 1):
                                    pool.wait_ge(s_x1l, 2 * j + u - 1)
                        if attend and u == 7:
                            pool.wait_ge(s_cl, 2 * j + 3)
                        if q_runs(j, u, 1, keys, prev):
                            q_norm(tj, tu)
                        if keys and prev:
                            if u < 3:
                                if due(8 * j + u - 2):
                                    pool.wait_ge(s_qnorm, 8 * j + u - 2)
                            if u == 0:
                                split_c(j, 1)
                            if u in (1, 2):
                                split_x1(j, u - 1)
                        if attend:
                            if u in (4, 5):
                                a_norm(j + 1, u - 4)
                            if u == 6:
                                if due(8 * j + u - 2):
                                    pool.wait_ge(s_qnorm, 8 * j + u - 2)
                                split_c(j + 1, 0)
                        if prev and u == 7:
                            keep_x2(j - 1)

                walk(pool, attention, iteration)


        pairs_stack.close()
        w_h = sb("w_h", [128, 2, WEXP], F16)
        w_l = sb("w_l", [128, 2, WEXP], F16)
        sg = sb("sg", [128, 2, I])
        z = sb("z", [128, 2, I])
        z_h = sb("z_h", [128, 2, 2, 128], F16)
        z_l = sb("z_l", [128, 2, 2, 128], F16)
        sig = sb("sig", [128, PAIRS, E])
        total = sb("total", [128, PAIRS])
        st3 = sb("st3", [128, PAIRS, 6])
        mv3 = sb("mv3", [128, PAIRS, 2])
        ln3 = sb("ln3", [128, PAIRS, 1])
        rstd3 = sb("rstd3", [128, PAIRS, 1])
        y3 = sb("y3", [128, 4, H])

        GUC = 2 * I * HC
        gu_raw = sb("gu_raw", [128, 2, GUC])
        dn_raw = sb("dn_raw", [128, 2, WEXP - GUC])
        sh_h = sb("sh_h", [128, WEXP], F16)
        sh_l = sb("sh_l", [128, WEXP], F16)
        tri = sb("tri", [128, 128], F16)
        count = sb("count", [128, 128])
        token = sb("token", [128, PAIRS])
        ones = sb("ones", [128, 128], F16)
        sel = sb("sel", [128, PAIRS, E], F16)
        mask = sb("mask", [128, PAIRS, TOPK, E])
        top = sb("top", [128, PAIRS, 8])
        top_e = sb("top_e", [128, PAIRS, 8], U32)
        top_f = sb("top_f", [128, PAIRS, 8])
        count_h = sb("count_h", [128, 128], F16)
        pick = sb("pick", [128, PAIRS, TOPK, E])
        blocks = sb("blocks", [128, E])
        begin = sb("begin", [128, E])
        end = sb("end", [128, E])
        by_pair = sb("by_pair", [128, BLOCKS // 2])
        pairs_f = sb("pairs_f", [128, 1])
        pairs_i = sb("pairs_i", [128, 1], mybir.dt.int32)
        wk = sb("wk", [128, PAIRS, TOPK])
        place = sb("place", [128, PAIRS, E])
        slot = sb("slot", [128, PAIRS, TOPK])
        tile_in = sb("tile_in", [128, PAIRS, TOPK])
        lane = sb("lane", [128, PAIRS, TOPK])
        slot_i = sb("slot_i", [128, PAIRS * TOPK], U32)
        at_lane = sb("at_lane", [128, PAIRS * TOPK, LANES], F16)
        at_tile = sb("at_tile", [128, PAIRS * TOPK, TILES], F16)
        neg = sb("neg", [128, PAIRS, 1])
        owner = sb("owner", [128, BLOCKS, E])
        earlier = sb("earlier", [128, E, E])
        row_f = sb("row_f", [128, BLOCKS])
        row_i = sb("row_i", [128, BLOCKS], U32)
        ids = sb("ids", [128, TILES], U32)
        at_w = sb("at_w", [128, 4], U32)
        at_x = sb("at_x", [128, 2 * SUBS], U32)
        xg = sb("xg", [128, 2 * SUBS, H])
        xg_h = sb("xg_h", [128, 2, HC, BLOCK], F16)
        xg_l = sb("xg_l", [128, 2, HC, BLOCK], F16)
        ysb = sb("ysb", [128, 2 * SUBS, H])
        bg = sb("bg", [128, 2, BLOCK])
        bz = sb("bz", [128, 2, BLOCK])
        bz_h = sb("bz_h", [128, 2, 2, BLOCK], F16)
        bz_l = sb("bz_l", [128, 2, 2, BLOCK], F16)
        yg = sb("yg", [128, 8, H])

        s_tab, s_sco, s_shh, s_shl, s_pos, s_ids = (
            sem(n) for n in ("s_tab", "s_sco", "s_shh", "s_shl", "s_pos", "s_ids"))
        h_gu, h_sg, h_z, h_zt, h_zh, h_zl, h_y = (sem(n) for n in ("h_gu", "h_sg", "h_z", "h_zt", "h_zh", "h_zl", "h_y"))
        s_xt, s_gxh, s_gxl, s_guh, s_gul, s_dnh, s_dnl, s_stage, s_yo, s_add = (
            sem(n) for n in ("s_xt", "s_gxh", "s_gxl", "s_guh", "s_gul", "s_dnh", "s_dnl", "s_stage", "s_yo", "s_add"))
        s_ldgu, s_lddn = ([sem(f"{n}{i}") for i in range(2)] for n in ("s_ldgu", "s_lddn"))
        s_ldx, s_sty = ([sem(f"{n}{i}") for i in range(2 * SUBS)] for n in ("s_ldx", "s_sty"))
        s_neg = sem("s_neg")
        s_max, s_put, s_put_act = (sem(n) for n in ("s_max", "s_put", "s_put_act"))
        s_passed = sem("s_passed")
        s_yg = [sem(f"s_yg{i}") for i in range(8)]

        EARLY, LATE = range(0, PAIRS // 2), range(PAIRS // 2, PAIRS)
        LATE_SLOTS = ((4, 5, 6), (7,), (8,), (9,))
        SHARED = [(1024 * c, 1024 * (c + 1)) for c in range(3)]
        PIECES = [(0, GUC // 2), (GUC // 2, GUC)]
        XT = [pa[:, 0:512], pa[:, 512:1024]]
        GU = [pk[:, 0:512], pk[:, 512:1024], px[:, 0:512], px[:, 512:1024]]
        gate_t = pk[:].rearrange("p (i c) -> p i c", i=2)[:, :, 0:BLOCK]
        up_t = px[:].rearrange("p (i c) -> p i c", i=2)[:, :, 0:BLOCK]
        YB = [pf[:], pa[:, 1024:1536]]

        def pairs_of_blocks(eng):
            return eng.value_load(pairs_i[0:1, 0:1], min_val=0, max_val=BLOCKS // 2 - LEAST) + LEAST

        with nc.Block() as block:
            @block.sync
            def _(sp):
                for name, tile in (("tri", tri), ("count", count), ("token", token)):
                    sp.dma_start(tile[:], d[name]).then_inc(s_tab, 16)
                sp.wait_ge(s_route, PAIRS_STEP)
                n = pairs_of_blocks(sp)
                with sp.Fori(0, n) as p:
                    for q in range(2 * SUBS):
                        sp.wait_ge(s_yo, 2 * SUBS * p + q + 1)
                        sp.dma_start(y_rows[bass.ds(2 * BLOCK * p + LANES * q, LANES)], ysb[0:LANES, q]).then_inc(s_sty[q], 16)
                for i in range(PAIRS):
                    sp.wait_ge(s_norm3, i + 1)
                    sp.dma_start(d["out"][i], y3[:, i % 4]).then_inc(s_out[i % 4], 16)
                for sent in s_out:
                    sp.wait_ge(sent, 16 * (PAIRS // 4))

            @block.tensor
            def _(pe):
                def shared(tiles):
                    first, behind = tiles[0], tiles[-1] + 1
                    for i in range(first, behind + 2):
                        if i < behind:
                            if i >= 2:
                                pe.wait_ge(h_z, i - 1)
                            for n, (x, w) in enumerate(((xf_h, sh_h), (xf_h, sh_l), (xf_l, sh_h))):
                                for c in range(HC):
                                    mm = pe.matmul(pgu[:, i % 2, :], x[:, i, c, :], w[:, 512 * c:512 * c + 512],
                                                   start=(n == 0 and c == 0), stop=(n == 2 and c == HC - 1))
                            mm.then_inc(h_gu, 1)
                        if first < i <= behind:
                            pe.wait_ge(h_z, i)
                            if i >= 2:
                                pe.wait_ge(h_zl, i - 1)
                            for c in range(2):
                                mm = pe.transpose(pzt[:, 128 * c:128 * c + 128], z[:, (i - 1) % 2, 128 * c:128 * c + 128], ident[:])
                            mm.then_inc(h_zt, 1)
                        if i >= first + 2:
                            pe.wait_ge(h_zl, i - 1)
                            if i >= 4:
                                pe.wait_ge(s_acc, i - 3)
                            for n, (x, w) in enumerate(((z_h, sh_h), (z_h, sh_l), (z_l, sh_h))):
                                for c in range(2):
                                    mm = pe.matmul(py[:, i % 2, :], x[:, i % 2, c, :], w[:, 2048 + 512 * c:2560 + 512 * c],
                                                   start=(n == 0 and c == 0), stop=(n == 2 and c == 1))
                            mm.then_inc(h_y, 1)

                pe.wait_ge(s_tab, 48)
                pe.wait_ge(s_route, SEL_STEP)
                pe.matmul(pa[:, 0:128], tri[:], sel[:].rearrange("p i e -> p (i e)"), start=True, stop=False)
                for k in range(1, PAIRS):
                    pe.matmul(pa[:, 16 * k:128], ones[:], sel[:, 0:PAIRS - k, :].rearrange("p i e -> p (i e)"),
                              start=False, stop=(k == PAIRS - 1))
                for k in range(PAIRS):
                    mm = pe.matmul(pa[:, 512:512 + E], ones[:], sel[:, k, :], start=(k == 0), stop=(k == PAIRS - 1))
                mm.then_inc(s_pos, 1)
                pe.wait_ge(s_shl, 3)
                shared(EARLY)

                for k in range(PAIRS * TOPK):
                    if k % (PAIRS * TOPK // 2) == 0:
                        pe.wait_ge(s_put, 2 + k // (PAIRS * TOPK // 2))
                    if k % TOPK == 0:
                        pe.wait_ge(s_put_act, k // TOPK + 1)
                    mm = pe.matmul(pa[0:LANES, 1024:1024 + TILES], at_lane[:, k, :], at_tile[:, k, :],
                                   start=(k == 0), stop=(k == PAIRS * TOPK - 1))
                mm.then_inc(s_ids, 1)

                def turn_x(h, sub):
                    q = SUBS * h + sub
                    for c in range(HC):
                        mm = pe.transpose(XT[q % 2][:, LANES * c:LANES * c + LANES], xg[0:LANES, q, 128 * c:128 * c + 128],
                                          ident[0:LANES, 0:LANES])
                    mm.then_inc(s_xt, 1)

                def gate_up(h):
                    for m in range(4):
                        for i, (x, w) in enumerate(((xg_h, w_h), (xg_l, w_h), (xg_h, w_l))):
                            for c in range(HC):
                                mm = pe.matmul(GU[m][:, 0:BLOCK], w[:, h, 512 * c + 128 * m:512 * c + 128 * m + 128], x[:, h, c, :],
                                               start=(i == 0 and c == 0), stop=(i == 2 and c == HC - 1))
                        if m % 2 == 1:
                            mm.then_inc(s_gu, 1)

                def project(h, sub):
                    q = SUBS * h + sub
                    for i, (x, w) in enumerate(((bz_h, w_h), (bz_h, w_l), (bz_l, w_h))):
                        for c in range(2):
                            mm = pe.matmul(YB[q % 2][0:LANES], x[:, h, c, LANES * sub:LANES * sub + LANES],
                                           w[:, h, GUC + 512 * c:GUC + 512 * c + 512],
                                           start=(i == 0 and c == 0), stop=(i == 2 and c == 1))
                    mm.then_inc(s_y, 1)

                def pair(p, first, last):
                    for h in range(2):
                        pe.wait_ge(s_gxl, 2 * SUBS * p + SUBS * h + SUBS)
                        pe.wait_ge(s_gul, 4 * p + 2 * h + 2)
                        if not (first and h == 0):
                            pe.wait_ge(s_z, 2 * p + h)
                        gate_up(h)
                        for sub in range(SUBS):
                            if not (last and h == 1):
                                if h == 0:
                                    pe.wait_ge(s_ldx[SUBS + sub], 16 * p + 16)
                                else:
                                    pe.wait_ge(s_ldx[sub], 16 * p + 32)
                                pe.wait_ge(s_gxl, 2 * SUBS * p + SUBS * h + SUBS + sub - 1)
                                turn_x(1 - h, sub)
                        for sub in range(SUBS):
                            if not (first and h == 0):
                                if sub == 0:
                                    pe.wait_ge(s_zl, 2 * p + h)
                                    pe.wait_ge(s_dnl, 2 * p + h)
                                if not (first and h == 1 and sub < 2):
                                    pe.wait_ge(s_yo, 2 * SUBS * p + SUBS * h - SUBS + sub - 1)
                                project(1 - h, sub)

                pe.wait_ge(s_route, PAIRS_STEP)
                n = pairs_of_blocks(pe)
                pe.wait_ge(s_route, TABLES_STEP)
                pe.wait_ge(s_acc, len(EARLY))
                for sub in range(SUBS):
                    pe.wait_ge(s_ldx[sub], 16)
                    turn_x(0, sub)
                pair(0, True, False)
                pair(1, False, False)
                with pe.Fori(2, n - 1) as p:
                    pair(p, False, False)
                pair(n - 1, False, True)
                pe.wait_ge(s_zl, 2 * n)
                pe.wait_ge(s_dnl, 2 * n)
                for sub in range(SUBS):
                    pe.wait_ge(s_yo, 2 * SUBS * n - SUBS + sub - 1)
                    project(1, sub)
                pe.wait_ge(s_yo, 2 * SUBS * n)
                shared(LATE)

            @block.scalar
            def _(act):
                act.wait_ge(s_route, 2)
                act.activation(score[:], score[:], ACT.Exp).then_inc(s_sco, 1)
                act.wait_ge(s_ldsh, 16)
                for lo, hi in SHARED:
                    act.activation(sh_h[:, lo:hi], sh_raw[:, lo:hi], ACT.Copy, scale=WS).then_inc(s_shh, 1)
                def shared(tiles):
                    first, behind = tiles[0], tiles[-1] + 1
                    for i in range(first, behind + 1):
                        if i < behind:
                            act.wait_ge(h_gu, i + 1)
                            if i >= 2:
                                act.wait_ge(h_z, i - 1)
                            act.activation(sg[:, i % 2, :], pgu[:, i % 2, 0:I], ACT.Silu, scale=1 / WS).then_inc(h_sg, 1)
                        if i > first:
                            act.wait_ge(h_zt, i)
                            if i >= 3:
                                act.wait_ge(h_y, i - 2)
                            act.activation(z_h[:, (i - 1) % 2].rearrange("p c t -> p (c t)"), pzt[:], ACT.Copy).then_inc(h_zh, 1)

                shared(EARLY)
                act.wait_ge(s_put, 1)
                for i in range(PAIRS):
                    part = at_tile[:, TOPK * i:TOPK * i + TOPK].rearrange("p k t -> p (k t)")
                    act.activation(part, part, ACT.Copy, scale=token[:, i:i + 1]).then_inc(s_put_act, 1)

                def split_gu(s, piece):
                    lo, hi = PIECES[piece]
                    act.activation(w_h[:, s, lo:hi], gu_raw[:, s, lo:hi], ACT.Copy, scale=WS).then_inc(s_guh, 1)

                def split_dn(s):
                    act.activation(w_h[:, s, GUC:WEXP], dn_raw[:, s], ACT.Copy, scale=WS).then_inc(s_dnh, 1)

                def split_x(h, sub):
                    act.activation(xg_h[:, h, :, LANES * sub:LANES * sub + LANES],
                                   XT[(SUBS * h + sub) % 2][:, 0:HC * LANES].rearrange("p (c t) -> p c t", c=HC), ACT.Copy).then_inc(s_gxh, 1)

                def out(h, sub):
                    q = SUBS * h + sub
                    act.activation(ysb[0:LANES, q], YB[q % 2][0:LANES], ACT.Copy, scale=1 / (WS * ZS)).then_inc(s_yo, 1)

                def pair(p, first, second, last):
                    for h in range(2):
                        if not (last and h == 1):
                            if h == 0:
                                act.wait_ge(s_ldgu[1], 16 * p + 16)
                            else:
                                act.wait_ge(s_ldgu[0], 16 * p + 32)
                            if not (first and h == 0):
                                act.wait_ge(s_gu, 4 * p + 2 * h)
                            split_gu(1 - h, 0)
                            split_gu(1 - h, 1)
                        act.wait_ge(s_lddn[h], 16 * p + 16)
                        if not first:
                            act.wait_ge(s_y, 2 * SUBS * p + SUBS * h - SUBS)
                        split_dn(h)
                        act.wait_ge(s_gu, 4 * p + 2 * h + 1)
                        if not (first and h == 0):
                            act.wait_ge(s_z, 2 * p + h)
                        act.activation(bg[:], gate_t, ACT.Silu, scale=1 / WS).then_inc(s_sg, 1)
                        if not (last and h == 1):
                            for sub in range(SUBS):
                                act.wait_ge(s_xt, 2 * SUBS * p + SUBS * h + SUBS + sub + 1)
                                split_x(1 - h, sub)
                        act.wait_ge(s_z, 2 * p + h + 1)
                        act.activation(bz_h[:, h], bz[:], ACT.Copy).then_inc(s_zh, 1)
                        if not (first and h == 0):
                            for sub in range(SUBS):
                                act.wait_ge(s_y, 2 * SUBS * p + SUBS * h - SUBS + sub + 1)
                                if h == 1 and not first:
                                    act.wait_ge(s_sty[sub], 16 * p)
                                if h == 0 and not second:
                                    act.wait_ge(s_sty[SUBS + sub], 16 * p - 16)
                                out(1 - h, sub)

                act.wait_ge(s_route, PAIRS_STEP)
                n = pairs_of_blocks(act)
                act.wait_ge(h_z, len(EARLY))
                act.wait_ge(h_y, len(EARLY))
                act.wait_ge(s_ldgu[0], 16)
                split_gu(0, 0)
                split_gu(0, 1)
                for sub in range(SUBS):
                    act.wait_ge(s_xt, sub + 1)
                    split_x(0, sub)
                pair(0, True, False, False)
                pair(1, False, True, False)
                with act.Fori(2, n - 1) as p:
                    pair(p, False, False, False)
                pair(n - 1, False, False, True)
                for sub in range(SUBS):
                    act.wait_ge(s_y, 2 * SUBS * n - SUBS + sub + 1)
                    act.wait_ge(s_sty[SUBS + sub], 16 * n - 16)
                    out(1, sub)
                shared(LATE)
                act.preload_act_table_set("natural_log_exp_and_others")
                def roots3(t):
                    act.wait_ge(s_stat3, t // 2 * 4 + 3 + t % 2)
                    act.activation(ln3[:, t, :], mv3[:, t, 1:2], ACT.Ln, bias=eps[:]).then_inc(s_rs3, 1)
                    act.wait_ge(s_rs3, 2 * t + 1)
                    act.activation(rstd3[:, t, :], ln3[:, t, :], ACT.Exp, scale=-0.5).then_inc(s_rs3, 1)

                for t in range(4):
                    roots3(t)
                for i in range(PAIRS // 2):
                    for t in (2 * i, 2 * i + 1):
                        if i >= 2:
                            roots3(t)
                    for t in (2 * i, 2 * i + 1):
                        act.wait_ge(s_neg, t + 1)
                        if t >= 4:
                            act.wait_ge(s_out[t % 4], 16)
                        act.activation(y3[:, t % 4], xres[:, t, :], ACT.Identity, bias=neg[:, t], scale=rstd3[:, t, :]).then_inc(s_norm3, 1)

            @block.vector
            def _(dve):
                steps = 0

                def step(ins):
                    nonlocal steps
                    ins.then_inc(s_route, 1)
                    steps += 1
                    dve.wait_ge(s_route, steps)

                choices = [128, PAIRS, TOPK, E]

                def route(part):
                    if part == 0:
                        step(dve.tensor_scalar(score[:], score[:], 88.0, None, ALU.min))
                        dve.wait_ge(s_sco, 1)
                        step(dve.tensor_scalar(sig[:], score[:], 1.0, None, ALU.add))
                        step(dve.reciprocal(sig[:], sig[:]))
                        step(dve.tensor_tensor(sig[:], sig[:], gbias[:].unsqueeze(1).to_broadcast([128, PAIRS, E]), ALU.add))
                        for i in range(PAIRS):
                            dve.max(top[:, i], sig[:, i]).then_inc(s_max, 1)
                        for i in range(PAIRS):
                            dve.wait_ge(s_max, i + 1)
                            dve.max_index(top_e[:, i], top[:, i], sig[:, i]).then_inc(s_max, 1)
                        dve.wait_ge(s_max, 2 * PAIRS)
                        step(dve.tensor_copy(top_f[:], top_e[:]))
                        dve.wait_ge(s_tab, 48)
                        step(dve.tensor_tensor(mask[:], top_f[:, :, 0:TOPK].unsqueeze(3).to_broadcast(choices),
                                               count[:, 0:E].unsqueeze(1).unsqueeze(2).to_broadcast(choices), ALU.is_equal))
                        step(dve.tensor_tensor(pick[:, :, 0:2, :], mask[:, :, 0:2, :], mask[:, :, 2:4, :], ALU.add))
                        step(dve.tensor_tensor(sel[:], pick[:, :, 0, :], pick[:, :, 1, :], ALU.add))
                        assert steps == SEL_STEP
                    if part == 1:
                        step(dve.tensor_reduce(total[:], top[:, :, 0:TOPK], AX.X, ALU.add))
                        step(dve.tensor_scalar(total[:], total[:], 1e-20, None, ALU.add))
                        step(dve.reciprocal(total[:], total[:]))
                        step(dve.tensor_tensor(wk[:], top[:, :, 0:TOPK], total[:].unsqueeze(2).to_broadcast([128, PAIRS, TOPK]), ALU.mult))
                        step(dve.tensor_copy(count_h[:], count[:]))
                        dve.wait_ge(s_pos, 1)
                        step(dve.tensor_scalar(blocks[:], pa[:, 512:512 + E], 1.0 / BLOCK, 0.5 - 0.5 / BLOCK, ALU.mult, ALU.add))
                        step(dve.tensor_scalar(blocks[:], blocks[:], ROUND, None, ALU.add))
                        step(dve.tensor_scalar(blocks[:], blocks[:], -ROUND, None, ALU.add))
                        step(dve.tensor_tensor(earlier[:], before[:], blocks[:].unsqueeze(1).to_broadcast([128, E, E]), ALU.mult))
                        step(dve.tensor_reduce(begin[:], earlier[:], AX.X, ALU.add))
                        step(dve.tensor_tensor(end[:], begin[:], blocks[:], ALU.add))
                        step(dve.tensor_scalar(by_pair[:], count[:, 0:BLOCKS // 2], 2.0, end[:, E - 1:E], ALU.mult, ALU.is_lt))
                        step(dve.tensor_reduce(pairs_f[:], by_pair[:], AX.X, ALU.add))
                        step(dve.tensor_scalar(pairs_i[:], pairs_f[:], -float(LEAST), None, ALU.add))
                        assert steps == PAIRS_STEP
                        step(dve.tensor_tensor(owner[:], end[:].unsqueeze(1).to_broadcast([128, BLOCKS, E]),
                                               count[:, 0:BLOCKS].unsqueeze(2).to_broadcast([128, BLOCKS, E]), ALU.is_le))
                        step(dve.tensor_reduce(row_f[:], owner[:], AX.X, ALU.add))
                        step(dve.tensor_scalar(row_f[:], row_f[:], E - 1.0, 128.0, ALU.min, ALU.mult))
                        step(dve.tensor_scalar(row_i[:], row_f[:], token[:, 0:1], None, ALU.add))
                        assert steps == ROWS_STEP
                    if part == 2:
                        step(dve.scalar_tensor_tensor(place[:], begin[:].unsqueeze(1).to_broadcast([128, PAIRS, E]), float(BLOCK),
                                                      pa[:, 0:128].rearrange("p (i e) -> p i e", e=E), ALU.mult, ALU.add))
                        step(dve.tensor_tensor(pick[:], mask[:], place[:].unsqueeze(2).to_broadcast(choices), ALU.mult))
                        step(dve.tensor_reduce(slot[:], pick[:], AX.X, ALU.add))
                    if part == 3:
                        step(dve.tensor_scalar(slot_i[:].rearrange("p (i k) -> p i k", k=TOPK), slot[:], 0.0, None, ALU.add))
                        step(dve.tensor_scalar(tile_in[:], slot[:], 1.0 / LANES, 0.5 / LANES - 0.5, ALU.mult, ALU.add))
                        step(dve.tensor_scalar(tile_in[:], tile_in[:], ROUND, None, ALU.add))
                        step(dve.tensor_scalar(tile_in[:], tile_in[:], -ROUND, None, ALU.add))
                        step(dve.scalar_tensor_tensor(lane[:], tile_in[:], -float(LANES), slot[:], ALU.mult, ALU.add))
                    if part == 4:
                        n = PAIRS * TOPK
                        dve.tensor_tensor(at_tile[:], count_h[:, 0:TILES].unsqueeze(1).to_broadcast([128, n, TILES]),
                                          tile_in[:].rearrange("p i k -> p (i k)").unsqueeze(2).to_broadcast([128, n, TILES]),
                                          ALU.is_equal).then_inc(s_put, 1)
                    if part == 5:
                        for half in range(2):
                            a, b = PAIRS // 2 * half, PAIRS // 2 * (half + 1)
                            m = PAIRS // 2 * TOPK
                            dve.tensor_tensor(at_lane[:, TOPK * a:TOPK * b], count_h[:, 0:LANES].unsqueeze(1).to_broadcast([128, m, LANES]),
                                              lane[:, a:b].rearrange("p i k -> p (i k)").unsqueeze(2).to_broadcast([128, m, LANES]),
                                              ALU.is_equal).then_inc(s_put, 1)

                step(dve.memset(ones[:], 1.0))
                route(0)
                for c, (lo, hi) in enumerate(SHARED):
                    dve.wait_ge(s_shh, c + 1)
                    dve.scalar_tensor_tensor(sh_l[:, lo:hi], sh_raw[:, lo:hi], WS, sh_h[:, lo:hi],
                                             ALU.mult, ALU.subtract).then_inc(s_shl, 1)

                def shared(i, first, behind):
                    if i < behind:
                        dve.wait_ge(h_sg, i + 1)
                        if i >= 2:
                            dve.wait_ge(h_zt, i - 1)
                        dve.scalar_tensor_tensor(z[:, i % 2, :], pgu[:, i % 2, I:2 * I], ZS / WS, sg[:, i % 2, :],
                                                 ALU.mult, ALU.mult).then_inc(h_z, 1)
                    if first < i <= behind:
                        dve.wait_ge(h_zh, i)
                        dve.tensor_tensor(z_l[:, (i - 1) % 2].rearrange("p c t -> p (c t)"), pzt[:],
                                          z_h[:, (i - 1) % 2].rearrange("p c t -> p (c t)"), ALU.subtract).then_inc(h_zl, 1)
                    if i >= first + 2:
                        dve.wait_ge(h_y, i - 1)
                        dve.scalar_tensor_tensor(xres[:, i - 2, :], py[:, i % 2, :], 1 / (WS * ZS), xres[:, i - 2, :],
                                                 ALU.mult, ALU.add).then_inc(s_acc, 1)

                route(1)
                for part in range(len(EARLY) + 2):
                    shared(part, 0, len(EARLY))
                    if part < 3:
                        route(2 + part)
                    if part == 4:
                        route(5)

                dve.wait_ge(s_ids, 1)
                assert steps == TABLES_STEP - 1
                step(dve.tensor_copy(ids[0:LANES], pa[0:LANES, 1024:1024 + TILES]))
                assert steps == TABLES_STEP

                def split_gu(s, piece):
                    lo, hi = PIECES[piece]
                    dve.scalar_tensor_tensor(w_l[:, s, lo:hi], gu_raw[:, s, lo:hi], WS, w_h[:, s, lo:hi],
                                             ALU.mult, ALU.subtract).then_inc(s_gul, 1)

                def split_x(h, sub):
                    hi = xg_h[:, h, :, LANES * sub:LANES * sub + LANES]
                    dve.tensor_tensor(xg_l[:, h, :, LANES * sub:LANES * sub + LANES],
                                      XT[(SUBS * h + sub) % 2][:, 0:HC * LANES].rearrange("p (c t) -> p c t", c=HC),
                                      hi, ALU.subtract).then_inc(s_gxl, 1)

                def pair(p, first, last):
                    for h in range(2):
                        if not (last and h == 1):
                            for piece in range(2):
                                dve.wait_ge(s_guh, 4 * p + 2 * h + piece + 3)
                                split_gu(1 - h, piece)
                        dve.wait_ge(s_dnh, 2 * p + h + 1)
                        dve.scalar_tensor_tensor(w_l[:, h, GUC:WEXP], dn_raw[:, h], WS, w_h[:, h, GUC:WEXP],
                                                 ALU.mult, ALU.subtract).then_inc(s_dnl, 1)
                        dve.wait_ge(s_sg, 2 * p + h + 1)
                        dve.wait_ge(s_gu, 4 * p + 2 * h + 2)
                        if not (first and h == 0):
                            dve.wait_ge(s_zl, 2 * p + h)
                        dve.scalar_tensor_tensor(bz[:], up_t, ZS / WS, bg[:], ALU.mult, ALU.mult).then_inc(s_z, 1)
                        if not (last and h == 1):
                            for sub in range(SUBS):
                                dve.wait_ge(s_gxh, 2 * SUBS * p + SUBS * h + SUBS + sub + 1)
                                split_x(1 - h, sub)
                        dve.wait_ge(s_zh, 2 * p + h + 1)
                        dve.tensor_tensor(bz_l[:, h], bz[:], bz_h[:, h], ALU.subtract).then_inc(s_zl, 1)

                n = pairs_of_blocks(dve)
                for piece in range(2):
                    dve.wait_ge(s_guh, piece + 1)
                    split_gu(0, piece)
                for sub in range(SUBS):
                    dve.wait_ge(s_gxh, sub + 1)
                    split_x(0, sub)
                pair(0, True, False)
                with dve.Fori(1, n - 1) as p:
                    pair(p, False, False)
                pair(n - 1, False, True)

                def centre3(t):
                    dve.wait_ge(s_rs3, 2 * t + 2)
                    dve.tensor_scalar(neg[:, t], mv3[:, t, 0:1], rstd3[:, t, :], -1.0, ALU.mult, ALU.mult).then_inc(s_neg, 1)

                for i in range(PAIRS // 2):
                    for late in LATE_SLOTS[i]:
                        shared(late, len(EARLY), PAIRS)
                    if i == 2:
                        for t in range(4):
                            centre3(t)
                    for k in range(TOPK):
                        if i == 3 and k == 2:
                            centre3(4)
                            centre3(5)
                        for t in (2 * i, 2 * i + 1):
                            m = 8 * i + 2 * k + t % 2
                            dve.wait_ge(s_yg[m % 8], 16 * i + 16)
                            if k == 0:
                                dve.wait_ge(s_acc, t + 1)
                            else:
                                dve.wait_ge(s_add, m - 1)
                            dve.scalar_tensor_tensor(xres[:, t, :], yg[:, m % 8], wk[:, t, k:k + 1], xres[:, t, :],
                                                     ALU.mult, ALU.add).then_inc(s_add, 1)
                    for t in (2 * i, 2 * i + 1):
                        dve.wait_ge(s_add, 8 * i + 7 + t % 2)
                        dve.bn_stats(st3[:, t, :], xres[:, t, :]).then_inc(s_stat3, 1)
                    for t in (2 * i, 2 * i + 1):
                        dve.wait_ge(s_stat3, 4 * i + 1 + t % 2)
                        dve.bn_aggr(mv3[:, t, :], st3[:, t, :]).then_inc(s_stat3, 1)
                centre3(6)
                centre3(7)

            @block.gpsimd
            def _(pool):
                def load_x(t, q, count):
                    pool.tensor_copy(at_x[0:LANES, q:q + 1], ids[0:LANES, bass.ds(t, 1)]).then_inc(s_stage, 1)
                    pool.wait_ge(s_stage, count + 1)
                    pool.sem_inc(s_passed, 1)
                    pool.indirect_dma_start(xg[0:LANES, q], None, x2_rows,
                                            bass.IndirectOffsetOnAxis(ap=at_x[0:LANES, q:q + 1], axis=0)).then_inc(s_ldx[q], 16)

                def load_gu(b, s, count):
                    pool.tensor_copy(at_w[:, s:s + 1], row_i[:, bass.ds(b, 1)]).then_inc(s_stage, 1)
                    pool.wait_ge(s_stage, count + 1)
                    pool.sem_inc(s_passed, 1)
                    pool.indirect_dma_start(gu_raw[:, s], None, d["wgu"], bass.IndirectOffsetOnAxis(ap=at_w[:, s:s + 1], axis=0)).then_inc(s_ldgu[s], 16)

                def load_dn(b, s, count):
                    pool.tensor_copy(at_w[:, 2 + s:3 + s], row_i[:, bass.ds(b, 1)]).then_inc(s_stage, 1)
                    pool.wait_ge(s_stage, count + 1)
                    pool.sem_inc(s_passed, 1)
                    pool.indirect_dma_start(dn_raw[:, s], None, d["wdn"], bass.IndirectOffsetOnAxis(ap=at_w[:, 2 + s:3 + s], axis=0)).then_inc(s_lddn[s], 16)

                pool.wait_ge(s_route, ROWS_STEP)
                load_gu(0, 0, 0)
                load_dn(0, 0, 1)
                load_gu(1, 1, 2)
                pool.wait_ge(s_x2w, 16 * PAIRS)
                pool.wait_ge(s_route, TABLES_STEP)
                for t in range(2 * SUBS):
                    load_x(t, t, 3 + t)
                load_dn(1, 1, 3 + 2 * SUBS)

                n = pairs_of_blocks(pool)
                with pool.Fori(0, n - 1) as p:
                    for h in range(2):
                        done = (2 * SUBS + 4) * p + (SUBS + 2) * h + 2 * SUBS + 4
                        pool.wait_ge(s_gul, 4 * p + 2 * h + 2)
                        pool.sem_inc(s_passed, 1)
                        load_gu(2 * p + h + 2, h, done)
                        pool.wait_ge(s_xt, 2 * SUBS * p + SUBS * h + SUBS)
                        pool.sem_inc(s_passed, 1)
                        for sub in range(SUBS):
                            load_x(2 * SUBS * p + SUBS * h + 2 * SUBS + sub, SUBS * h + sub, done + 1 + sub)
                        pool.wait_ge(s_dnl, 2 * p + h + 1)
                        pool.sem_inc(s_passed, 1)
                        load_dn(2 * p + h + 2, h, done + 1 + SUBS)
                for sent in s_sty:
                    pool.wait_ge(sent, 16 * n)
                    pool.sem_inc(s_passed, 1)
                for m in range(PAIRS * TOPK):
                    c = TOPK * (m // 8 * 2 + m % 2) + m % 8 // 2
                    if m >= 8:
                        pool.wait_ge(s_add, m - 7)
                    pool.indirect_dma_start(yg[:, m % 8], None, y_rows,
                                            bass.IndirectOffsetOnAxis(ap=slot_i[:, c:c + 1], axis=0)).then_inc(s_yg[m % 8], 16)



def layouts(i):
    c = np.ascontiguousarray
    x = i["x"].reshape(PAIRS, 128, H)
    cx = i["ctx_4096"].reshape(PAIRS, 128, H)
    wq = i["L0_attn_Wq"].reshape(H, NHKV, REP, D).transpose(0, 2, 1, 3).reshape(H, H)
    wo = i["L0_attn_Wo"].reshape(NHKV, REP, D, H).transpose(1, 0, 2, 3).reshape(REP, 128, H)
    wqkv = np.concatenate([wq, i["L0_attn_Wk"], i["L0_attn_Wv"]], 1)
    xwkv = i["L0_xattn_Wkv"]
    dup = lambda w: np.concatenate([w, w], 0)
    b, g = i["L0_xattn_b_out"], i["L0_xattn_g"].reshape(XD)
    inv = (1.0 / np.float32(10000.0) ** (np.arange(0, D, 2, dtype=np.float32) / D)).astype(np.float32)
    ang = (np.arange(S, dtype=np.float32)[:, None] * inv[None, :]).astype(np.float32)
    cos, sin = np.cos(ang) / np.float32(WS), np.sin(ang) / np.float32(WS)
    rope = np.stack([np.concatenate([cos, cos], 1), np.concatenate([-sin, sin], 1)], 1)
    q = np.arange(S)
    mask_k = np.where(q[None, :] > q[:, None], np.float32(NEG), np.float32(0))[:, None, :].repeat(NHKV, 1)
    mask_q = np.tile(np.eye(S, dtype=np.float32), (1, 2))
    mask_q, mask_k = (np.concatenate([m, np.zeros_like(m)], 0) for m in (mask_q, mask_k))
    wg, wu, wd = (np.concatenate([i["L0_ffn_S" + n][None], i["L0_ffn_W" + n]], 0) for n in "gud")
    gu = np.stack([wg, wu], 1).transpose(0, 3, 1, 2).reshape(E + 1, HC, 128, 2 * I).transpose(0, 2, 1, 3)
    down = wd.transpose(0, 2, 1).reshape(E + 1, I // 128, 128, H).transpose(0, 2, 1, 3)
    gu, down = gu.reshape(E + 1, 128, -1), down.reshape(E + 1, 128, -1)
    return {
        "wgu": c(gu[1:].reshape(E * 128, -1)), "wdn": c(down[1:].reshape(E * 128, -1)), "wsh": c(np.concatenate([gu[0], down[0]], 1)),
        "tri": np.triu(np.ones((128, 128), np.float16), 1),
        "count": c(np.broadcast_to(np.arange(128, dtype=np.float32), (128, 128))),
        "token": c(np.arange(B * S, dtype=np.float32).reshape(PAIRS, 128).T),
        "before": c(np.broadcast_to(np.tril(np.ones((E, E), np.float32), -1), (128, E, E))),
        "x": c(x), "xt": c(x.reshape(PAIRS, 128, HC, 128).transpose(0, 3, 2, 1)),
        "ctx": c(cx), "ctxt": c(cx.reshape(PAIRS, 128, 4, 128).transpose(0, 3, 2, 1)),
        "wqkv": c(wqkv.reshape(HC, 128, 768).transpose(1, 0, 2)), "wo": c(wo.transpose(1, 0, 2)),
        "xw": c(np.stack([dup(i["L0_xattn_Wq"].T), dup(xwkv[:H].T)], 1)),
        "wv": c(xwkv[H:].reshape(XH, XD, XD).transpose(1, 0, 2)),
        "wout": c(i["L0_xattn_Wout"].T.reshape(XH, XD, XD).transpose(1, 0, 2)),
        "xvec": c(np.concatenate([dup(b[:, None]), dup(g[:, None]), np.broadcast_to(b, (128, XD))], 1)),
        "gw": c(i["L0_ffn_gate_w"].T.reshape(HC, 128, E).transpose(1, 0, 2)),
        "gbias": c(np.broadcast_to(i["L0_ffn_bias"], (128, E))),
        "ident": np.eye(128, dtype=np.float32), "rope": c(dup(rope)),
        "kmask": c(np.repeat(np.eye(NHKV, dtype=np.float32), D, 0)),
        "mask_q": c(mask_q), "mask_k": c(mask_k),
        "onesbd": c(np.kron(np.eye(2, dtype=np.float32), np.full((S, S), 1 / S, np.float32))),
    }


def kernel(**inputs):
    import concourse.bacc as bacc
    from concourse.bass_utils import run_bass_kernel_spmd

    arrays = {f"{n}_dram": a for n, a in layouts({n: np.asarray(a) for n, a in inputs.items()}).items()}
    nc = bacc.Bacc("TRN2", target_bir_lowering=False, num_devices=1)
    d = {n[:-5]: nc.dram_tensor(n, a.shape, mybir.dt.from_np(a.dtype), kind="ExternalInput").ap() for n, a in arrays.items()}
    d["out"] = nc.dram_tensor("out_dram", (PAIRS, 128, H), F32, kind="ExternalOutput").ap()
    decoder_layer(nc, d)
    r = run_bass_kernel_spmd(nc, [arrays], core_ids=[0])
    return r.results[0]["out_dram"].reshape(B, S, H)
```
